# Optimizing a Trainium2 kernel written in Bass

```python
import numpy as np
import jax
import jax.numpy as jnp

def _softmax(x, axis=-1):
    return jax.nn.softmax(x, axis=axis)

def _gelu(x):
    return jax.nn.gelu(x, approximate=True)

def _silu(x):
    return jax.nn.silu(x)

def _sigmoid(x):
    return jax.nn.sigmoid(x)

def _layernorm(x, axis=-1, eps=1e-05):
    m = jnp.mean(x, axis=axis, keepdims=True)
    v = jnp.var(x, axis=axis, keepdims=True)
    return (x - m) / jnp.sqrt(v + eps)

def _scatter_add(tgt, idx, src, axis=0):
    return tgt.at[idx].add(src)

def _segment_sum(src, seg, n):
    return jax.ops.segment_sum(src, seg, n)
kernel_name = 'mk_prb_d2_jaxref_r8_e541f4'

def setup_inputs(seed: int=0):
    np.random.seed(seed)
    _w = jnp.asarray

    def _L0_attn_setup():
        import jax, jax.numpy as jnp
        import numpy as np
        D_MODEL = 128
        NUM_HEADS = 16
        HEAD_DIM = D_MODEL // NUM_HEADS
        key = jax.random.key(seed)
        ks = jax.random.split(key, 7)
        B, T, C = (4, 256, D_MODEL)
        s = 1.0 / np.sqrt(C)
        return {'x': jax.random.normal(ks[0], (B, T, C), dtype=jnp.float32), 'ln_gamma': jnp.ones((C,), dtype=jnp.float32), 'ln_beta': jnp.zeros((C,), dtype=jnp.float32), 'w_qkv': jax.random.normal(ks[1], (C, 3 * C), dtype=jnp.float32) * s, 'b_qkv': jnp.zeros((3 * C,), dtype=jnp.float32), 'w_out': jax.random.normal(ks[2], (C, C), dtype=jnp.float32) * s, 'b_out': jnp.zeros((C,), dtype=jnp.float32)}
    _L0_attn_in = _L0_attn_setup()

    def _L0_ffn_setup():
        import jax, jax.numpy as jnp
        import numpy as np
        D = 128
        H = 16
        HD = D // H
        E = 32
        ES = 128
        K = 4
        B, S = (2, 128)
        ROPE_BASE = 10000.0

        def _layernorm(x, g, b):
            m = x.mean(-1, keepdims=True)
            v = ((x - m) ** 2).mean(-1, keepdims=True)
            return (x - m) * jax.lax.rsqrt(v + 1e-05) * g + b

        def _forward(src, wq, wk, wv, wp, wo, ln1_g, ln1_b, ln2_g, ln2_b, sel_w, keys, values):
            Bs, Ss, Ds = src.shape
            scale = 1.0 / jnp.sqrt(jnp.array(HD, dtype=src.dtype))
            x = _layernorm(src, ln1_g, ln1_b)
            q = (x @ wq).reshape(Bs, Ss, H, HD)
            k = (x @ wk).reshape(Bs, Ss, H, HD)
            v = (x @ wv).reshape(Bs, Ss, H, HD)
            pos = jnp.arange(Ss - 1, -Ss, -1, dtype=src.dtype)
            inv_freq = 1.0 / ROPE_BASE ** (jnp.arange(0, Ds, 2, dtype=src.dtype) / Ds)
            ang = pos[:, None] * inv_freq[None, :]
            pe = jnp.concatenate([jnp.sin(ang), jnp.cos(ang)], axis=-1)
            p = (pe @ wp).reshape(2 * Ss - 1, H, HD)
            ac = jnp.einsum('bihd,bjhd->bhij', q, k)
            bd_full = jnp.einsum('bihd,phd->bhip', q, p)
            rel = jnp.arange(Ss)[:, None] - jnp.arange(Ss)[None, :] + (Ss - 1)
            bd = bd_full[:, :, jnp.arange(Ss)[:, None], rel]
            att = jax.nn.softmax((ac + bd) * scale, axis=-1)
            attn_out = jnp.einsum('bhij,bjhd->bihd', att, v).reshape(Bs, Ss, Ds) @ wo
            src = src + attn_out
            x2 = _layernorm(src, ln2_g, ln2_b)
            sel = jax.nn.sigmoid(x2 @ sel_w)
            scores, idx = jax.lax.top_k(sel, K)
            gate = (jax.nn.one_hot(idx, E, dtype=sel.dtype) * scores[..., None]).sum(-2)
            h = jax.nn.relu(jnp.einsum('bsd,edh->bseh', x2, keys))
            moe_out = jnp.einsum('bseh,ehd,bse->bsd', h, values, gate)
            return src + moe_out
        key = jax.random.key(seed)
        ks = jax.random.split(key, 10)
        std_scale = np.sqrt(2.0 / 18)
        w_std = std_scale / np.sqrt(D)
        return {'src': jax.random.normal(ks[0], (B, S, D), jnp.float32), 'wq': jax.random.normal(ks[1], (D, H * HD), jnp.float32) * w_std, 'wk': jax.random.normal(ks[2], (D, H * HD), jnp.float32) * w_std, 'wv': jax.random.normal(ks[3], (D, H * HD), jnp.float32) * w_std, 'wp': jax.random.normal(ks[4], (D, H * HD), jnp.float32) * w_std, 'wo': jax.random.normal(ks[5], (H * HD, D), jnp.float32) * w_std, 'ln1_g': jnp.ones((D,), jnp.float32), 'ln1_b': jnp.zeros((D,), jnp.float32), 'ln2_g': jnp.ones((D,), jnp.float32), 'ln2_b': jnp.zeros((D,), jnp.float32), 'sel_w': jax.random.normal(ks[6], (D, E), jnp.float32) / np.sqrt(D), 'keys': jax.random.normal(ks[7], (E, D, ES), jnp.float32) * w_std, 'values': jax.random.normal(ks[8], (E, ES, D), jnp.float32) * (std_scale / np.sqrt(ES))}
    _L0_ffn_in = _L0_ffn_setup()

    def _L1_attn_setup():
        import math
        import jax, jax.numpy as jnp
        import numpy as np
        DIM = 128
        DIM_QK = 128
        DIM_V = 128
        NUM_BUCKETS = 32
        MAX_DISTANCE = 128

        def _rel_pos_bucket_causal(seq_len):
            q = np.arange(seq_len)
            n = np.maximum(q[:, None] - q[None, :], 0)
            max_exact = NUM_BUCKETS // 2
            is_small = n < max_exact
            nf = np.maximum(n, 1).astype(np.float32)
            val_if_large = max_exact + (np.log(nf / max_exact) / math.log(MAX_DISTANCE / max_exact) * (NUM_BUCKETS - max_exact)).astype(np.int32)
            val_if_large = np.minimum(val_if_large, NUM_BUCKETS - 1)
            return jnp.asarray(np.where(is_small, n, val_if_large), dtype=jnp.int32)

        def laplacian_attn_fn(x):
            mu = math.sqrt(0.5)
            std = math.sqrt(0.25 * math.pi)
            return (1.0 + jax.lax.erf((x - mu) / (std * math.sqrt(2.0)))) * 0.5
        key = jax.random.key(seed)
        ks = jax.random.split(key, 8)
        B, S = (8, 256)
        x = jax.random.normal(ks[0], (B, S, DIM), dtype=jnp.float32)
        Wqk = jax.random.normal(ks[1], (DIM, DIM_QK), dtype=jnp.float32) * (1.0 / math.sqrt(DIM))
        bqk = jnp.zeros((DIM_QK,), dtype=jnp.float32)
        gamma = jax.random.normal(ks[2], (2, DIM_QK), dtype=jnp.float32) * 0.02
        beta = jnp.zeros((2, DIM_QK), dtype=jnp.float32)
        Wv = jax.random.normal(ks[3], (DIM, DIM_V), dtype=jnp.float32) * (1.0 / math.sqrt(DIM))
        bv = jnp.zeros((DIM_V,), dtype=jnp.float32)
        rel_emb = jax.random.normal(ks[4], (NUM_BUCKETS, 1), dtype=jnp.float32) * 0.02
        return {'x': x, 'Wqk': Wqk, 'bqk': bqk, 'gamma': gamma, 'beta': beta, 'Wv': Wv, 'bv': bv, 'rel_emb': rel_emb}
    _L1_attn_in = _L1_attn_setup()

    def _L1_ffn_setup():
        import jax, jax.numpy as jnp
        import numpy as np
        H = 128
        I = 256
        E = 8
        B, S = (2, 512)
        EPS = 1e-05
        INIT = 0.02

        def _layernorm(x, w, b):
            mu = jnp.mean(x, axis=-1, keepdims=True)
            var = jnp.mean(jnp.square(x - mu), axis=-1, keepdims=True)
            return (x - mu) * jax.lax.rsqrt(var + EPS) * w + b
        key = jax.random.key(seed)
        ks = jax.random.split(key, 9)
        return {'hidden_states': jax.random.normal(ks[0], (B, S, H), jnp.float32), 'ln_w': jnp.ones((H,), jnp.float32), 'ln_b': jnp.zeros((H,), jnp.float32), 'router_w': jax.random.normal(ks[1], (H, E), jnp.float32) * INIT, 'gate_w': jax.random.normal(ks[2], (E, H, I), jnp.float32) * INIT, 'up_w': jax.random.normal(ks[3], (E, H, I), jnp.float32) * INIT, 'down_w': jax.random.normal(ks[4], (E, I, H), jnp.float32) * INIT, 'sh_gate': jax.random.normal(ks[5], (H, I), jnp.float32) * INIT, 'sh_up': jax.random.normal(ks[6], (H, I), jnp.float32) * INIT, 'sh_down': jax.random.normal(ks[7], (I, H), jnp.float32) * INIT}
    _L1_ffn_in = _L1_ffn_setup()
    _d = {'L0_attn_x': _L0_attn_in['x'], 'L0_attn_ln_gamma': _L0_attn_in['ln_gamma'], 'L0_attn_ln_beta': _L0_attn_in['ln_beta'], 'L0_attn_w_qkv': _L0_attn_in['w_qkv'], 'L0_attn_b_qkv': _L0_attn_in['b_qkv'], 'L0_attn_w_out': _L0_attn_in['w_out'], 'L0_attn_b_out': _L0_attn_in['b_out'], 'L0_ffn_wq': _L0_ffn_in['wq'], 'L0_ffn_wk': _L0_ffn_in['wk'], 'L0_ffn_wv': _L0_ffn_in['wv'], 'L0_ffn_wp': _L0_ffn_in['wp'], 'L0_ffn_wo': _L0_ffn_in['wo'], 'L0_ffn_ln1_g': _L0_ffn_in['ln1_g'], 'L0_ffn_ln1_b': _L0_ffn_in['ln1_b'], 'L0_ffn_ln2_g': _L0_ffn_in['ln2_g'], 'L0_ffn_ln2_b': _L0_ffn_in['ln2_b'], 'L0_ffn_sel_w': _L0_ffn_in['sel_w'], 'L0_ffn_keys': _L0_ffn_in['keys'], 'L0_ffn_values': _L0_ffn_in['values'], 'L1_attn_Wqk': _L1_attn_in['Wqk'], 'L1_attn_bqk': _L1_attn_in['bqk'], 'L1_attn_gamma': _L1_attn_in['gamma'], 'L1_attn_beta': _L1_attn_in['beta'], 'L1_attn_Wv': _L1_attn_in['Wv'], 'L1_attn_bv': _L1_attn_in['bv'], 'L1_attn_rel_emb': _L1_attn_in['rel_emb'], 'L1_ffn_ln_w': _L1_ffn_in['ln_w'], 'L1_ffn_ln_b': _L1_ffn_in['ln_b'], 'L1_ffn_router_w': _L1_ffn_in['router_w'], 'L1_ffn_gate_w': _L1_ffn_in['gate_w'], 'L1_ffn_up_w': _L1_ffn_in['up_w'], 'L1_ffn_down_w': _L1_ffn_in['down_w'], 'L1_ffn_sh_gate': _L1_ffn_in['sh_gate'], 'L1_ffn_sh_up': _L1_ffn_in['sh_up'], 'L1_ffn_sh_down': _L1_ffn_in['sh_down']}
    _x0 = _d['L0_attn_x']
    _d['L0_attn_x'] = jax.random.normal(jax.random.fold_in(jax.random.key(seed), 1), (8, 512, 128), dtype=_x0.dtype)
    del _x0
    return _d

def reference(L0_attn_x, L0_attn_ln_gamma, L0_attn_ln_beta, L0_attn_w_qkv, L0_attn_b_qkv, L0_attn_w_out, L0_attn_b_out, L0_ffn_wq, L0_ffn_wk, L0_ffn_wv, L0_ffn_wp, L0_ffn_wo, L0_ffn_ln1_g, L0_ffn_ln1_b, L0_ffn_ln2_g, L0_ffn_ln2_b, L0_ffn_sel_w, L0_ffn_keys, L0_ffn_values, L1_attn_Wqk, L1_attn_bqk, L1_attn_gamma, L1_attn_beta, L1_attn_Wv, L1_attn_bv, L1_attn_rel_emb, L1_ffn_ln_w, L1_ffn_ln_b, L1_ffn_router_w, L1_ffn_gate_w, L1_ffn_up_w, L1_ffn_down_w, L1_ffn_sh_gate, L1_ffn_sh_up, L1_ffn_sh_down):

    def _L0_attn_ref(x, ln_gamma, ln_beta, w_qkv, b_qkv, w_out, b_out):
        import jax, jax.numpy as jnp
        import numpy as np
        D_MODEL = 128
        NUM_HEADS = 16
        HEAD_DIM = D_MODEL // NUM_HEADS
        B, T, C = x.shape
        residual = x
        mu = jnp.mean(x, axis=-1, keepdims=True)
        var = jnp.var(x, axis=-1, keepdims=True)
        h = (x - mu) * jax.lax.rsqrt(var + 1e-05) * ln_gamma + ln_beta
        qkv = (h @ w_qkv + b_qkv).reshape(B, T, 3, NUM_HEADS, HEAD_DIM)
        qkv = jnp.transpose(qkv, (2, 0, 3, 1, 4))
        q, k, v = (qkv[0], qkv[1], qkv[2])
        scores = jnp.einsum('bhqd,bhkd->bhqk', q, k) / np.sqrt(HEAD_DIM)
        attn = jax.nn.softmax(scores, axis=-1)
        out = jnp.einsum('bhqk,bhkd->bhqd', attn, v)
        out = jnp.transpose(out, (0, 2, 1, 3)).reshape(B, T, C)
        out = out @ w_out + b_out
        return residual + out

    def _L0_ffn_ref(src, wq, wk, wv, wp, wo, ln1_g, ln1_b, ln2_g, ln2_b, sel_w, keys, values):
        import jax, jax.numpy as jnp
        import numpy as np
        D = 128
        H = 16
        HD = D // H
        E = 32
        ES = 128
        K = 4
        B, S = (2, 128)
        ROPE_BASE = 10000.0

        def _layernorm(x, g, b):
            m = x.mean(-1, keepdims=True)
            v = ((x - m) ** 2).mean(-1, keepdims=True)
            return (x - m) * jax.lax.rsqrt(v + 1e-05) * g + b

        def _forward(src, wq, wk, wv, wp, wo, ln1_g, ln1_b, ln2_g, ln2_b, sel_w, keys, values):
            Bs, Ss, Ds = src.shape
            scale = 1.0 / jnp.sqrt(jnp.array(HD, dtype=src.dtype))
            x = _layernorm(src, ln1_g, ln1_b)
            q = (x @ wq).reshape(Bs, Ss, H, HD)
            k = (x @ wk).reshape(Bs, Ss, H, HD)
            v = (x @ wv).reshape(Bs, Ss, H, HD)
            pos = jnp.arange(Ss - 1, -Ss, -1, dtype=src.dtype)
            inv_freq = 1.0 / ROPE_BASE ** (jnp.arange(0, Ds, 2, dtype=src.dtype) / Ds)
            ang = pos[:, None] * inv_freq[None, :]
            pe = jnp.concatenate([jnp.sin(ang), jnp.cos(ang)], axis=-1)
            p = (pe @ wp).reshape(2 * Ss - 1, H, HD)
            ac = jnp.einsum('bihd,bjhd->bhij', q, k)
            bd_full = jnp.einsum('bihd,phd->bhip', q, p)
            rel = jnp.arange(Ss)[:, None] - jnp.arange(Ss)[None, :] + (Ss - 1)
            bd = bd_full[:, :, jnp.arange(Ss)[:, None], rel]
            att = jax.nn.softmax((ac + bd) * scale, axis=-1)
            attn_out = jnp.einsum('bhij,bjhd->bihd', att, v).reshape(Bs, Ss, Ds) @ wo
            src = src + attn_out
            x2 = _layernorm(src, ln2_g, ln2_b)
            sel = jax.nn.sigmoid(x2 @ sel_w)
            scores, idx = jax.lax.top_k(sel, K)
            gate = (jax.nn.one_hot(idx, E, dtype=sel.dtype) * scores[..., None]).sum(-2)
            h = jax.nn.relu(jnp.einsum('bsd,edh->bseh', x2, keys))
            moe_out = jnp.einsum('bseh,ehd,bse->bsd', h, values, gate)
            return src + moe_out
        return _forward(src, wq, wk, wv, wp, wo, ln1_g, ln1_b, ln2_g, ln2_b, sel_w, keys, values)

    def _L1_attn_ref(x, Wqk, bqk, gamma, beta, Wv, bv, rel_emb):
        import math
        import jax, jax.numpy as jnp
        import numpy as np
        DIM = 128
        DIM_QK = 128
        DIM_V = 128
        NUM_BUCKETS = 32
        MAX_DISTANCE = 128

        def _rel_pos_bucket_causal(seq_len):
            q = np.arange(seq_len)
            n = np.maximum(q[:, None] - q[None, :], 0)
            max_exact = NUM_BUCKETS // 2
            is_small = n < max_exact
            nf = np.maximum(n, 1).astype(np.float32)
            val_if_large = max_exact + (np.log(nf / max_exact) / math.log(MAX_DISTANCE / max_exact) * (NUM_BUCKETS - max_exact)).astype(np.int32)
            val_if_large = np.minimum(val_if_large, NUM_BUCKETS - 1)
            return jnp.asarray(np.where(is_small, n, val_if_large), dtype=jnp.int32)

        def laplacian_attn_fn(x):
            mu = math.sqrt(0.5)
            std = math.sqrt(0.25 * math.pi)
            return (1.0 + jax.lax.erf((x - mu) / (std * math.sqrt(2.0)))) * 0.5
        B, S, _ = x.shape
        qk = jax.nn.swish(jnp.einsum('bsd,de->bse', x, Wqk) + bqk)
        q = qk * gamma[0] + beta[0]
        k = qk * gamma[1] + beta[1]
        v = jax.nn.swish(jnp.einsum('bsd,de->bse', x, Wv) + bv)
        scale = 1.0 / S
        sim = jnp.einsum('bid,bjd->bij', q, k) * scale
        buckets = _rel_pos_bucket_causal(S)
        bias = rel_emb[buckets, 0] * DIM_QK ** 0.5
        sim = sim + bias
        attn = laplacian_attn_fn(sim)
        i = jnp.arange(S)
        future = i[None, :] > i[:, None]
        attn = jnp.where(future, 0.0, attn)
        return jnp.einsum('bij,bjd->bid', attn, v)

    def _L1_ffn_ref(hidden_states, ln_w, ln_b, router_w, gate_w, up_w, down_w, sh_gate, sh_up, sh_down):
        import jax, jax.numpy as jnp
        import numpy as np
        H = 128
        I = 256
        E = 8
        B, S = (2, 512)
        EPS = 1e-05
        INIT = 0.02

        def _layernorm(x, w, b):
            mu = jnp.mean(x, axis=-1, keepdims=True)
            var = jnp.mean(jnp.square(x - mu), axis=-1, keepdims=True)
            return (x - mu) * jax.lax.rsqrt(var + EPS) * w + b
        b, s, h = hidden_states.shape
        normed = _layernorm(hidden_states, ln_w, ln_b)
        xf = normed.reshape(-1, h)
        logits = xf @ router_w
        top_idx = jnp.argmax(logits, axis=-1)
        top_score = jax.nn.sigmoid(jnp.max(logits, axis=-1))

        def body(acc, ew):
            g, u, d, e = ew
            w = jnp.where(top_idx == e, top_score, 0.0)[:, None]
            xe = xf * w
            hmid = jax.nn.silu(xe @ g) * (xe @ u)
            return (acc + hmid @ d, None)
        routed, _ = jax.lax.scan(body, jnp.zeros_like(xf), (gate_w, up_w, down_w, jnp.arange(E)))
        shared = jax.nn.silu(xf @ sh_gate) * (xf @ sh_up) @ sh_down
        moe_out = (routed + shared).reshape(b, s, h)
        return hidden_states + moe_out
    x = L0_attn_x
    xn = _layernorm(x, axis=-1)
    x = x + _L0_attn_ref(xn, L0_attn_ln_gamma, L0_attn_ln_beta, L0_attn_w_qkv, L0_attn_b_qkv, L0_attn_w_out, L0_attn_b_out) + _L0_ffn_ref(xn, L0_ffn_wq, L0_ffn_wk, L0_ffn_wv, L0_ffn_wp, L0_ffn_wo, L0_ffn_ln1_g, L0_ffn_ln1_b, L0_ffn_ln2_g, L0_ffn_ln2_b, L0_ffn_sel_w, L0_ffn_keys, L0_ffn_values)
    xn = _layernorm(x, axis=-1)
    x = x + _L1_attn_ref(xn, L1_attn_Wqk, L1_attn_bqk, L1_attn_gamma, L1_attn_beta, L1_attn_Wv, L1_attn_bv, L1_attn_rel_emb) + _L1_ffn_ref(xn, L1_ffn_ln_w, L1_ffn_ln_b, L1_ffn_router_w, L1_ffn_gate_w, L1_ffn_up_w, L1_ffn_down_w, L1_ffn_sh_gate, L1_ffn_sh_up, L1_ffn_sh_down)
    return x

_drawn_inputs = setup_inputs


def setup_inputs(seed=0):
    import zlib

    import numpy as np

    out = dict(_drawn_inputs(seed))
    spreads = {'L0_attn_ln_gamma': (1.0, 0.6),
     'L0_attn_ln_beta': (0.0, 0.1),
     'L0_attn_b_qkv': (0.0, 0.1),
     'L0_attn_b_out': (0.0, 0.1),
     'L0_ffn_ln1_g': (1.0, 0.6),
     'L0_ffn_ln1_b': (0.0, 0.8),
     'L0_ffn_ln2_g': (1.0, 0.6),
     'L0_ffn_ln2_b': (0.0, 0.8),
     'L1_attn_bqk': (0.0, 0.8),
     'L1_attn_beta': (0.0, 0.8),
     'L1_attn_bv': (0.0, 0.1),
     'L1_ffn_ln_w': (1.0, 0.6),
     'L1_ffn_ln_b': (0.0, 0.8)}
    factors = {'L0_ffn_wq': 8.0,
     'L0_ffn_wk': 8.0,
     'L0_ffn_wv': 6.196,
     'L0_ffn_wp': 8.0,
     'L0_ffn_wo': 5.636,
     'L0_ffn_sel_w': 4.191,
     'L0_ffn_keys': 4.652,
     'L1_attn_Wqk': 8.0,
     'L1_attn_gamma': 8.0,
     'L1_ffn_router_w': 8.0,
     'L1_ffn_gate_w': 8.0,
     'L1_ffn_up_w': 8.0,
     'L1_ffn_down_w': 8.0,
     'L1_ffn_sh_gate': 8.0,
     'L1_ffn_sh_up': 8.0,
     'L1_ffn_sh_down': 8.0}
    for name, (base, spread) in spreads.items():
        noise = np.random.default_rng([zlib.crc32(name.encode()), seed]).standard_normal(out[name].shape)
        drawn = base * np.exp(spread * noise) if base else spread * noise
        out[name] = jnp.asarray(drawn.astype(out[name].dtype))
    for name, factor in factors.items():
        out[name] = (out[name] * factor).astype(out[name].dtype)
    return out
```

```python
from contextlib import ExitStack

import numpy as np
import concourse.bass as bass
from concourse import mybir

ALU = mybir.AluOpType
ACT = mybir.ActivationFunctionType
AX = mybir.AxisListType
F32 = mybir.dt.float32
F32R = mybir.dt.float32r
U32 = mybir.dt.uint32

P = 128
TT = 4
T = P * TT
HD = 8
HG = 4
NG = 4
E0, TOPK = 32, 4
E1 = 8
EPS = 1e-5
STEPS = 52
MAX_BUCKETS, MAX_DISTANCE = 32, 128
ERF_P = 0.3275911
ERF_A = (0.254829592, -0.284496736, 1.421413741, -1.453152027, 1.061405429)


def group_steps(cur):
    nxt = cur + 1
    steps = []
    if nxt < 2 * NG:
        if nxt == NG:
            steps.append(("proj", 1, 0))
        steps.append(("rep", nxt, 0))
    for n in range(16):
        if cur >= 0:
            steps.append(("prob", cur, n))
        if nxt < 2 * NG:
            if nxt >= NG and n in (1, 3, 6, 9):
                steps.append(("rot", nxt, (1, 3, 6, 9).index(n)))
            if nxt >= NG and n in (3, 5, 8, 11):
                steps.append(("rot_split", nxt, (3, 5, 8, 11).index(n)))
            steps += [("max", nxt, m) for m in range(16) if 4 + m * 12 // 16 == n]
        if cur >= 0 and n in (5, 9, 13):
            steps.append(("pv", cur, (n - 5) // 4))
        if cur >= 1 and n == 3:
            steps.append(("heads", cur - 1, 0))
        if cur == NG and n == 7:
            steps.append(("out", 0, 0))
    if cur >= 0:
        steps += [("pv", cur, 3), ("acc", cur, 0)]
    if nxt < 2 * NG:
        steps.append(("shift", nxt, 0))
    if cur == 2 * NG - 1:
        steps += [("heads", cur, 0), ("out", 1, 0)]
    return steps


ATTENTION = [s for cur in range(-1, 2 * NG) for s in group_steps(cur)]

MISC = ["zT", "v0"]
for _what, _g, _ in ATTENTION:
    if _what == "proj":
        MISC += [f"v{_g}"]
    if _what == "shift":
        MISC += [f"shift{_g}"]
    if _what == "heads":
        MISC += [f"heads{_g}"]
    if _what == "out":
        MISC += [f"onT{_g}", f"out{_g}"]
MISC += ["x2T", "sel", "gT", "moe", "xn1T", "xfT", "router", "v1l", "wT", "fin"]
PAIR = ["proj0"]
for _what, _g, _h in ATTENTION:
    if _what in ("proj", "rep"):
        PAIR.append(f"{_what}{_g}")
    if _what == "rot":
        PAIR.append(f"rot{_g}_{_h}")
PAIR += [f"w{e}" for e in range(E1)]


def build(nc, io, out):
    rounds = io["x"].shape[0]
    ctx = ExitStack()
    with ctx:
        base = (nc.sbuf_base + 63) // 64 * 64
        cursor = [base]

        def at(name, shape, dt, where):
            return nc.alloc_sbuf_tensor_at(name, shape, dt, offset=where)

        def size(shape):
            return int(np.prod(shape[1:])) * 4

        def sb(name, shape, dt=F32):
            t = at(name, shape, dt, cursor[0])
            cursor[0] += (size(shape) + 31) // 32 * 32
            return t

        def region(nbytes, *layouts):
            start = cursor[0]
            got = []
            for layout in layouts:
                here = start
                for name, shape, dt in layout:
                    got.append(at(name, shape, dt, here))
                    here += (size(shape) + 31) // 32 * 32
                assert here - start <= nbytes, (here - start, nbytes)
            cursor[0] += nbytes
            return got

        ident = sb("ident", [P, P])
        strip = sb("strip", [P, NG, 9, 32], F32R)
        headmask = sb("headmask", [P, HG])
        pick = sb("pick", [64, E0], F32R)
        pick1 = sb("pick1", [16, E1], F32R)
        iota = sb("iota", [P, E0])
        tri = sb("tri", [P, P])
        pos_hi = sb("pos_hi", [P, T], F32R)
        pos_lo = sb("pos_lo", [P, T], F32R)
        cos_t = sb("cos_t", [P, T])
        sin_t = sb("sin_t", [P, T])
        biasl = sb("biasl", [P, T])
        w_att = sb("w_att", [P, 2, 3 * P])
        w_o = sb("w_o", [P, 2, P])
        w_l1 = sb("w_l1", [P, 2, P])
        w_sel = sb("w_sel", [P, E0])
        w_rt = sb("w_rt", [P, E1])
        keys_hi = sb("keys_hi", [P, E0, P], F32R)
        keys_lo = sb("keys_lo", [P, E0, P], F32R)
        vals = sb("vals", [P, E0, P])
        wpu = sb("wpu", [P, 4 * HG, 192], F32R)
        cols = sb("cols", [P, 24])
        rows = sb("rows", [P, 3, P])
        relb = sb("relb", [P, MAX_BUCKETS])
        neghalf = sb("neghalf", [P, TT])
        vext = sb("vext", [P, 2, TT, 4 * HG, 16])
        stat = sb("stat", [P, TT, 6])
        mv = sb("mv", [P, TT, 2])
        var = sb("var", [P, TT])
        rstd = sb("rstd", [P, TT])
        x_in = sb("x_in", [P, TT, P])
        xn = sb("xn", [P, TT, P])
        acc_tm = sb("acc_tm", [P, TT, P])
        q_hi = sb("q_hi", [P, T], F32R)
        q_lo = sb("q_lo", [P, T], F32R)
        k_hi = sb("k_hi", [P, T], F32R)
        k_lo = sb("k_lo", [P, T], F32R)
        qrep = sb("qrep", [P, 2, T], F32R)
        krep = sb("krep", [P, T])
        negmax = sb("negmax", [P, 2, TT, 32])
        rot_a = sb("rot_a", [P, 2, T])
        rot_b = sb("rot_b", [P, 2, T])
        o_sb = sb("o_sb", [P, T])
        on_tm = sb("on_tm", [P, TT, P])
        rden = sb("rden", [P, TT, HG])
        spare = sb("spare", [P, 1])
        pool_spare = sb("pool_spare", [P, 1])
        out_tm = sb("out_tm", [P, TT, P])

        (u_hi, u_lo, z_tm, hT0, hT1, gate_w, up_w, down_w, keys_f) = region(
            2 * 8 * T * 4,
            [("u_hi", [P, 8, T], F32R), ("u_lo", [P, 8, T], F32R)],
            [("z_tm", [P, TT, P], F32), ("hT0", [P, T], F32), ("hT1", [P, T], F32)],
            [("gate_w", [P, E1 + 1, 2 * P], F32), ("up_w", [P, E1 + 1, 2 * P], F32),
             ("down_w", [P, E1 + 1, 2, P], F32)],
            [("keys_f", [P, E0, P], F32)])
        (probs, kmask, src, z2, x2T, x2_hi, x2_lo, gate_bc, hmoe, sg0, eqt, gate, ghl, gT, m8, i8, i8f,
         x1, z1, xn1T, xfT, q1T, k1T, v1, lg, m81, i81, i81f, sc1, w_tm, whl, wT, xe, sg, hm,
         lz, la, lt, lp, prep_t, prep_e, pm_f, pos_f) = region(
            49 * 1024,
            [("probs", [P, 8, T], F32), ("kmask", [P, 8, T], F32R)],
            [("src", [P, TT, P], F32), ("z2", [P, TT, P], F32), ("x2T", [P, T], F32),
             ("x2_hi", [P, T], F32R), ("x2_lo", [P, T], F32R), ("gate_bc", [P, 2, T], F32),
             ("hmoe", [P, 2, T], F32), ("sg0", [P, TT, E0], F32), ("eqt", [P, TT, TOPK, E0], F32),
             ("gate", [P, TT, E0], F32), ("ghl", [P, TT, 2 * E0], F32), ("gT", [64, T], F32R),
             ("m8", [P, TT, 8], F32), ("i8", [P, TT, 8], U32), ("i8f", [P, TT, 8], F32)],
            [("x1", [P, TT, P], F32), ("z1", [P, TT, P], F32), ("xn1T", [P, T], F32),
             ("xfT", [P, T], F32), ("q1T", [P, T], F32), ("k1T", [P, T], F32),
             ("v1", [P, TT, P], F32), ("lg", [P, TT, E1], F32), ("m81", [P, TT, 8], F32),
             ("i81", [P, TT, 8], U32), ("i81f", [P, TT, 8], F32), ("sc1", [P, TT], F32),
             ("w_tm", [P, TT, E1], F32), ("whl", [P, TT, 2 * E1], F32), ("wT", [16, T], F32R),
             ("xe", [P, 2, T], F32), ("sg", [P, 2, T], F32), ("hm", [P, 2, T], F32),
             ("lz", [P, 10 * P], F32), ("la", [P, 10 * P], F32), ("lt", [P, 10 * P], F32),
             ("lp", [P, 10 * P], F32)],
            [("prep_t", [P, T], F32), ("prep_e", [P, T], F32), ("pm_f", [P, P], F32), ("pos_f", [P, T], F32)])
        assert cursor[0] <= nc.sbuf_usable_end, (cursor[0], nc.sbuf_usable_end)

        def bank(name, shape):
            return ctx.enter_context(nc.psum_tensor(name, shape, F32))

        ring1 = bank("ring1", [P, 2, T])
        ring2 = bank("ring2", [P, 2, T])
        acc = bank("acc", [P, T])
        pair = bank("pair", [P, 2, T])
        misc = bank("misc", [P, T])

        def sem(name):
            return ctx.enter_context(nc.semaphore(name))

        w_loaded = sem("w_loaded")
        keys_loaded = sem("keys_loaded")
        act_prep = sem("act_prep")
        dve_prep = sem("dve_prep")
        pe_prep = sem("pe_prep")
        pool_prep = sem("pool_prep")
        dve_step = sem("dve_step")
        x_loaded = sem("x_loaded")
        x_used = sem("x_used")
        ffn_loaded = sem("ffn_loaded")
        out_stored = sem("out_stored")
        round_done = sem("round_done")
        var_ready = sem("var_ready")
        rstd_ready = sem("rstd_ready")
        z_ready = sem("z_ready")
        misc_full = sem("misc_full")
        misc_free = sem("misc_free")
        pair_full = sem("pair_full")
        pair_free = sem("pair_free")
        ring1_full = sem("ring1_full")
        ring1_free = sem("ring1_free")
        ring2_full = sem("ring2_full")
        ring2_free = sem("ring2_free")
        acc_free = sem("acc_free")
        hi_ready = sem("hi_ready")
        mask_ready = sem("mask_ready")
        usum_ready = sem("usum_ready")
        uhi_ready = sem("uhi_ready")
        ulo_ready = sem("ulo_ready")
        pv_done = sem("pv_done")
        x2hi_ready = sem("x2hi_ready")
        x2lo_ready = sem("x2lo_ready")
        gate_ready = sem("gate_ready")
        val_done = sem("val_done")
        top1_ready = sem("top1_ready")
        top1exp_ready = sem("top1exp_ready")
        w_ready = sem("w_ready")
        q1_ready = sem("q1_ready")
        v1_ready = sem("v1_ready")
        labs_ready = sem("labs_ready")
        lsq_ready = sem("lsq_ready")
        lexp_ready = sem("lexp_ready")
        attn_ready = sem("attn_ready")
        down_done = sem("down_done")
        lap_done = sem("lap_done")

        GROUPS = 2 * NG
        ROTS = NG * HG
        LNS = 5
        FFN_LOADS = 7 * 16
        NM, NP = len(MISC), len(PAIR)
        R_ATT = GROUPS * 16
        R_SIM = R_ATT + E0
        R_FFN = R_SIM + TT
        N1 = R_FFN + 2 * (E1 + 1)
        R2_QK = R_ATT + E0
        R2_FFN = R2_QK + 1
        N2 = R2_FFN + 2 * (E1 + 1)
        NA = GROUPS + 2
        N_LOADS = 39

        (C_BQ, C_BK, C_GA, C_BA, C_G1, C_B1, C_G2, C_B2, C_BQK, C_GM0, C_GM1, C_BE0, C_BE1,
         C_LW, C_LB, C_Z) = range(16)

        def col(c):
            return cols[:, c:c + 1]

        def tiles(ap):
            return ap.rearrange("p (t c) -> p t c", t=TT)

        qkT = on_tm[:, :, :].rearrange("p t c -> p (t c)")
        LAP = [0, 4 * P, 7 * P, 9 * P, 10 * P]
        LAP_STD = (0.25 * np.pi) ** 0.5 * 2 ** 0.5
        LAP_MU = 0.5 ** 0.5
        block = ctx.enter_context(nc.Block())

        @block.sync
        def _(sp):
            n = 0
            with nc.allow_non_contiguous_dma(reason="per-feature columns, once"):
                for c, ap in ((C_BQ, io["b_qkv"][0:P]), (C_BK, io["b_qkv"][P:2 * P]), (C_GA, io["ga"]),
                              (C_BA, io["ba"]), (C_G1, io["ln1_g"]), (C_B1, io["ln1_b"]),
                              (C_G2, io["ln2_g"]), (C_B2, io["ln2_b"]), (C_BQK, io["bqk"]),
                              (C_GM0, io["gamma"][0, :]), (C_GM1, io["gamma"][1, :]),
                              (C_BE0, io["beta"][0, :]), (C_BE1, io["beta"][1, :]),
                              (C_LW, io["ln_w"]), (C_LB, io["ln_b"])):
                    sp.dma_start(col(c), ap.rearrange("(p a) -> p a", a=1)).then_inc(w_loaded, 16)
                    n += 1
            for dst, ap in ((ident[:, :], io["eye"]), (headmask[:, :], io["headmask"]),
                            (iota[:, :], io["iota"].partition_broadcast(P)), (tri[:, :], io["tri"]),
                            (pos_f[:, :], io["pos"]), (cos_t[:, :], io["cos"]), (sin_t[:, :], io["sin"]),
                            (krep[96:P, :], io["ones_rows"]), (biasl[:, :], io["bucket"]),
                            (relb[:, :], io["rel_emb"].rearrange("b a -> (b a)").partition_broadcast(P)),
                            (w_att[:, 0, :], io["w_qkv"]), (w_att[:, 1, 0:P], io["wq"]),
                            (w_att[:, 1, P:2 * P], io["wk"]), (w_att[:, 1, 2 * P:3 * P], io["wv"]),
                            (w_o[:, 0, :], io["w_out"]), (w_o[:, 1, :], io["wo"]),
                            (w_l1[:, 0, :], io["Wqk"]), (w_l1[:, 1, :], io["Wv"]),
                            (w_sel[:, :], io["sel_w"]), (w_rt[:, :], io["router_w"]),
                            (pm_f[:, :], io["wp"]),
                            (rows[:, 0, :], io["b_qkv"][2 * P:3 * P].partition_broadcast(P)),
                            (rows[:, 1, :], io["b_out"].partition_broadcast(P)),
                            (rows[:, 2, :], io["bv"].partition_broadcast(P))):
                sp.dma_start(dst, ap).then_inc(w_loaded, 16)
                n += 1
            assert n == N_LOADS
            sp.dma_start(keys_f[:, :, :], io["keys"].rearrange("e d s -> d e s")).then_inc(keys_loaded, 16)
            sp.dma_start(vals[:, :, :], io["values"].rearrange("e s d -> s e d")).then_inc(keys_loaded, 16)
            sp.dma_start(x_in[:, :, :], io["x"][0].rearrange("(t p) c -> p t c", p=P)).then_inc(x_loaded, 16)

            def one_round(it, last):
                if not last:
                    sp.wait_ge(x_used, it + 1)
                    sp.dma_start(x_in[:, :, :], io["x"][it + 1].rearrange("(t p) c -> p t c", p=P))\
                        .then_inc(x_loaded, 16)
                sp.wait_ge(pv_done, it * (4 * GROUPS) + 4 * GROUPS)
                sp.dma_start(gate_w[:, 0:E1, :], io["gate_w"].rearrange("e d i -> d e i")).then_inc(ffn_loaded, 16)
                sp.dma_start(gate_w[:, E1, :], io["sh_gate"]).then_inc(ffn_loaded, 16)
                sp.dma_start(up_w[:, 0:E1, :], io["up_w"].rearrange("e d i -> d e i")).then_inc(ffn_loaded, 16)
                sp.dma_start(up_w[:, E1, :], io["sh_up"]).then_inc(ffn_loaded, 16)
                for a in range(2):
                    sp.dma_start(down_w[:, 0:E1, a, :], io["down_w"][:, a * P:(a + 1) * P, :]
                                 .rearrange("e i h -> i e h")).then_inc(ffn_loaded, 16)
                sp.dma_start(down_w[:, E1, :, :],
                             io["sh_down"].rearrange("(a i) h -> i a h", a=2)).then_inc(ffn_loaded, 16)
                sp.wait_ge(misc_free, it * NM + NM)
                sp.dma_start(out[it].rearrange("(t p) c -> p t c", p=P), out_tm[:, :, :]).then_inc(out_stored, 16)

            with sp.Fori(0, rounds - 1) as it:
                one_round(it, False)
            one_round(rounds - 1, True)
            sp.wait_ge(out_stored, rounds * 16 + 16)

        @block.gpsimd
        def _(pool):
            pool.memset(neghalf[:, :], -0.5).then_inc(pool_prep, 1)
            pool.memset(vext[:, :, :, :, :], 0.0).then_inc(pool_prep, 1)
            pool.memset(negmax[:, :, :, :], 0.0).then_inc(pool_prep, 1)
            pool.wait_ge(pool_prep, 2)
            pool.memset(vext[:, :, :, :, HD:HD + 1], 1.0).then_inc(pool_prep, 1)
            pool.memset(out_tm[:, :, :], 0.0).then_inc(out_stored, 16)
            pool.wait_ge(pool_prep, 4)
            pool.wait_ge(w_loaded, N_LOADS * 16)
            pool.drain().then_inc(round_done, 1)
            with pool.Fori(0, rounds) as it:
                pool.wait_ge(round_done, it * 4 + 4)

                def power(n):
                    pool.wait_ge(var_ready, it * LNS + n + 1)
                    pool.tensor_tensor(rstd[:, :], var[:, :], neghalf[:, :], ALU.pow).then_inc(rstd_ready, 1)

                power(0)
                power(1)
                for what, g, n in ATTENTION:
                    b = g % 2
                    k = (g - NG) * HG + n
                    if what == "rep":
                        pool.wait_ge(pair_free, it * NP + PAIR.index(f"rep{g}") + 1)
                        if g >= 2:
                            pool.wait_ge(ring2_full, it * N2 + (g - 1) * 16)
                        pool.tensor_tensor(pool_spare[:, :], neghalf[:, 0:1], neghalf[:, 0:1], ALU.add)
                        for h in range(HG):
                            ins = pool.tensor_scalar(kmask[:, HG * b + h, :], krep[:, :], headmask[:, h:h + 1],
                                                     1.0, ALU.mult, ALU.mult)
                        ins.then_inc(mask_ready, 1)
                    elif what == "rot":
                        pool.wait_ge(pair_free, it * NP + PAIR.index(f"rot{g}_{n}") + 1)
                        pool.tensor_tensor(rot_a[:, k % 2, :], rot_a[:, k % 2, :], rot_b[:, k % 2, :],
                                           ALU.add).then_inc(usum_ready, 1)
                    elif what == "rot_split":
                        pool.wait_ge(uhi_ready, it * ROTS + k + 1)
                        pool.tensor_tensor(u_lo[:, HG * b + n, :], rot_a[:, k % 2, :],
                                           u_hi[:, HG * b + n, :].bitcast(F32), ALU.subtract).then_inc(ulo_ready, 1)
                power(2)
                power(3)
                power(4)
                pool.drain().then_inc(round_done, 1)

        @block.scalar
        def _(act):
            act.wait_ge(w_loaded, N_LOADS * 16)
            act.activation(pos_hi[:, :], pos_f[:, :], ACT.Copy).then_inc(act_prep, 1)
            act.wait_ge(pe_prep, 1)
            act.activation(q_hi[:, 0:P], misc[:, 0:P], ACT.Copy).then_inc(act_prep, 1)
            act.wait_ge(keys_loaded, 32)
            act.activation(keys_hi[:, :, :], keys_f[:, :, :], ACT.Copy).then_inc(act_prep, 1)
            act.drain().then_inc(round_done, 1)
            with act.Fori(0, rounds) as it:
                act.wait_ge(round_done, it * 4 + 4)

                def misc_filled(name):
                    return it * NM + MISC.index(name) + 1

                def project(a):
                    act.wait_ge(pair_full, it * NP + PAIR.index(f"proj{a}") + 1)
                    act.activation(q_hi[:, :], pair[:, 0, :], ACT.Identity, bias=col(C_Z if a else C_BQ))
                    act.activation(k_hi[:, :], pair[:, 1, :], ACT.Identity, bias=col(C_Z if a else C_BK))\
                        .then_inc(hi_ready, 1)

                project(0)
                for what, g, n in ATTENTION:
                    b = g % 2
                    if what == "proj":
                        project(g)
                    elif what == "rep":
                        act.wait_ge(pair_full, it * NP + PAIR.index(f"rep{g}") + 1)
                        if g >= 1:
                            act.wait_ge(mask_ready, it * GROUPS + g)
                        act.activation(qrep[0:96, b, :], pair[0:96, 0, :], ACT.Copy)
                        act.activation(krep[0:96, :], pair[0:96, 1, :], ACT.Copy).then_inc(pair_free, 1)
                    elif what == "prob":
                        i = g * 16 + n
                        act.wait_ge(ring2_full, it * N2 + i + 1)
                        if i >= 8:
                            act.wait_ge(pv_done, it * (4 * GROUPS) + i // 4 - 1)
                        act.activation(probs[:, i % 8, :], ring2[:, i % 2, :], ACT.Exp,
                                       scale=float(HD) ** -0.5).then_inc(ring2_free, 1)
                    elif what == "rot_split":
                        k = (g - NG) * HG + n
                        act.wait_ge(usum_ready, it * ROTS + k + 1)
                        act.activation(u_hi[:, HG * b + n, :], rot_a[:, k % 2, :], ACT.Copy).then_inc(uhi_ready, 1)
                    elif what == "shift":
                        act.wait_ge(misc_full, misc_filled(f"shift{g}"))
                        act.activation(qrep[96:P, b, :], misc[0:32, :], ACT.Copy).then_inc(misc_free, 1)
                    elif what == "acc":
                        act.wait_ge(pv_done, it * (4 * GROUPS) + 4 * (g + 1))
                        if g >= 1:
                            act.wait_ge(misc_full, misc_filled(f"heads{g - 1}"))
                        act.activation(o_sb[:, :], acc[:, :], ACT.Copy).then_inc(acc_free, 1)
                    elif what == "out":
                        act.wait_ge(misc_full, misc_filled(f"onT{g}"))
                        if g == 0:
                            act.wait_ge(out_stored, it * 16 + 16)
                        act.activation(tiles(out_tm[:, :, :].rearrange("p t c -> p (t c)")), tiles(misc[:, :]),
                                       ACT.Copy).then_inc(misc_free, 1)

                act.wait_ge(misc_free, misc_filled("x2T"))
                act.activation(x2_hi[:, :], x2T[:, :], ACT.Copy).then_inc(x2hi_ready, 1)
                act.wait_ge(misc_full, misc_filled("sel"))
                act.activation(sg0[:, :, :].rearrange("p t e -> p (t e)"), misc[:, 0:TT * E0], ACT.Exp,
                               scale=-1.0).then_inc(misc_free, 1)
                act.wait_ge(misc_full, misc_filled("gT"))
                act.activation(gT[:, :], misc[0:64, :], ACT.Copy).then_inc(misc_free, 1)
                for e in range(E0):
                    act.wait_ge(ring2_full, it * N2 + R_ATT + e + 1)
                    if e >= 2:
                        act.wait_ge(ring1_free, it * N1 + R_ATT + e - 1)
                    act.activation(gate_bc[:, e % 2, :], ring2[:, (R_ATT + e) % 2, :], ACT.Copy)\
                        .then_inc(ring2_free, 1)
                act.wait_ge(val_done, it * E0 + E0)
                act.activation(o_sb[:, :], acc[:, :], ACT.Copy).then_inc(acc_free, 1)

                act.wait_ge(misc_full, misc_filled("xn1T"))
                act.activation(xn1T[:, :], misc[:, :], ACT.Copy).then_inc(misc_free, 1)
                act.wait_ge(top1_ready, it + 1)
                act.activation(sc1[:, :], m81[:, :, 0], ACT.Exp, scale=-1.0).then_inc(top1exp_ready, 1)
                act.wait_ge(ring2_full, it * N2 + R2_QK + 1)
                act.activation(qkT, ring2[:, R2_QK % 2, :], ACT.Silu, bias=col(C_BQK)).then_inc(ring2_free, 1)
                act.wait_ge(misc_free, misc_filled("v1l"))
                act.activation(v1[:, :, :], v1[:, :, :], ACT.Silu).then_inc(v1_ready, 1)
                act.wait_ge(misc_full, misc_filled("wT"))
                act.activation(wT[:, :], misc[0:16, :], ACT.Copy).then_inc(misc_free, 1)
                act.wait_ge(ring1_free, it * N1 + R_FFN)
                act.activation(la[:, :], lz[:, :], ACT.Abs).then_inc(labs_ready, 1)
                for i in range(2 * (E1 + 1)):
                    act.wait_ge(ring2_full, it * N2 + R2_FFN + i + 1)
                    if i >= 2:
                        act.wait_ge(ring1_free, it * N1 + R_FFN + i - 1)
                    act.activation(sg[:, i % 2, :], ring2[:, (R2_FFN + i) % 2, :], ACT.Silu).then_inc(ring2_free, 1)
                    if i == 5:
                        act.wait_ge(lsq_ready, it + 1)
                        act.activation(lp[:, :], lp[:, :], ACT.Exp, scale=-1.0).then_inc(lexp_ready, 1)
                act.wait_ge(lap_done, it + 1)
                act.activation(o_sb[:, :], acc[:, :], ACT.Copy).then_inc(acc_free, 1)
                act.drain().then_inc(round_done, 1)

        @block.tensor
        def _(pe):
            pe.wait_ge(w_loaded, N_LOADS * 16)
            pe.transpose(misc[:, 0:P], pm_f[:, :], ident[:, :]).then_inc(pe_prep, 1)
            pe.wait_ge(dve_prep, 2)
            for g in range(NG):
                pe.matmul(pair[:, 0, g * P:(g + 1) * P], strip[:, g, 4:8, :], q_hi[:, 0:P], start=True, stop=False)
                ins = pe.matmul(pair[:, 0, g * P:(g + 1) * P], strip[:, g, 5:9, :], q_lo[:, 0:P],
                                start=False, stop=True)
            ins.then_inc(pe_prep, 1)
            pe.drain().then_inc(round_done, 1)
            with pe.Fori(0, rounds) as it:
                pe.wait_ge(round_done, it * 4 + 4)

                def misc_turn(name):
                    if MISC.index(name):
                        pe.wait_ge(misc_free, it * NM + MISC.index(name))

                def pair_turn(name):
                    if PAIR.index(name):
                        pe.wait_ge(pair_free, it * NP + PAIR.index(name))

                def transposed(src_tm, name):
                    misc_turn(name)
                    for t in range(TT):
                        ins = pe.transpose(misc[:, t * P:(t + 1) * P], src_tm[:, t * P:(t + 1) * P], ident[:, :])
                    ins.then_inc(misc_full, 1)

                def flat(ap):
                    return ap[:, :, :].rearrange("p t c -> p (t c)")

                def token_major(name, lhs, rhs, width):
                    misc_turn(name)
                    for t in range(TT):
                        ins = pe.matmul(misc[:, t * width:(t + 1) * width], lhs[:, t * P:(t + 1) * P], rhs,
                                        start=True, stop=True)
                    ins.then_inc(misc_full, 1)

                def project(a):
                    hT = hT1 if a else hT0
                    pair_turn(f"proj{a}")
                    pe.matmul(pair[:, 0, :], w_att[:, a, 0:P], hT[:, :], start=True, stop=True)
                    pe.matmul(pair[:, 1, :], w_att[:, a, P:2 * P], hT[:, :], start=True, stop=True)\
                        .then_inc(pair_full, 1)
                    token_major(f"v{a}", hT, w_att[:, a, 2 * P:3 * P], P)

                pe.wait_ge(z_ready, it * 4 + 1)
                transposed(flat(z_tm), "zT")
                pe.wait_ge(misc_free, it * NM + 1)
                project(0)
                for what, g, n in ATTENTION:
                    b = g % 2
                    rel = g >= NG
                    if what == "proj":
                        project(g)
                    elif what == "rep":
                        pair_turn(f"rep{g}")
                        gl = g % NG
                        pe.matmul(pair[:, 0, :], strip[:, gl, 0:4, :], q_hi[:, :], start=True, stop=False)
                        pe.matmul(pair[:, 0, :], strip[:, gl, 2:6, :], q_lo[:, :], start=False, stop=True)
                        pe.matmul(pair[:, 1, :], strip[:, gl, 4:8, :], k_hi[:, :], start=True, stop=False)
                        pe.matmul(pair[:, 1, :], strip[:, gl, 5:9, :], k_lo[:, :], start=False, stop=True)\
                            .then_inc(pair_full, 1)
                    elif what == "rot":
                        pair_turn(f"rot{g}_{n}")
                        head = (g - NG) * HG + n
                        pe.matmul(pair[:, 0, :], wpu[0:96, head, 0:P], qrep[0:96, b, :], start=True, stop=True)
                        pe.matmul(pair[:, 1, :], wpu[0:96, head, 64:192], qrep[0:96, b, :], start=True, stop=True)\
                            .then_inc(pair_full, 1)
                    elif what == "max":
                        h, t = n // TT, n % TT
                        i = g * 16 + n
                        if n == 0:
                            pe.wait_ge(pair_free, it * NP + PAIR.index(f"rep{g}") + 1)
                            pe.wait_ge(mask_ready, it * GROUPS + g + 1)
                        if rel and t == 0:
                            pe.wait_ge(uhi_ready, it * ROTS + (g - NG) * HG + h + 1)
                        if i >= 2:
                            pe.wait_ge(ring1_free, it * N1 + i - 1)
                        ins = pe.matmul(ring1[:, i % 2, :], qrep[0:96, b, t * P:(t + 1) * P],
                                        kmask[0:96, HG * b + h, :], start=True, stop=not rel)
                        if rel:
                            ins = pe.matmul(ring1[:, i % 2, :], u_hi[:, HG * b + h, t * P:(t + 1) * P],
                                            pos_hi[:, :], start=False, stop=True)
                        ins.then_inc(ring1_full, 1)
                    elif what == "shift":
                        pe.wait_ge(ring1_free, it * N1 + (g + 1) * 16)
                        misc_turn(f"shift{g}")
                        for t in range(TT):
                            ins = pe.transpose(misc[0:32, t * P:(t + 1) * P], negmax[:, b, t, :], ident[:, :])
                        ins.then_inc(misc_full, 1)
                    elif what == "prob":
                        t, h = n // HG, n % HG
                        i = g * 16 + n
                        if n == 0:
                            pe.wait_ge(misc_free, it * NM + MISC.index(f"shift{g}") + 1)
                            if rel:
                                pe.wait_ge(ulo_ready, it * ROTS + (g - NG + 1) * HG)
                        if i >= 2:
                            pe.wait_ge(ring2_free, it * N2 + i - 1)
                        keys = slice(t * P, (t + 1) * P)
                        ins = pe.matmul(ring2[:, i % 2, :], kmask[:, HG * b + h, keys], qrep[:, b, :],
                                        start=True, stop=not rel)
                        if rel:
                            pe.matmul(ring2[:, i % 2, :], pos_hi[:, keys], u_hi[:, HG * b + h, :],
                                      start=False, stop=False)
                            pe.matmul(ring2[:, i % 2, :], pos_lo[:, keys], u_hi[:, HG * b + h, :],
                                      start=False, stop=False)
                            ins = pe.matmul(ring2[:, i % 2, :], pos_hi[:, keys], u_lo[:, HG * b + h, :],
                                            start=False, stop=True)
                        ins.then_inc(ring2_full, 1)
                    elif what == "pv":
                        pe.wait_ge(ring2_free, it * N2 + g * 16 + HG * (n + 1))
                        if n == 0:
                            pe.wait_ge(misc_free, it * NM + MISC.index(f"v{g // NG}") + 1)
                            if g >= 1:
                                pe.wait_ge(acc_free, it * NA + g)
                        for h in range(HG):
                            ins = pe.matmul(acc[32 * h:32 * h + 16, :], vext[:, g // NG, n, HG * (g % NG) + h, :],
                                            probs[:, (g * 16 + HG * n + h) % 8, :], start=n == 0, stop=n == TT - 1)
                        ins.then_inc(pv_done, 1)
                    elif what == "heads":
                        pe.wait_ge(acc_free, it * NA + g + 1)
                        transposed(o_sb, f"heads{g}")
                    elif what == "out":
                        transposed(flat(on_tm), f"onT{g}")
                        token_major(f"out{g}", flat(out_tm), w_o[:, g, :], P)

                pe.wait_ge(z_ready, it * 4 + 2)
                transposed(flat(z2), "x2T")
                token_major("sel", x2T, w_sel[:, :], E0)
                pe.wait_ge(gate_ready, it + 1)
                misc_turn("gT")
                for t in range(TT):
                    ins = pe.matmul(misc[0:64, t * P:(t + 1) * P], ghl[:, t, :], ident[:, :], start=True, stop=True)
                ins.then_inc(misc_full, 1)
                pe.wait_ge(x2lo_ready, it + 1)
                pe.wait_ge(misc_free, it * NM + MISC.index("gT") + 1)

                def values(e):
                    pe.wait_ge(ring1_free, it * N1 + R_ATT + e + 1)
                    if e == 0:
                        pe.wait_ge(acc_free, it * NA + GROUPS)
                    pe.matmul(acc[:, :], vals[:, e, :], hmoe[:, e % 2, :], start=e == 0, stop=e == E0 - 1)\
                        .then_inc(val_done, 1)

                for e in range(E0):
                    i = R_ATT + e
                    pe.wait_ge(ring2_free, it * N2 + i - 1)
                    pe.matmul(ring2[:, i % 2, :], pick[:, e:e + 1].to_broadcast([64, P]), gT[:, :],
                              start=True, stop=True).then_inc(ring2_full, 1)
                    pe.wait_ge(ring1_free, it * N1 + i - 1)
                    pe.matmul(ring1[:, i % 2, :], keys_hi[:, e, :], x2_hi[:, :], start=True, stop=False)
                    pe.matmul(ring1[:, i % 2, :], keys_hi[:, e, :], x2_lo[:, :], start=False, stop=False)
                    pe.matmul(ring1[:, i % 2, :], keys_lo[:, e, :], x2_hi[:, :], start=False, stop=True)\
                        .then_inc(ring1_full, 1)
                    if e:
                        values(e - 1)
                values(E0 - 1)
                pe.wait_ge(acc_free, it * NA + GROUPS + 1)
                transposed(o_sb, "moe")

                pe.wait_ge(z_ready, it * 4 + 3)
                transposed(flat(xn), "xn1T")
                pe.wait_ge(z_ready, it * 4 + 4)
                transposed(flat(z1), "xfT")
                token_major("router", xfT, w_rt[:, :], E1)
                pe.wait_ge(ring2_free, it * N2 + R2_QK - 1)
                pe.matmul(ring2[:, R2_QK % 2, :], w_l1[:, 0, :], xn1T[:, :], start=True, stop=True)\
                    .then_inc(ring2_full, 1)
                token_major("v1l", xn1T, w_l1[:, 1, :], P)
                pe.wait_ge(q1_ready, it + 1)
                for jt in range(TT):
                    i = R_SIM + jt
                    pe.wait_ge(ring1_free, it * N1 + i - 1)
                    pe.matmul(ring1[:, i % 2, 0:T - jt * P], k1T[:, jt * P:(jt + 1) * P], q1T[:, jt * P:T],
                              start=True, stop=True).then_inc(ring1_full, 1)
                pe.wait_ge(w_ready, it + 1)
                misc_turn("wT")
                for t in range(TT):
                    ins = pe.transpose(misc[0:16, t * P:(t + 1) * P], whl[:, t, :], ident[:, :])
                ins.then_inc(misc_full, 1)
                pe.wait_ge(misc_free, it * NM + MISC.index("wT") + 1)
                pe.wait_ge(ffn_loaded, it * FFN_LOADS + FFN_LOADS)

                def weight(e):
                    pair_turn(f"w{e}")
                    pe.matmul(pair[:, 0, :], pick1[:, e:e + 1].to_broadcast([16, P]), wT[:, :],
                              start=True, stop=True).then_inc(pair_full, 1)

                def down(e):
                    for a in range(2):
                        i = 2 * e + a
                        pe.wait_ge(ring1_free, it * N1 + R_FFN + i + 1)
                        if i == 0:
                            pe.wait_ge(acc_free, it * NA + GROUPS + 1)
                        pe.matmul(acc[:, :], down_w[:, e, a, :], hm[:, i % 2, :], start=i == 0, stop=False)\
                            .then_inc(down_done, 1)

                weight(0)
                for e in range(E1 + 1):
                    if e + 1 < E1:
                        weight(e + 1)
                    if e < E1:
                        pe.wait_ge(pair_free, it * NP + PAIR.index(f"w{e}") + 1)
                    src_e = xe[:, e % 2, :] if e < E1 else xfT[:, :]
                    for a in range(2):
                        i = 2 * e + a
                        pe.wait_ge(ring2_free, it * N2 + R2_FFN + i - 1)
                        pe.matmul(ring2[:, (R2_FFN + i) % 2, :], gate_w[:, e, a * P:(a + 1) * P], src_e,
                                  start=True, stop=True).then_inc(ring2_full, 1)
                        pe.wait_ge(ring1_free, it * N1 + R_FFN + i - 1)
                        pe.matmul(ring1[:, (R_FFN + i) % 2, :], up_w[:, e, a * P:(a + 1) * P], src_e,
                                  start=True, stop=True).then_inc(ring1_full, 1)
                    if e:
                        down(e - 1)
                down(E1)
                pe.wait_ge(attn_ready, it + 1)
                pe.wait_ge(v1_ready, it + 1)
                for jt in reversed(range(TT)):
                    ins = pe.matmul(acc[:, jt * P:T], v1[:, jt, :], lz[:, LAP[jt]:LAP[jt + 1]],
                                    start=False, stop=jt == 0)
                ins.then_inc(lap_done, 1)
                pe.wait_ge(acc_free, it * NA + GROUPS + 2)
                transposed(o_sb, "fin")
                pe.drain().then_inc(round_done, 1)

        @block.vector
        def _(dve):
            steps = [0]

            def prep(ins):
                steps[0] += 1
                ins.then_inc(dve_step, 1)
                dve.wait_ge(dve_step, steps[0])

            prep(dve.memset(cols[:, C_Z:C_Z + 1], 0.0))
            prep(dve.memset(strip[:, :, :, :].bitcast(F32), 0.0))
            dve.wait_ge(w_loaded, N_LOADS * 16)
            for blk in (0, 1, 4, 6):
                prep(dve.tensor_copy(strip[:, :, blk, :], ident[:, :].rearrange("p (g c) -> p g c", g=NG)))
            prep(dve.tensor_copy(pick[0:32, :], ident[0:32, 0:32]))
            prep(dve.tensor_copy(pick[32:64, :], ident[32:64, 32:64]))
            prep(dve.tensor_tensor(pick1[:, :], ident[0:16, 0:E1], ident[0:16, E1:2 * E1], ALU.add))
            dve.wait_ge(act_prep, 1)
            dve.tensor_tensor(pos_lo[:, :], pos_f[:, :], pos_hi[:, :].bitcast(F32), ALU.subtract)\
                .then_inc(dve_prep, 1)
            dve.wait_ge(act_prep, 2)
            dve.tensor_tensor(q_lo[:, 0:P], misc[:, 0:P], q_hi[:, 0:P].bitcast(F32), ALU.subtract)\
                .then_inc(dve_prep, 1)
            prep(dve.tensor_scalar(prep_t[:, :], biasl[:, :], 0.0, relb[:, 0:1], ALU.is_equal, ALU.mult))
            for n in range(1, MAX_BUCKETS):
                prep(dve.tensor_scalar(prep_e[:, :], biasl[:, :], float(n), relb[:, n:n + 1],
                                       ALU.is_equal, ALU.mult))
                prep(dve.tensor_tensor(prep_t[:, :], prep_t[:, :], prep_e[:, :], ALU.add))
            prep(dve.tensor_scalar(biasl[:, :], prep_t[:, :], float(P ** 0.5 / LAP_STD), float(-LAP_MU / LAP_STD),
                                   ALU.mult, ALU.add))
            dve.wait_ge(pe_prep, 2)
            for g in range(NG):
                for h in range(HG):
                    w = pair[:, 0, g * P:(g + 1) * P]
                    dve.tensor_scalar(wpu[:, g * HG + h, 0:P], w, headmask[:, h:h + 1], None, ALU.mult)
                    ins = dve.tensor_scalar(wpu[:, g * HG + h, P:192], w[:, 0:64], headmask[:, h:h + 1], None, ALU.mult)
            prep(ins)
            prep(dve.memset(acc[:, :], 0.0))
            dve.wait_ge(act_prep, 3)
            dve.tensor_tensor(keys_lo[:, :, :], keys_f[:, :, :], keys_hi[:, :, :].bitcast(F32), ALU.subtract)\
                .then_inc(dve_prep, 1)
            dve.memset(stat[:, :, :], 0.0).then_inc(dve_prep, 1)
            dve.drain().then_inc(round_done, 1)
            BEFORE = steps[0]
            steps[0] = 0
            with dve.Fori(0, rounds) as it:
                dve.wait_ge(round_done, it * 4 + 4)

                def chain(ins):
                    steps[0] += 1
                    ins.then_inc(dve_step, 1)
                    dve.wait_ge(dve_step, it * STEPS + BEFORE + steps[0])

                def settle():
                    dve.memset(spare[:, :], 0.0)

                def misc_filled(name):
                    dve.wait_ge(misc_full, it * NM + MISC.index(name) + 1)

                def layer_norm(n, src_tm, dst_tm):
                    for t in range(TT):
                        ins = dve.bn_stats(stat[:, t, :], src_tm[:, t, :])
                    chain(ins)
                    settle()
                    for t in range(TT):
                        ins = dve.bn_aggr(mv[:, t, :], stat[:, t, :])
                    chain(ins)
                    dve.tensor_scalar(var[:, :], mv[:, :, 1], EPS, None, ALU.add).then_inc(var_ready, 1)
                    dve.wait_ge(rstd_ready, it * LNS + n + 1)
                    for t in range(TT):
                        ins = dve.tensor_scalar(dst_tm[:, t, :], src_tm[:, t, :], mv[:, t, 0:1], rstd[:, t:t + 1],
                                                ALU.subtract, ALU.mult)
                    return ins

                def project(a):
                    dve.wait_ge(pair_full, it * NP + PAIR.index(f"proj{a}") + 1)
                    dve.wait_ge(hi_ready, it * 2 + a + 1)
                    dve.scalar_tensor_tensor(q_lo[:, :], pair[:, 0, :], col(C_Z if a else C_BQ),
                                             q_hi[:, :].bitcast(F32), ALU.add, ALU.subtract)
                    dve.scalar_tensor_tensor(k_lo[:, :], pair[:, 1, :], col(C_Z if a else C_BK),
                                             k_hi[:, :].bitcast(F32), ALU.add, ALU.subtract).then_inc(pair_free, 1)
                    misc_filled(f"v{a}")
                    v = misc[:, :].rearrange("p (t h d) -> p t h d", t=TT, d=HD)
                    if a:
                        ins = dve.tensor_copy(vext[:, 1, :, :, 0:HD], v)
                    else:
                        bias = rows[:, 0:1, :].rearrange("p a (h d) -> p a h d", d=HD)
                        ins = dve.tensor_tensor(vext[:, 0, :, :, 0:HD], v, bias.to_broadcast([P, TT, 4 * HG, HD]),
                                                ALU.add)
                    ins.then_inc(misc_free, 1)

                dve.wait_ge(x_loaded, it * 16 + 16)
                chain(layer_norm(0, x_in, xn))
                dve.scalar_tensor_tensor(acc_tm[:, :, :], xn[:, :, :], 2.0, x_in[:, :, :], ALU.mult, ALU.add)\
                    .then_inc(x_used, 1)
                layer_norm(1, xn, z_tm).then_inc(z_ready, 1)
                misc_filled("zT")
                dve.tensor_scalar(hT0[:, :], misc[:, :], col(C_GA), col(C_BA), ALU.mult, ALU.add)
                dve.tensor_scalar(hT1[:, :], misc[:, :], col(C_G1), col(C_B1), ALU.mult, ALU.add)\
                    .then_inc(misc_free, 1)
                project(0)
                for what, g, n in ATTENTION:
                    b = g % 2
                    if what == "proj":
                        project(g)
                    elif what == "rot":
                        k = (g - NG) * HG + n
                        dve.wait_ge(pair_full, it * NP + PAIR.index(f"rot{g}_{n}") + 1)
                        if k >= 2:
                            dve.wait_ge(ulo_ready, it * ROTS + k - 1)
                        dve.tensor_tensor(rot_a[:, k % 2, :], pair[:, 0, :], cos_t[:, :], ALU.mult)
                        dve.tensor_tensor(rot_b[:, k % 2, :], pair[:, 1, :], sin_t[:, :], ALU.mult)\
                            .then_inc(pair_free, 1)
                    elif what == "max":
                        h, t = n // TT, n % TT
                        i = g * 16 + n
                        dve.wait_ge(ring1_full, it * N1 + i + 1)
                        if n == 0 and g >= 2:
                            misc_filled(f"shift{g - 2}")
                        dve.tensor_reduce(negmax[:, b, t, h:h + 1], ring1[:, i % 2, :], AX.X, ALU.max,
                                          negate=True).then_inc(ring1_free, 1)
                    elif what == "heads":
                        misc_filled(f"heads{g}")
                        o = misc[:, :].rearrange("p (t h d) -> p t h d", t=TT, h=HG)
                        chain(dve.reciprocal(rden[:, :, :], o[:, :, :, HD]))
                        gl = g % NG
                        dst = on_tm[:, :, 32 * gl:32 * gl + 32].rearrange("p t (h d) -> p t h d", h=HG)
                        dve.tensor_tensor(dst, o[:, :, :, 0:HD],
                                          rden[:, :, :].unsqueeze(3).to_broadcast([P, TT, HG, HD]), ALU.mult)\
                            .then_inc(misc_free, 1)
                    elif what == "out":
                        misc_filled(f"out{g}")
                        o = tiles(misc[:, :])
                        if g == 0:
                            dve.tensor_tensor(acc_tm[:, :, :], acc_tm[:, :, :], o, ALU.add).then_inc(misc_free, 1)
                            dve.wait_ge(misc_free, it * NM + MISC.index("out0") + 1)
                            chain(dve.tensor_tensor(acc_tm[:, :, :], acc_tm[:, :, :],
                                                    rows[:, 1:2, :].to_broadcast([P, TT, P]), ALU.add))
                        else:
                            chain(dve.tensor_tensor(src[:, :, :], xn[:, :, :], o, ALU.add))
                            dve.tensor_tensor(acc_tm[:, :, :], acc_tm[:, :, :], o, ALU.add).then_inc(misc_free, 1)

                layer_norm(2, src, z2).then_inc(z_ready, 1)
                misc_filled("x2T")
                dve.tensor_scalar(x2T[:, :], misc[:, :], col(C_G2), col(C_B2), ALU.mult, ALU.add)\
                    .then_inc(misc_free, 1)
                dve.wait_ge(x2hi_ready, it + 1)
                dve.tensor_tensor(x2_lo[:, :], x2T[:, :], x2_hi[:, :].bitcast(F32), ALU.subtract)\
                    .then_inc(x2lo_ready, 1)
                dve.wait_ge(misc_free, it * NM + MISC.index("sel") + 1)
                chain(dve.tensor_scalar(sg0[:, :, :], sg0[:, :, :], 1.0, None, ALU.add))
                chain(dve.reciprocal(sg0[:, :, :], sg0[:, :, :]))
                settle()
                for t in range(TT):
                    ins = dve.max(m8[:, t, :], sg0[:, t, :])
                chain(ins)
                settle()
                for t in range(TT):
                    ins = dve.max_index(i8[:, t, :], m8[:, t, :], sg0[:, t, :])
                chain(ins)
                chain(dve.tensor_copy(i8f[:, :, :], i8[:, :, :]))
                full = [P, TT, TOPK, E0]
                chain(dve.tensor_tensor(eqt[:, :, :, :], iota[:, :].unsqueeze(1).unsqueeze(1).to_broadcast(full),
                                        i8f[:, :, 0:TOPK].unsqueeze(3).to_broadcast(full), ALU.is_equal))
                chain(dve.tensor_tensor(eqt[:, :, :, :], eqt[:, :, :, :],
                                        m8[:, :, 0:TOPK].unsqueeze(3).to_broadcast(full), ALU.mult))
                chain(dve.tensor_reduce(gate[:, :, :], eqt[:, :, :, :].rearrange("p t k e -> p t e k"), AX.X, ALU.add))
                chain(dve.tensor_copy(ghl[:, :, 0:E0].bitcast(F32R), gate[:, :, :]))
                dve.tensor_tensor(ghl[:, :, E0:2 * E0], gate[:, :, :], ghl[:, :, 0:E0], ALU.subtract)\
                    .then_inc(gate_ready, 1)
                for e in range(E0):
                    i = R_ATT + e
                    dve.wait_ge(ring1_full, it * N1 + i + 1)
                    dve.wait_ge(ring2_free, it * N2 + i + 1)
                    if e >= 2:
                        dve.wait_ge(val_done, it * E0 + e - 1)
                    dve.scalar_tensor_tensor(hmoe[:, e % 2, :], ring1[:, i % 2, :], 0.0, gate_bc[:, e % 2, :],
                                             ALU.max, ALU.mult).then_inc(ring1_free, 1)
                misc_filled("moe")
                dve.tensor_tensor(x1[:, :, :], acc_tm[:, :, :], tiles(misc[:, :]), ALU.add).then_inc(misc_free, 1)
                dve.wait_ge(misc_free, it * NM + MISC.index("moe") + 1)

                ins = layer_norm(3, x1, xn)
                ins.then_inc(z_ready, 1)
                dve.wait_ge(z_ready, it * 4 + 3)
                chain(dve.tensor_tensor(acc_tm[:, :, :], x1[:, :, :], xn[:, :, :], ALU.add))
                layer_norm(4, xn, z1).then_inc(z_ready, 1)
                misc_filled("xfT")
                dve.tensor_scalar(xfT[:, :], misc[:, :], col(C_LW), col(C_LB), ALU.mult, ALU.add)\
                    .then_inc(misc_free, 1)
                misc_filled("router")
                dve.tensor_copy(lg[:, :, :].rearrange("p t e -> p (t e)"), misc[:, 0:TT * E1]).then_inc(misc_free, 1)
                dve.wait_ge(misc_free, it * NM + MISC.index("router") + 1)
                settle()
                for t in range(TT):
                    ins = dve.max(m81[:, t, :], lg[:, t, :])
                ins.then_inc(top1_ready, 1)
                dve.wait_ge(top1_ready, it + 1)
                settle()
                for t in range(TT):
                    ins = dve.max_index(i81[:, t, :], m81[:, t, :], lg[:, t, :])
                chain(ins)
                chain(dve.tensor_copy(i81f[:, :, :], i81[:, :, :]))
                dve.wait_ge(top1exp_ready, it + 1)
                chain(dve.tensor_scalar(sc1[:, :], sc1[:, :], 1.0, None, ALU.add))
                chain(dve.reciprocal(sc1[:, :], sc1[:, :]))
                full = [P, TT, E1]
                chain(dve.tensor_tensor(w_tm[:, :, :], iota[:, 0:E1].unsqueeze(1).to_broadcast(full),
                                        i81f[:, :, 0:1].to_broadcast(full), ALU.is_equal))
                chain(dve.tensor_tensor(w_tm[:, :, :], w_tm[:, :, :], sc1[:, :].unsqueeze(2).to_broadcast(full),
                                        ALU.mult))
                chain(dve.tensor_copy(whl[:, :, 0:E1].bitcast(F32R), w_tm[:, :, :]))
                dve.tensor_tensor(whl[:, :, E1:2 * E1], w_tm[:, :, :], whl[:, :, 0:E1], ALU.subtract)\
                    .then_inc(w_ready, 1)
                dve.wait_ge(ring2_free, it * N2 + R2_QK + 1)
                dve.tensor_scalar(q1T[:, :], qkT, col(C_GM0), col(C_BE0), ALU.mult, ALU.add)
                dve.tensor_scalar(k1T[:, :], qkT, col(C_GM1), col(C_BE1), ALU.mult, ALU.add).then_inc(q1_ready, 1)
                misc_filled("v1l")
                dve.tensor_tensor(v1[:, :, :], tiles(misc[:, :]), rows[:, 2:3, :].to_broadcast([P, TT, P]),
                                  ALU.add).then_inc(misc_free, 1)
                for jt in range(TT):
                    i = R_SIM + jt
                    dve.wait_ge(ring1_full, it * N1 + i + 1)
                    dve.scalar_tensor_tensor(lz[:, LAP[jt]:LAP[jt + 1]], ring1[:, i % 2, 0:T - jt * P],
                                             float(1.0 / (T * LAP_STD)), biasl[:, 0:T - jt * P], ALU.mult, ALU.add)\
                        .then_inc(ring1_free, 1)

                def erf_step(n):
                    if n == 0:
                        dve.wait_ge(labs_ready, it + 1)
                        dve.tensor_tensor(lp[:, :], la[:, :], la[:, :], ALU.mult).then_inc(lsq_ready, 1)
                        chain(dve.tensor_scalar(lt[:, :], la[:, :], ERF_P, 1.0, ALU.mult, ALU.add))
                    elif n <= 4:
                        part = slice((n - 1) * 320, n * 320)
                        chain(dve.reciprocal(lt[:, part], lt[:, part]))
                    elif n == 5:
                        chain(dve.tensor_scalar(la[:, :], lt[:, :], ERF_A[4], None, ALU.mult))
                    elif n <= 9:
                        chain(dve.scalar_tensor_tensor(la[:, :], la[:, :], ERF_A[9 - n], lt[:, :], ALU.add, ALU.mult))
                    elif n == 10:
                        dve.wait_ge(lexp_ready, it + 1)
                        chain(dve.tensor_tensor(la[:, :], la[:, :], lp[:, :], ALU.mult))
                    elif n == 11:
                        chain(dve.tensor_scalar(lt[:, :], lz[:, :], 0.0, None, ALU.is_ge))
                    elif n == 12:
                        chain(dve.scalar_tensor_tensor(la[:, :], lt[:, :], -0.5, la[:, :], ALU.add, ALU.mult))
                    elif n == 13:
                        chain(dve.tensor_tensor(lz[:, :], lt[:, :], la[:, :], ALU.subtract))
                    elif n == 14:
                        for jt in range(TT):
                            diag = lz[:, LAP[jt]:LAP[jt] + P]
                            ins = dve.tensor_tensor(diag, diag, tri[:, :], ALU.mult)
                        ins.then_inc(attn_ready, 1)

                def expert_input(e):
                    dve.wait_ge(pair_full, it * NP + PAIR.index(f"w{e}") + 1)
                    if e >= 2:
                        dve.wait_ge(ring1_full, it * N1 + R_FFN + 2 * (e - 2) + 2)
                    dve.tensor_tensor(xe[:, e % 2, :], xfT[:, :], pair[:, 0, :], ALU.mult).then_inc(pair_free, 1)

                expert_input(0)
                for e in range(E1 + 1):
                    if e + 1 < E1:
                        expert_input(e + 1)
                    for a in range(2):
                        i = 2 * e + a
                        dve.wait_ge(ring1_full, it * N1 + R_FFN + i + 1)
                        dve.wait_ge(ring2_free, it * N2 + R2_FFN + i + 1)
                        if i >= 2:
                            dve.wait_ge(down_done, it * (2 * (E1 + 1)) + i - 1)
                        dve.tensor_tensor(hm[:, i % 2, :], sg[:, i % 2, :], ring1[:, (R_FFN + i) % 2, :],
                                          ALU.mult).then_inc(ring1_free, 1)
                        if i < 15:
                            erf_step(i)
                misc_filled("fin")
                dve.tensor_tensor(out_tm[:, :, :], acc_tm[:, :, :], tiles(misc[:, :]), ALU.add).then_inc(misc_free, 1)
                dve.drain().then_inc(round_done, 1)

                assert steps[0] == STEPS, steps[0]


_INS = {"x": "L0_attn_x", "ga": "L0_attn_ln_gamma", "ba": "L0_attn_ln_beta", "w_qkv": "L0_attn_w_qkv",
        "b_qkv": "L0_attn_b_qkv", "w_out": "L0_attn_w_out", "b_out": "L0_attn_b_out", "wq": "L0_ffn_wq",
        "wk": "L0_ffn_wk", "wv": "L0_ffn_wv", "wp": "L0_ffn_wp", "wo": "L0_ffn_wo", "ln1_g": "L0_ffn_ln1_g",
        "ln1_b": "L0_ffn_ln1_b", "ln2_g": "L0_ffn_ln2_g", "ln2_b": "L0_ffn_ln2_b", "sel_w": "L0_ffn_sel_w",
        "keys": "L0_ffn_keys", "values": "L0_ffn_values", "Wqk": "L1_attn_Wqk", "bqk": "L1_attn_bqk",
        "gamma": "L1_attn_gamma", "beta": "L1_attn_beta", "Wv": "L1_attn_Wv", "bv": "L1_attn_bv",
        "rel_emb": "L1_attn_rel_emb", "ln_w": "L1_ffn_ln_w", "ln_b": "L1_ffn_ln_b",
        "router_w": "L1_ffn_router_w", "gate_w": "L1_ffn_gate_w", "up_w": "L1_ffn_up_w",
        "down_w": "L1_ffn_down_w", "sh_gate": "L1_ffn_sh_gate", "sh_up": "L1_ffn_sh_up",
        "sh_down": "L1_ffn_sh_down"}


def _tables():
    import math

    r = np.arange(P)
    freq = (1.0 / np.float32(10000.0) ** (np.arange(0, P, 2, dtype=np.float32) / np.float32(P))).astype(np.float64)
    ang = freq[:, None] * np.arange(T)[None, :]
    s, c = np.sin(ang), np.cos(ang)
    mask = np.zeros((P, HG), np.float32)
    for h in range(HG):
        mask[:96, h] = (r[:96] % 32) // HD == h
        mask[96 + h, h] = 1.0
    ones = np.zeros((32, T), np.float32)
    ones[:HG] = 1.0
    n = np.maximum(np.arange(T)[None, :] - r[:, None], 0)
    half = MAX_BUCKETS // 2
    large = half + (np.log(np.maximum(n, 1).astype(np.float32) / half) / math.log(MAX_DISTANCE / half)
                    * (MAX_BUCKETS - half)).astype(np.int32)
    bucket = np.where(n < half, n, np.minimum(large, MAX_BUCKETS - 1))
    return {"eye": np.eye(P), "pos": np.concatenate([s, c]), "cos": np.concatenate([c, c]),
            "sin": np.concatenate([s, -s]), "headmask": mask, "ones_rows": ones,
            "iota": np.arange(E0), "tri": r[None, :] >= r[:, None], "bucket": bucket}


def kernel(**inputs):
    import concourse.bacc as _bacc
    from concourse.bass_utils import run_bass_kernel_spmd as _run

    nc = _bacc.Bacc("TRN2", target_bir_lowering=False, num_devices=1)
    arrays = {short: np.ascontiguousarray(inputs[name]) for short, name in _INS.items()}
    arrays.update({name: np.ascontiguousarray(a, dtype=np.float32) for name, a in _tables().items()})
    io = {name: nc.dram_tensor(f"in_{name}", a.shape, F32, kind="ExternalInput").ap() for name, a in arrays.items()}
    out = nc.dram_tensor("out_0", arrays["x"].shape, F32, kind="ExternalOutput").ap()
    build(nc, io, out)
    r = _run(nc, [{f"in_{name}": a for name, a in arrays.items()}], core_ids=[0])
    return r.results[0]["out_0"]
```

```python
from contextlib import ExitStack

import numpy as np
import concourse.bass as bass
from concourse import mybir

ALU = mybir.AluOpType
ACT = mybir.ActivationFunctionType
AX = mybir.AxisListType
F32 = mybir.dt.float32
F32R = mybir.dt.float32r
U32 = mybir.dt.uint32

P = 128
TT = 4
T = P * TT
HD = 8
HG = 4
NG = 4
E0, TOPK = 32, 4
E1 = 8
EPS = 1e-5
STEPS = 44
MAX_BUCKETS, MAX_DISTANCE = 32, 128
ERF_P = 0.3275911
ERF_A = (0.254829592, -0.284496736, 1.421413741, -1.453152027, 1.061405429)


def group_steps(cur):
    steps = []
    for n in range(16):
        def at(*slots):
            return n in slots

        if at(15) and cur + 1 < 2 * NG:
            steps.append(("shift", cur + 1, 0))
        if cur >= 0:
            steps.append(("prob", cur, n))
        if cur >= 1 and at(1):
            steps.append(("pv", cur - 1, 3))
        if cur >= 1 and at(2):
            steps.append(("acc", cur - 1, 0))
        if cur + 2 == NG and at(0):
            steps.append(("proj", 1, 0))
        if cur + 2 < 2 * NG and at(2 if cur >= 0 else 12):
            steps.append(("rep", cur + 2, 0))
        if 0 <= cur + 1 < NG:
            if at(0, 3, 6, 9):
                steps.append(("rot", cur + 1, n // 3))
            if at(2, 5, 8, 11):
                steps.append(("rot_split", cur + 1, n // 3))
            steps += [("max", cur + 1, m) for m in range(16) if 3 + m * 12 // 16 == n]
        elif NG <= cur + 1 < 2 * NG:
            steps += [("max", cur + 1, m) for m in range(16) if m * 14 // 16 == n]
        if cur >= 0 and at(5, 9, 13):
            steps.append(("pv", cur, (n - 5) // 4))
        if cur >= 1 and at(5):
            steps.append(("heads", cur - 1, 0))
        if cur == NG:
            steps += [(what, 0, 0) for what, slot in (("onT", 7), ("out", 9), ("ln2_stats", 10), ("ln2_scale", 12))
                      if at(slot)]
        if cur == NG + 1:
            steps += [(what, 0, k) for what, slot, k in
                      [("x2T", 0, 0), ("sel", 2, 0), ("gT", 14, 0)] +
                      [("top4", (3, 5, 6, 7, 8, 9, 10, 11)[k], k) for k in range(8)] if at(slot)]
        if cur >= NG + 2 and n % 2:
            steps += experts(8 * (cur - NG - 2) + n // 2)
    return steps


def experts(e):
    return [("expert", 0, e)] + ([("val", 0, e - 1)] if e else [])


def end_steps():
    steps = [("pv", 2 * NG - 1, 3)]
    last = {17: [("acc", 2 * NG - 1, 0)], 19: [("heads", 2 * NG - 1, 0)], 22: [("onT", 1, 0)], 24: [("out", 1, 0)]}
    for e in range(16, E0):
        steps += experts(e) + last.get(e, [])
    return steps + [("val", 0, E0 - 1)]


LAYER0 = ([("rep", 0, 0)] + [s for cur in range(-1, 2 * NG) for s in group_steps(cur)] + end_steps())

MISC = []
PAIR = []
RING1, RING2 = [], []
for _what, _g, _n in LAYER0:
    if _what == "proj":
        MISC += [f"v{_g}"]
    if _what in ("shift", "heads", "onT", "out"):
        MISC += [f"{_what}{_g}"]
    if _what in ("x2T", "sel", "gT"):
        MISC += [_what]
    if _what in ("proj", "rep"):
        PAIR.append(f"{_what}{_g}")
    if _what == "rot":
        PAIR.append(f"rot{_g}_{_n}")
    if _what == "max":
        RING1.append(f"max{_g * 16 + _n}")
    if _what == "prob":
        RING2.append(f"prob{_g * 16 + _n}")
    if _what == "expert":
        RING1.append(f"key{_n}")
        RING2.append(f"gate{_n}")
MISC += ["moe", "xn1T", "xfT", "router", "v1l", "wT", "zT", "v0", "fin"]
PAIR += ["moe"] + [f"w{e}" for e in range(E1)] + ["proj0"]
R_SIM = len(RING1)
R_FFN = R_SIM + TT
N1 = R_FFN + 2 * (E1 + 1)
R2_QK = len(RING2)
R2_FFN = R2_QK + 1
N2 = R2_FFN + 2 * (E1 + 1)


def build(nc, io, out):
    rounds = io["x"].shape[0]
    ctx = ExitStack()
    with ctx:
        base = (nc.sbuf_base + 63) // 64 * 64
        cursor = [base]

        def at(name, shape, dt, where):
            return nc.alloc_sbuf_tensor_at(name, shape, dt, offset=where)

        def size(shape):
            return int(np.prod(shape[1:])) * 4

        def sb(name, shape, dt=F32):
            t = at(name, shape, dt, cursor[0])
            cursor[0] += (size(shape) + 31) // 32 * 32
            return t

        def region(nbytes, *layouts):
            start = cursor[0]
            got = []
            for layout in layouts:
                here = start
                for name, shape, dt in layout:
                    got.append(at(name, shape, dt, here))
                    here += (size(shape) + 31) // 32 * 32
                assert here - start <= nbytes, (here - start, nbytes)
            cursor[0] += nbytes
            return got

        ident = sb("ident", [P, P])
        strip = sb("strip", [P, NG, 9, 32], F32R)
        headmask = sb("headmask", [P, HG])
        pick = sb("pick", [64, E0], F32R)
        pick1 = sb("pick1", [16, E1], F32R)
        iota = sb("iota", [P, E0])
        tri = sb("tri", [P, P])
        pos_hi = sb("pos_hi", [P, T], F32R)
        pos_lo = sb("pos_lo", [P, T], F32R)
        cos_t = sb("cos_t", [P, T])
        sin_t = sb("sin_t", [P, T])
        biasl = sb("biasl", [P, T])
        w_att = sb("w_att", [P, 2, 3 * P])
        w_o = sb("w_o", [P, 2, P])
        w_l1 = sb("w_l1", [P, 2, P])
        w_sel = sb("w_sel", [P, E0])
        w_rt = sb("w_rt", [P, E1])
        keys_hi = sb("keys_hi", [P, E0, P], F32R)
        keys_lo = sb("keys_lo", [P, E0, P], F32R)
        vals = sb("vals", [P, E0, P])
        wpu = sb("wpu", [P, 4 * HG, 192], F32R)
        cols = sb("cols", [P, 24])
        rows = sb("rows", [P, 3, P])
        relb = sb("relb", [P, MAX_BUCKETS])
        neghalf = sb("neghalf", [P, TT])
        vext = sb("vext", [P, 2, TT, 4 * HG, 16])
        stat = sb("stat", [P, TT, 6])
        mv = sb("mv", [P, TT, 2])
        var = sb("var", [P, TT])
        rstd = sb("rstd", [P, TT])
        x_in = sb("x_in", [P, TT, P])
        xn = sb("xn", [P, TT, P])
        acc_tm = sb("acc_tm", [P, TT, P])
        hT0 = sb("hT0", [P, T])
        q_hi = sb("q_hi", [P, T], F32R)
        q_lo = sb("q_lo", [P, T], F32R)
        k_hi = sb("k_hi", [P, T], F32R)
        k_lo = sb("k_lo", [P, T], F32R)
        krep = sb("krep", [P, T])
        negmax = sb("negmax", [P, 2, TT, 32])
        rot_a = sb("rot_a", [P, 2, T])
        rot_b = sb("rot_b", [P, 2, T])
        o_sb = sb("o_sb", [P, T])
        on_tm = sb("on_tm", [P, TT, P])
        rden = sb("rden", [P, TT, HG])
        spare = sb("spare", [P, 1])
        pool_spare = sb("pool_spare", [P, 1])
        out_tm = sb("out_tm", [P, TT, P])

        (u_hi, u_lo, src, z2, x2T, x2_hi, x2_lo, gate_bc, hmoe, sg0, eqt, gate, ghl, gT, m8, i8, i8f,
         x1, z1, xn1T, xfT, q1T, k1T, v1, lg, m81, i81, i81f, sc1, w_tm, whl, wT, xe, sg, hm, z_tm, hT1, keys_f) = region(
            33 * 1024,
            [("u_hi", [P, 8, T], F32R), ("u_lo", [P, 8, T], F32R)],
            [("src", [P, TT, P], F32), ("z2", [P, TT, P], F32), ("x2T", [P, T], F32),
             ("x2_hi", [P, T], F32R), ("x2_lo", [P, T], F32R), ("gate_bc", [P, 2, T], F32),
             ("hmoe", [P, 2, T], F32), ("sg0", [P, TT, E0], F32), ("eqt", [P, TT, TOPK, E0], F32),
             ("gate", [P, TT, E0], F32), ("ghl", [P, TT, 2 * E0], F32), ("gT", [64, T], F32R),
             ("m8", [P, TT, 8], F32), ("i8", [P, TT, 8], U32), ("i8f", [P, TT, 8], F32)],
            [("x1", [P, TT, P], F32), ("z1", [P, TT, P], F32), ("xn1T", [P, T], F32),
             ("xfT", [P, T], F32), ("q1T", [P, T], F32), ("k1T", [P, T], F32),
             ("v1", [P, TT, P], F32), ("lg", [P, TT, E1], F32), ("m81", [P, TT, 8], F32),
             ("i81", [P, TT, 8], U32), ("i81f", [P, TT, 8], F32), ("sc1", [P, TT], F32),
             ("w_tm", [P, TT, E1], F32), ("whl", [P, TT, 2 * E1], F32), ("wT", [16, T], F32R),
             ("xe", [P, 2, T], F32), ("sg", [P, 2, T], F32), ("hm", [P, 2, T], F32), ("z_tm", [P, TT, P], F32),
             ("hT1", [P, T], F32)],
            [("keys_f", [P, E0, P], F32)])
        (probs, kmask, qrep, gate_w, up_w, down_w, lz, la, lt, lp, prep_t, prep_e, pm_f, pos_f) = region(
            48 * 1024,
            [("probs", [P, 8, T], F32), ("kmask", [P, 3 * HG, T], F32R), ("qrep", [P, 3, T], F32R)],
            [("gate_w", [P, E1 + 1, 2 * P], F32), ("up_w", [P, E1 + 1, 2 * P], F32),
             ("down_w", [P, E1 + 1, 2, P], F32),
             ("lz", [P, 10 * P], F32), ("la", [P, 10 * P], F32), ("lt", [P, 10 * P], F32),
             ("lp", [P, 10 * P], F32)],
            [("prep_t", [P, T], F32), ("prep_e", [P, T], F32), ("pm_f", [P, P], F32), ("pos_f", [P, T], F32)])
        assert cursor[0] <= nc.sbuf_usable_end, (cursor[0], nc.sbuf_usable_end)

        def bank(name, shape):
            return ctx.enter_context(nc.psum_tensor(name, shape, F32))

        ring1 = bank("ring1", [P, 2, T])
        ring2 = bank("ring2", [P, 2, T])
        acc = bank("acc", [P, T])
        pair = bank("pair", [P, 2, T])
        misc = bank("misc", [P, T])

        def sem(name):
            return ctx.enter_context(nc.semaphore(name))

        w_loaded = sem("w_loaded")
        keys_loaded = sem("keys_loaded")
        act_prep = sem("act_prep")
        dve_prep = sem("dve_prep")
        pe_prep = sem("pe_prep")
        pool_prep = sem("pool_prep")
        dve_step = sem("dve_step")
        x_loaded = sem("x_loaded")
        x_used = sem("x_used")
        ffn_loaded = sem("ffn_loaded")
        out_stored = sem("out_stored")
        round_done = sem("round_done")
        var_ready = sem("var_ready")
        rstd_ready = sem("rstd_ready")
        z_ready = sem("z_ready")
        misc_full = sem("misc_full")
        misc_free = sem("misc_free")
        pair_full = sem("pair_full")
        pair_free = sem("pair_free")
        ring1_full = sem("ring1_full")
        ring1_free = sem("ring1_free")
        ring2_full = sem("ring2_full")
        ring2_free = sem("ring2_free")
        acc_free = sem("acc_free")
        hi_ready = sem("hi_ready")
        mask_ready = sem("mask_ready")
        usum_ready = sem("usum_ready")
        uhi_ready = sem("uhi_ready")
        ulo_ready = sem("ulo_ready")
        pv_done = sem("pv_done")
        x2hi_ready = sem("x2hi_ready")
        x2lo_ready = sem("x2lo_ready")
        gate_ready = sem("gate_ready")
        val_done = sem("val_done")
        top1_ready = sem("top1_ready")
        top1exp_ready = sem("top1exp_ready")
        w_ready = sem("w_ready")
        q1_ready = sem("q1_ready")
        v1_ready = sem("v1_ready")
        labs_ready = sem("labs_ready")
        lsq_ready = sem("lsq_ready")
        lexp_ready = sem("lexp_ready")
        xe_ready = sem("xe_ready")
        lrec_ready = sem("lrec_ready")
        lap_step = sem("lap_step")
        attn_ready = sem("attn_ready")
        down_done = sem("down_done")

        GROUPS = 2 * NG
        ROTS = NG * HG
        LNS = 5
        LAP_STEPS = 2
        FFN_LOADS = 7 * 16
        NM, NP = len(MISC), len(PAIR)
        NA = GROUPS + 1
        N_LOADS = 39

        (C_BQ, C_BK, C_GA, C_BA, C_G1, C_B1, C_G2, C_B2, C_BQK, C_GM0, C_GM1, C_BE0, C_BE1,
         C_LW, C_LB, C_Z) = range(16)

        def col(c):
            return cols[:, c:c + 1]

        def tiles(ap):
            return ap.rearrange("p (t c) -> p t c", t=TT)

        qkT = on_tm[:, :, :].rearrange("p t c -> p (t c)")
        LAP = [0, 4 * P, 7 * P, 9 * P, 10 * P]
        LAP_STD = (0.25 * np.pi) ** 0.5 * 2 ** 0.5
        LAP_MU = 0.5 ** 0.5

        START_MISC, START_PAIR = ["zT", "v0"], ["proj0"]

        def misc_before(it, name):
            return START_MISC.index(name) if it is None else it * NM + len(START_MISC) + MISC.index(name)

        def norms_before(it, n):
            return n if it is None else it * LNS + (n if n >= 2 else n + LNS)

        def pair_before(it, name):
            return START_PAIR.index(name) if it is None else it * NP + len(START_PAIR) + PAIR.index(name)

        START_PROJ = 2 * E1
        START = {1: 2, 3: 3, START_PROJ: 4}
        ERF = (2, 4, 5, 6, 7, 8, 9, 10, 11, 12, 12, 13, 14, 15)

        block = ctx.enter_context(nc.Block())

        @block.sync
        def _(sp):
            n = 0
            with nc.allow_non_contiguous_dma(reason="per-feature columns, once"):
                for c, ap in ((C_BQ, io["b_qkv"][0:P]), (C_BK, io["b_qkv"][P:2 * P]), (C_GA, io["ga"]),
                              (C_BA, io["ba"]), (C_G1, io["ln1_g"]), (C_B1, io["ln1_b"]),
                              (C_G2, io["ln2_g"]), (C_B2, io["ln2_b"]), (C_BQK, io["bqk"]),
                              (C_GM0, io["gamma"][0, :]), (C_GM1, io["gamma"][1, :]),
                              (C_BE0, io["beta"][0, :]), (C_BE1, io["beta"][1, :]),
                              (C_LW, io["ln_w"]), (C_LB, io["ln_b"])):
                    sp.dma_start(col(c), ap.rearrange("(p a) -> p a", a=1)).then_inc(w_loaded, 16)
                    n += 1
            for dst, ap in ((ident[:, :], io["eye"]), (headmask[:, :], io["headmask"]),
                            (iota[:, :], io["iota"].partition_broadcast(P)), (tri[:, :], io["tri"]),
                            (pos_f[:, :], io["pos"]), (cos_t[:, :], io["cos"]), (sin_t[:, :], io["sin"]),
                            (krep[96:P, :], io["ones_rows"]), (biasl[:, :], io["bucket"]),
                            (relb[:, :], io["rel_emb"].rearrange("b a -> (b a)").partition_broadcast(P)),
                            (w_att[:, 0, :], io["w_qkv"]), (w_att[:, 1, 0:P], io["wq"]),
                            (w_att[:, 1, P:2 * P], io["wk"]), (w_att[:, 1, 2 * P:3 * P], io["wv"]),
                            (w_o[:, 0, :], io["w_out"]), (w_o[:, 1, :], io["wo"]),
                            (w_l1[:, 0, :], io["Wqk"]), (w_l1[:, 1, :], io["Wv"]),
                            (w_sel[:, :], io["sel_w"]), (w_rt[:, :], io["router_w"]),
                            (pm_f[:, :], io["wp"]),
                            (rows[:, 0, :], io["b_qkv"][2 * P:3 * P].partition_broadcast(P)),
                            (rows[:, 1, :], io["b_out"].partition_broadcast(P)),
                            (rows[:, 2, :], io["bv"].partition_broadcast(P))):
                sp.dma_start(dst, ap).then_inc(w_loaded, 16)
                n += 1
            assert n == N_LOADS
            sp.dma_start(keys_f[:, :, :], io["keys"].rearrange("e d s -> d e s")).then_inc(keys_loaded, 16)
            sp.dma_start(vals[:, :, :], io["values"].rearrange("e s d -> s e d")).then_inc(keys_loaded, 16)
            sp.dma_start(x_in[:, :, :], io["x"][0].rearrange("(t p) c -> p t c", p=P)).then_inc(x_loaded, 16)

            def one_round(it, following):
                sp.wait_ge(x_used, it + 1)
                sp.dma_start(x_in[:, :, :], io["x"][following].rearrange("(t p) c -> p t c", p=P))\
                    .then_inc(x_loaded, 16)
                sp.wait_ge(pv_done, it * (4 * GROUPS) + 4 * GROUPS)
                sp.dma_start(gate_w[:, 0:E1, :], io["gate_w"].rearrange("e d i -> d e i")).then_inc(ffn_loaded, 16)
                sp.dma_start(gate_w[:, E1, :], io["sh_gate"]).then_inc(ffn_loaded, 16)
                sp.dma_start(up_w[:, 0:E1, :], io["up_w"].rearrange("e d i -> d e i")).then_inc(ffn_loaded, 16)
                sp.dma_start(up_w[:, E1, :], io["sh_up"]).then_inc(ffn_loaded, 16)
                for a in range(2):
                    sp.dma_start(down_w[:, 0:E1, a, :], io["down_w"][:, a * P:(a + 1) * P, :]
                                 .rearrange("e i h -> i e h")).then_inc(ffn_loaded, 16)
                sp.dma_start(down_w[:, E1, :, :],
                             io["sh_down"].rearrange("(a i) h -> i a h", a=2)).then_inc(ffn_loaded, 16)
                sp.wait_ge(misc_free, misc_before(it, "fin") + 1)
                sp.dma_start(out[it].rearrange("(t p) c -> p t c", p=P), out_tm[:, :, :]).then_inc(out_stored, 16)

            with sp.Fori(0, rounds - 1) as it:
                one_round(it, it + 1)
            one_round(rounds - 1, rounds - 1)
            sp.wait_ge(out_stored, rounds * 16 + 16)

        @block.gpsimd
        def _(pool):
            pool.memset(neghalf[:, :], -0.5).then_inc(pool_prep, 1)
            pool.memset(vext[:, :, :, :, :], 0.0).then_inc(pool_prep, 1)
            pool.memset(negmax[:, :, :, :], 0.0).then_inc(pool_prep, 1)
            pool.wait_ge(pool_prep, 2)
            pool.memset(vext[:, :, :, :, HD:HD + 1], 1.0).then_inc(pool_prep, 1)
            pool.memset(out_tm[:, :, :], 0.0).then_inc(out_stored, 16)
            pool.wait_ge(pool_prep, 4)
            pool.wait_ge(w_loaded, N_LOADS * 16)
            pool.drain().then_inc(round_done, 1)

            def power(it, n):
                pool.wait_ge(var_ready, norms_before(it, n) + 1)
                pool.tensor_tensor(rstd[:, :], var[:, :], neghalf[:, :], ALU.pow).then_inc(rstd_ready, 1)

            power(None, 0)
            power(None, 1)
            with pool.Fori(0, rounds) as it:
                pool.wait_ge(round_done, it * 4 + 4)

                for what, g, n in LAYER0:
                    b = g % 2
                    k = g * HG + n
                    if what == "ln2_stats":
                        power(it, 2)
                    elif what == "rep":
                        pool.wait_ge(pair_free, pair_before(it, f"rep{g}") + 1)
                        if g >= 3:
                            pool.wait_ge(ring2_full, it * N2 + RING2.index(f"prob{(g - 2) * 16 - 1}") + 1)
                        pool.tensor_tensor(pool_spare[:, :], neghalf[:, 0:1], neghalf[:, 0:1], ALU.add)
                        for h in range(HG):
                            ins = pool.tensor_scalar(kmask[:, HG * (g % 3) + h, :], krep[:, :], headmask[:, h:h + 1],
                                                     1.0, ALU.mult, ALU.mult)
                        ins.then_inc(mask_ready, 1)
                    elif what == "rot":
                        pool.wait_ge(pair_free, pair_before(it, f"rot{g}_{n}") + 1)
                        pool.tensor_tensor(rot_a[:, k % 2, :], rot_a[:, k % 2, :], rot_b[:, k % 2, :],
                                           ALU.add).then_inc(usum_ready, 1)
                    elif what == "rot_split":
                        pool.wait_ge(uhi_ready, it * ROTS + k + 1)
                        pool.tensor_tensor(u_lo[:, HG * b + n, :], rot_a[:, k % 2, :],
                                           u_hi[:, HG * b + n, :].bitcast(F32), ALU.subtract).then_inc(ulo_ready, 1)
                power(it, 3)
                power(it, 4)

                def expert_input(e):
                    pool.wait_ge(pair_free, pair_before(it, f"w{e}") + 1)
                    x_e = xe[:, (e + 1) % 2, :]
                    pool.tensor_tensor(x_e, xfT[:, :], x_e, ALU.mult).then_inc(xe_ready, 1)

                def settle():
                    pool.tensor_tensor(pool_spare[:, :], neghalf[:, 0:1], neghalf[:, 0:1], ALU.add)

                def lap(n):
                    if n == 0:
                        pool.wait_ge(labs_ready, it + 1)
                        settle()
                        pool.tensor_scalar(lt[:, :], la[:, :], ERF_P, 1.0, ALU.mult, ALU.add).then_inc(lap_step, 1)
                        return
                    pool.wait_ge(lap_step, it * LAP_STEPS + n)
                    if n == 1:
                        pool.wait_ge(lrec_ready, it + 1)
                    settle()
                    pool.tensor_scalar(la[:, :], lt[:, :], ERF_A[4], 1.0, ALU.mult, ALU.mult).then_inc(lap_step, 1)

                power(it, 0)
                power(it, 1)
                expert_input(0)
                lap(0)
                for e in range(1, 5):
                    expert_input(e)
                lap(1)
                for e in range(5, E1):
                    expert_input(e)
                pool.drain().then_inc(round_done, 1)

        @block.scalar
        def _(act):
            act.wait_ge(w_loaded, N_LOADS * 16)
            act.activation(pos_hi[:, :], pos_f[:, :], ACT.Copy).then_inc(act_prep, 1)
            act.wait_ge(pe_prep, 1)
            act.activation(q_hi[:, 0:P], misc[:, 0:P], ACT.Copy).then_inc(act_prep, 1)
            act.wait_ge(keys_loaded, 32)
            act.activation(keys_hi[:, :, :], keys_f[:, :, :], ACT.Copy).then_inc(act_prep, 1)
            act.drain().then_inc(round_done, 1)

            def project(it, a):
                act.wait_ge(pair_full, pair_before(it, f"proj{a}") + 1)
                act.activation(q_hi[:, :], pair[:, 0, :], ACT.Identity, bias=col(C_BQ if a else C_Z))
                act.activation(k_hi[:, :], pair[:, 1, :], ACT.Identity, bias=col(C_BK if a else C_Z))\
                    .then_inc(hi_ready, 1)

            act.wait_ge(round_done, 4)
            project(None, 0)
            with act.Fori(0, rounds) as it:
                act.wait_ge(round_done, it * 4 + 4)

                def misc_filled(name):
                    return misc_before(it, name) + 1

                for what, g, n in LAYER0:
                    b = g % 2
                    if what == "proj":
                        project(it, g)
                    elif what == "rep":
                        act.wait_ge(pair_full, pair_before(it, f"rep{g}") + 1)
                        if g >= 1:
                            act.wait_ge(mask_ready, it * GROUPS + g)
                        act.activation(qrep[0:96, g % 3, :], pair[0:96, 0, :], ACT.Copy)
                        act.activation(krep[0:96, :], pair[0:96, 1, :], ACT.Copy).then_inc(pair_free, 1)
                    elif what == "prob":
                        i = g * 16 + n
                        r = RING2.index(f"prob{i}")
                        act.wait_ge(ring2_full, it * N2 + r + 1)
                        if i >= 8:
                            act.wait_ge(pv_done, it * (4 * GROUPS) + i // 4 - 1)
                        act.activation(probs[:, i % 8, :], ring2[:, r % 2, :], ACT.Exp,
                                       scale=float(HD) ** -0.5).then_inc(ring2_free, 1)
                    elif what == "rot_split":
                        k = g * HG + n
                        act.wait_ge(usum_ready, it * ROTS + k + 1)
                        act.activation(u_hi[:, HG * b + n, :], rot_a[:, k % 2, :], ACT.Copy).then_inc(uhi_ready, 1)
                    elif what == "shift":
                        act.wait_ge(misc_full, misc_filled(f"shift{g}"))
                        act.activation(qrep[96:P, g % 3, :], misc[0:32, :], ACT.Copy).then_inc(misc_free, 1)
                    elif what == "acc":
                        act.wait_ge(pv_done, it * (4 * GROUPS) + 4 * (g + 1))
                        if g >= 1:
                            act.wait_ge(misc_full, misc_filled(f"heads{g - 1}"))
                        act.activation(o_sb[:, :], acc[:, :], ACT.Copy).then_inc(acc_free, 1)
                    elif what == "onT":
                        act.wait_ge(misc_full, misc_filled(f"onT{g}"))
                        if g == 0:
                            act.wait_ge(out_stored, it * 16 + 16)
                        act.activation(tiles(out_tm[:, :, :].rearrange("p t c -> p (t c)")), tiles(misc[:, :]),
                                       ACT.Copy).then_inc(misc_free, 1)

                    elif what == "x2T":
                        act.wait_ge(misc_free, misc_filled("x2T"))
                        act.activation(x2_hi[:, :], x2T[:, :], ACT.Copy).then_inc(x2hi_ready, 1)
                    elif what == "sel":
                        act.wait_ge(misc_full, misc_filled("sel"))
                        act.activation(sg0[:, :, :].rearrange("p t e -> p (t e)"), misc[:, 0:TT * E0], ACT.Exp,
                                       scale=-1.0).then_inc(misc_free, 1)
                    elif what == "gT":
                        act.wait_ge(misc_full, misc_filled("gT"))
                        act.activation(gT[:, :], misc[0:64, :], ACT.Copy).then_inc(misc_free, 1)
                    elif what == "expert":
                        r = RING2.index(f"gate{n}")
                        act.wait_ge(ring2_full, it * N2 + r + 1)
                        if n >= 2:
                            act.wait_ge(ring1_free, it * N1 + RING1.index(f"key{n - 2}") + 1)
                        act.activation(gate_bc[:, n % 2, :], ring2[:, r % 2, :], ACT.Copy).then_inc(ring2_free, 1)
                act.wait_ge(pair_full, pair_before(it, "moe") + 1)
                act.activation(o_sb[:, :], pair[:, 1, :], ACT.Copy).then_inc(pair_free, 1)

                act.wait_ge(misc_full, misc_filled("xn1T"))
                act.activation(xn1T[:, :], misc[:, :], ACT.Copy).then_inc(misc_free, 1)
                act.wait_ge(ring2_full, it * N2 + R2_QK + 1)
                act.activation(qkT, ring2[:, R2_QK % 2, :], ACT.Silu, bias=col(C_BQK)).then_inc(ring2_free, 1)

                def gate_unit(i):
                    act.wait_ge(ring2_full, it * N2 + R2_FFN + i + 1)
                    if i >= 2:
                        act.wait_ge(ring1_free, it * N1 + R_FFN + i - 1)
                    act.activation(sg[:, i % 2, :], ring2[:, (R2_FFN + i) % 2, :], ACT.Silu).then_inc(ring2_free, 1)

                act.wait_ge(top1_ready, it + 1)
                act.activation(sc1[:, :], m81[:, :, 0], ACT.Sigmoid).then_inc(top1exp_ready, 1)
                gate_unit(0)
                gate_unit(1)
                act.wait_ge(misc_free, misc_filled("v1l"))
                act.activation(v1[:, :, :], v1[:, :, :], ACT.Silu).then_inc(v1_ready, 1)
                act.wait_ge(misc_full, misc_filled("wT"))
                act.activation(wT[:, :], misc[0:16, :], ACT.Copy).then_inc(misc_free, 1)
                def weights_bc(e):
                    act.wait_ge(pair_full, pair_before(it, f"w{e}") + 1)
                    if e >= 2:
                        act.wait_ge(ring1_full, it * N1 + R_FFN + 2 * (e - 1) + 2)
                    act.activation(xe[:, (e + 1) % 2, :], pair[:, 0, :], ACT.Copy).then_inc(pair_free, 1)

                weights_bc(0)
                act.wait_ge(ring1_free, it * N1 + R_FFN)
                act.activation(la[:, :], lz[:, :], ACT.Abs).then_inc(labs_ready, 1)
                act.activation(lp[:, :], lz[:, :], ACT.Square).then_inc(lsq_ready, 1)
                for i in range(2, 2 * (E1 + 1)):
                    if i % 2 == 0 and i // 2 < E1:
                        weights_bc(i // 2)
                    gate_unit(i)
                    if i == 5:
                        act.wait_ge(lsq_ready, it + 1)
                        act.activation(lp[:, :], lp[:, :], ACT.Exp, scale=-1.0).then_inc(lexp_ready, 1)
                    if i == START_PROJ:
                        project(it, 0)
                act.wait_ge(down_done, it * (2 * (E1 + 1)) + 2 * (E1 + 1))
                act.activation(o_sb[:, :], acc[:, :], ACT.Copy).then_inc(acc_free, 1)
                act.drain().then_inc(round_done, 1)

        @block.tensor
        def _(pe):
            pe.wait_ge(w_loaded, N_LOADS * 16)
            pe.transpose(misc[:, 0:P], pm_f[:, :], ident[:, :]).then_inc(pe_prep, 1)
            pe.wait_ge(dve_prep, 2)
            for g in range(NG):
                pe.matmul(pair[:, 0, g * P:(g + 1) * P], strip[:, g, 4:8, :], q_hi[:, 0:P], start=True, stop=False)
                ins = pe.matmul(pair[:, 0, g * P:(g + 1) * P], strip[:, g, 5:9, :], q_lo[:, 0:P],
                                start=False, stop=True)
            ins.then_inc(pe_prep, 1)
            pe.drain().then_inc(round_done, 1)

            def misc_turn(it, name):
                if it is not None or START_MISC.index(name):
                    pe.wait_ge(misc_free, misc_before(it, name))

            def transposed(it, src_tm, name):
                misc_turn(it, name)
                for t in range(TT):
                    ins = pe.transpose(misc[:, t * P:(t + 1) * P], src_tm[:, t * P:(t + 1) * P], ident[:, :])
                ins.then_inc(misc_full, 1)

            def flat(ap):
                return ap[:, :, :].rearrange("p t c -> p (t c)")

            def token_major(it, name, lhs, rhs, width):
                misc_turn(it, name)
                for t in range(TT):
                    ins = pe.matmul(misc[:, t * width:(t + 1) * width], lhs[:, t * P:(t + 1) * P], rhs,
                                    start=True, stop=True)
                ins.then_inc(misc_full, 1)

            def project(it, a):
                hT = hT0 if a else hT1
                if it is not None:
                    pe.wait_ge(pair_free, pair_before(it, f"proj{a}"))
                pe.matmul(pair[:, 0, :], w_att[:, 1 - a, 0:P], hT[:, :], start=True, stop=True)
                pe.matmul(pair[:, 1, :], w_att[:, 1 - a, P:2 * P], hT[:, :], start=True, stop=True)\
                    .then_inc(pair_full, 1)
                token_major(it, f"v{a}", hT, w_att[:, 1 - a, 2 * P:3 * P], P)

            def start(it):
                pe.wait_ge(z_ready, 1 if it is None else it * 4 + 5)
                transposed(it, flat(z_tm), "zT")

            def start_project(it):
                pe.wait_ge(misc_free, misc_before(it, "zT") + 1)
                project(it, 0)

            pe.wait_ge(round_done, 4)
            start(None)
            start_project(None)
            with pe.Fori(0, rounds) as it:
                pe.wait_ge(round_done, it * 4 + 4)

                def pair_turn(name):
                    pe.wait_ge(pair_free, pair_before(it, name))

                for what, g, n in LAYER0:
                    b = g % 2
                    q = qrep[:, g % 3, :]
                    rel = g < NG
                    if what == "proj":
                        project(it, g)
                    elif what == "rep":
                        pair_turn(f"rep{g}")
                        gl = g % NG
                        pe.matmul(pair[:, 0, :], strip[:, gl, 0:4, :], q_hi[:, :], start=True, stop=False)
                        pe.matmul(pair[:, 0, :], strip[:, gl, 2:6, :], q_lo[:, :], start=False, stop=True)
                        pe.matmul(pair[:, 1, :], strip[:, gl, 4:8, :], k_hi[:, :], start=True, stop=False)
                        pe.matmul(pair[:, 1, :], strip[:, gl, 5:9, :], k_lo[:, :], start=False, stop=True)\
                            .then_inc(pair_full, 1)
                    elif what == "rot":
                        pair_turn(f"rot{g}_{n}")
                        head = g * HG + n
                        pe.matmul(pair[:, 0, :], wpu[0:96, head, 0:P], q[0:96, :], start=True, stop=True)
                        pe.matmul(pair[:, 1, :], wpu[0:96, head, 64:192], q[0:96, :], start=True, stop=True)\
                            .then_inc(pair_full, 1)
                    elif what == "max":
                        h, t = n // TT, n % TT
                        r = RING1.index(f"max{g * 16 + n}")
                        if n == 0:
                            pe.wait_ge(pair_free, pair_before(it, f"rep{g}") + 1)
                            pe.wait_ge(mask_ready, it * GROUPS + g + 1)
                        if rel and t == 0:
                            pe.wait_ge(uhi_ready, it * ROTS + g * HG + h + 1)
                        if r >= 2:
                            pe.wait_ge(ring1_free, it * N1 + r - 1)
                        ins = pe.matmul(ring1[:, r % 2, :], q[0:96, t * P:(t + 1) * P],
                                        kmask[0:96, HG * (g % 3) + h, :], start=True, stop=not rel)
                        if rel:
                            ins = pe.matmul(ring1[:, r % 2, :], u_hi[:, HG * b + h, t * P:(t + 1) * P],
                                            pos_hi[:, :], start=False, stop=True)
                        ins.then_inc(ring1_full, 1)
                    elif what == "shift":
                        pe.wait_ge(ring1_free, it * N1 + RING1.index(f"max{g * 16 + 15}") + 1)
                        misc_turn(it, f"shift{g}")
                        for t in range(TT):
                            ins = pe.transpose(misc[0:32, t * P:(t + 1) * P], negmax[:, b, t, :], ident[:, :])
                        ins.then_inc(misc_full, 1)
                    elif what == "prob":
                        t, h = n // HG, n % HG
                        r = RING2.index(f"prob{g * 16 + n}")
                        if n == 0:
                            pe.wait_ge(misc_free, misc_before(it, f"shift{g}") + 1)
                            if rel:
                                pe.wait_ge(ulo_ready, it * ROTS + (g + 1) * HG)
                        if r >= 2:
                            pe.wait_ge(ring2_free, it * N2 + r - 1)
                        keys = slice(t * P, (t + 1) * P)
                        ins = pe.matmul(ring2[:, r % 2, :], kmask[:, HG * (g % 3) + h, keys], q,
                                        start=True, stop=not rel)
                        if rel:
                            pe.matmul(ring2[:, r % 2, :], pos_hi[:, keys], u_hi[:, HG * b + h, :],
                                      start=False, stop=False)
                            pe.matmul(ring2[:, r % 2, :], pos_lo[:, keys], u_hi[:, HG * b + h, :],
                                      start=False, stop=False)
                            ins = pe.matmul(ring2[:, r % 2, :], pos_hi[:, keys], u_lo[:, HG * b + h, :],
                                            start=False, stop=True)
                        ins.then_inc(ring2_full, 1)
                    elif what == "pv":
                        pe.wait_ge(ring2_free, it * N2 + RING2.index(f"prob{g * 16 + HG * n + HG - 1}") + 1)
                        if n == 0:
                            pe.wait_ge(misc_free, misc_before(it, "v1") + 1 if g >= NG else it * NM + len(START_MISC))
                            if g >= 1:
                                pe.wait_ge(acc_free, it * NA + g)
                        for h in range(HG):
                            ins = pe.matmul(acc[32 * h:32 * h + 16, :], vext[:, g // NG, n, HG * (g % NG) + h, :],
                                            probs[:, (g * 16 + HG * n + h) % 8, :], start=n == 0, stop=n == TT - 1)
                        ins.then_inc(pv_done, 1)
                    elif what == "heads":
                        pe.wait_ge(acc_free, it * NA + g + 1)
                        transposed(it, o_sb, f"heads{g}")
                    elif what == "onT":
                        transposed(it, flat(on_tm), f"onT{g}")
                    elif what == "out":
                        token_major(it, f"out{g}", flat(out_tm), w_o[:, 1 - g, :], P)
                    elif what == "x2T":
                        pe.wait_ge(z_ready, it * 4 + 2)
                        transposed(it, flat(z2), "x2T")
                    elif what == "sel":
                        token_major(it, "sel", x2T, w_sel[:, :], E0)
                    elif what == "gT":
                        pe.wait_ge(gate_ready, it + 1)
                        misc_turn(it, "gT")
                        for t in range(TT):
                            ins = pe.matmul(misc[0:64, t * P:(t + 1) * P], ghl[:, t, :], ident[:, :],
                                            start=True, stop=True)
                        ins.then_inc(misc_full, 1)
                    elif what == "expert":
                        if n == 0:
                            pe.wait_ge(x2lo_ready, it + 1)
                            pe.wait_ge(misc_free, misc_before(it, "gT") + 1)
                        r = RING2.index(f"gate{n}")
                        pe.wait_ge(ring2_free, it * N2 + r - 1)
                        pe.matmul(ring2[:, r % 2, :], pick[:, n:n + 1].to_broadcast([64, P]), gT[:, :],
                                  start=True, stop=True).then_inc(ring2_full, 1)
                        r = RING1.index(f"key{n}")
                        pe.wait_ge(ring1_free, it * N1 + r - 1)
                        pe.matmul(ring1[:, r % 2, :], keys_hi[:, n, :], x2_hi[:, :], start=True, stop=False)
                        pe.matmul(ring1[:, r % 2, :], keys_hi[:, n, :], x2_lo[:, :], start=False, stop=False)
                        pe.matmul(ring1[:, r % 2, :], keys_lo[:, n, :], x2_hi[:, :], start=False, stop=True)\
                            .then_inc(ring1_full, 1)
                    elif what == "val":
                        pe.wait_ge(ring1_free, it * N1 + RING1.index(f"key{n}") + 1)
                        if n == 0:
                            pair_turn("moe")
                        pe.matmul(pair[:, 1, :], vals[:, n, :], hmoe[:, n % 2, :], start=n == 0, stop=n == E0 - 1)\
                            .then_inc(val_done if n < E0 - 1 else pair_full, 1)

                pe.wait_ge(pair_free, pair_before(it, "moe") + 1)
                transposed(it, o_sb, "moe")

                pe.wait_ge(z_ready, it * 4 + 3)
                transposed(it, flat(xn), "xn1T")
                pe.wait_ge(z_ready, it * 4 + 4)
                transposed(it, flat(z1), "xfT")
                token_major(it, "router", xfT, w_rt[:, :], E1)
                pe.wait_ge(ring2_free, it * N2 + R2_QK - 1)
                pe.matmul(ring2[:, R2_QK % 2, :], w_l1[:, 0, :], xn1T[:, :], start=True, stop=True)\
                    .then_inc(ring2_full, 1)
                token_major(it, "v1l", xn1T, w_l1[:, 1, :], P)

                def gate_up(e, gates, ups):
                    w = e - 1 if e else E1
                    if e and gates:
                        pe.wait_ge(xe_ready, it * E1 + e)
                    src_e = xe[:, e % 2, :] if e else xfT[:, :]
                    for a in range(2):
                        i = 2 * e + a
                        half = slice(a * P, (a + 1) * P)
                        if gates:
                            pe.wait_ge(ring2_free, it * N2 + R2_FFN + i - 1)
                            pe.matmul(ring2[:, (R2_FFN + i) % 2, :], gate_w[:, w, half], src_e,
                                      start=True, stop=True).then_inc(ring2_full, 1)
                        if ups:
                            pe.wait_ge(ring1_free, it * N1 + R_FFN + i - 1)
                            pe.matmul(ring1[:, (R_FFN + i) % 2, :], up_w[:, w, half], src_e,
                                      start=True, stop=True).then_inc(ring1_full, 1)

                pe.wait_ge(ffn_loaded, it * FFN_LOADS + FFN_LOADS)
                gate_up(0, True, False)
                pe.wait_ge(q1_ready, it + 1)
                for jt in range(TT):
                    i = R_SIM + jt
                    pe.wait_ge(ring1_free, it * N1 + i - 1)
                    pe.matmul(ring1[:, i % 2, 0:T - jt * P], k1T[:, jt * P:(jt + 1) * P], q1T[:, jt * P:T],
                              start=True, stop=True).then_inc(ring1_full, 1)
                gate_up(0, False, True)
                pe.wait_ge(w_ready, it + 1)
                misc_turn(it, "wT")
                for t in range(TT):
                    ins = pe.transpose(misc[0:16, t * P:(t + 1) * P], whl[:, t, :], ident[:, :])
                ins.then_inc(misc_full, 1)
                pe.wait_ge(misc_free, misc_before(it, "wT") + 1)

                def weight(e):
                    pair_turn(f"w{e}")
                    pe.matmul(pair[:, 0, :], pick1[:, e:e + 1].to_broadcast([16, P]), wT[:, :],
                              start=True, stop=True).then_inc(pair_full, 1)

                def down(e):
                    for a in range(2):
                        i = 2 * e + a
                        pe.wait_ge(ring1_free, it * N1 + R_FFN + i + 1)
                        if i == 0:
                            pe.wait_ge(acc_free, it * NA + GROUPS)
                        pe.matmul(acc[:, :], down_w[:, e - 1 if e else E1, a, :], hm[:, i % 2, :],
                                  start=i == 0, stop=i == 2 * E1 + 1).then_inc(down_done, 1)

                weight(0)
                for e in range(1, E1 + 1):
                    if e < E1:
                        weight(e)
                    gate_up(e, True, True)
                    down(e - 1)
                    if e == 1:
                        start(it)
                    if e == 8:
                        pe.wait_ge(attn_ready, it + 1)
                        pe.wait_ge(v1_ready, it + 1)
                        for jt in reversed(range(TT)):
                            pe.matmul(acc[:, jt * P:T], v1[:, jt, :], lz[:, LAP[jt]:LAP[jt + 1]],
                                      start=False, stop=False)
                    if 2 * e == START_PROJ:
                        start_project(it)
                down(E1)
                pe.wait_ge(acc_free, it * NA + GROUPS + 1)
                transposed(it, o_sb, "fin")
                pe.drain().then_inc(round_done, 1)

        @block.vector
        def _(dve):
            steps, now = [0], [None]

            def prep(ins):
                steps[0] += 1
                ins.then_inc(dve_step, 1)
                dve.wait_ge(dve_step, steps[0])

            prep(dve.memset(cols[:, C_Z:C_Z + 1], 0.0))
            prep(dve.memset(strip[:, :, :, :].bitcast(F32), 0.0))
            dve.wait_ge(w_loaded, N_LOADS * 16)
            for blk in (0, 1, 4, 6):
                prep(dve.tensor_copy(strip[:, :, blk, :], ident[:, :].rearrange("p (g c) -> p g c", g=NG)))
            prep(dve.tensor_copy(pick[0:32, :], ident[0:32, 0:32]))
            prep(dve.tensor_copy(pick[32:64, :], ident[32:64, 32:64]))
            prep(dve.tensor_tensor(pick1[:, :], ident[0:16, 0:E1], ident[0:16, E1:2 * E1], ALU.add))
            dve.wait_ge(act_prep, 1)
            dve.tensor_tensor(pos_lo[:, :], pos_f[:, :], pos_hi[:, :].bitcast(F32), ALU.subtract)\
                .then_inc(dve_prep, 1)
            dve.wait_ge(act_prep, 2)
            dve.tensor_tensor(q_lo[:, 0:P], misc[:, 0:P], q_hi[:, 0:P].bitcast(F32), ALU.subtract)\
                .then_inc(dve_prep, 1)
            prep(dve.tensor_scalar(prep_t[:, :], biasl[:, :], 0.0, relb[:, 0:1], ALU.is_equal, ALU.mult))
            for n in range(1, MAX_BUCKETS):
                prep(dve.tensor_scalar(prep_e[:, :], biasl[:, :], float(n), relb[:, n:n + 1],
                                       ALU.is_equal, ALU.mult))
                prep(dve.tensor_tensor(prep_t[:, :], prep_t[:, :], prep_e[:, :], ALU.add))
            prep(dve.tensor_scalar(biasl[:, :], prep_t[:, :], float(P ** 0.5 / LAP_STD), float(-LAP_MU / LAP_STD),
                                   ALU.mult, ALU.add))
            dve.wait_ge(pe_prep, 2)
            for g in range(NG):
                for h in range(HG):
                    w = pair[:, 0, g * P:(g + 1) * P]
                    dve.tensor_scalar(wpu[:, g * HG + h, 0:P], w, headmask[:, h:h + 1], None, ALU.mult)
                    ins = dve.tensor_scalar(wpu[:, g * HG + h, P:192], w[:, 0:64], headmask[:, h:h + 1], None, ALU.mult)
            prep(ins)
            prep(dve.memset(acc[:, :], 0.0))
            dve.wait_ge(act_prep, 3)
            dve.tensor_tensor(keys_lo[:, :, :], keys_f[:, :, :], keys_hi[:, :, :].bitcast(F32), ALU.subtract)\
                .then_inc(dve_prep, 1)
            dve.memset(stat[:, :, :], 0.0).then_inc(dve_prep, 1)
            dve.drain().then_inc(round_done, 1)

            def chain(ins):
                steps[0] += 1
                ins.then_inc(dve_step, 1)
                dve.wait_ge(dve_step, steps[0] if now[0] is None else now[0] * STEPS + BEFORE + steps[0])

            def settle():
                dve.memset(spare[:, :], 0.0)

            def misc_filled(name):
                dve.wait_ge(misc_full, misc_before(now[0], name) + 1)

            def norm_stats(src_tm):
                for t in range(TT):
                    ins = dve.bn_stats(stat[:, t, :], src_tm[:, t, :])
                chain(ins)
                settle()
                for t in range(TT):
                    ins = dve.bn_aggr(mv[:, t, :], stat[:, t, :])
                chain(ins)
                dve.tensor_scalar(var[:, :], mv[:, :, 1], EPS, None, ALU.add).then_inc(var_ready, 1)

            def norm_scale(n, src_tm, dst_tm):
                dve.wait_ge(rstd_ready, norms_before(now[0], n) + 1)
                for t in range(TT):
                    ins = dve.tensor_scalar(dst_tm[:, t, :], src_tm[:, t, :], mv[:, t, 0:1], rstd[:, t:t + 1],
                                            ALU.subtract, ALU.mult)
                return ins

            def layer_norm(n, src_tm, dst_tm):
                norm_stats(src_tm)
                return norm_scale(n, src_tm, dst_tm)

            def project(a):
                dve.wait_ge(pair_full, pair_before(now[0], f"proj{a}") + 1)
                dve.wait_ge(hi_ready, 1 if now[0] is None else now[0] * 2 + (2 if a else 3))
                dve.scalar_tensor_tensor(q_lo[:, :], pair[:, 0, :], col(C_BQ if a else C_Z),
                                         q_hi[:, :].bitcast(F32), ALU.add, ALU.subtract)
                dve.scalar_tensor_tensor(k_lo[:, :], pair[:, 1, :], col(C_BK if a else C_Z),
                                         k_hi[:, :].bitcast(F32), ALU.add, ALU.subtract).then_inc(pair_free, 1)
                misc_filled(f"v{a}")
                v = misc[:, :].rearrange("p (t h d) -> p t h d", t=TT, d=HD)
                if not a:
                    ins = dve.tensor_copy(vext[:, 0, :, :, 0:HD], v)
                else:
                    bias = rows[:, 0:1, :].rearrange("p a (h d) -> p a h d", d=HD)
                    ins = dve.tensor_tensor(vext[:, 1, :, :, 0:HD], v, bias.to_broadcast([P, TT, 4 * HG, HD]),
                                            ALU.add)
                ins.then_inc(misc_free, 1)

            def start(n):
                if n == 0:
                    dve.wait_ge(x_loaded, 16 if now[0] is None else now[0] * 16 + 32)
                    norm_stats(x_in)
                elif n == 1:
                    chain(norm_scale(0, x_in, xn))
                    norm_stats(xn)
                elif n == 2:
                    norm_scale(1, xn, z_tm).then_inc(z_ready, 1)
                elif n == 3:
                    misc_filled("zT")
                    dve.tensor_scalar(hT0[:, :], misc[:, :], col(C_GA), col(C_BA), ALU.mult, ALU.add)
                    dve.tensor_scalar(hT1[:, :], misc[:, :], col(C_G1), col(C_B1), ALU.mult, ALU.add)\
                        .then_inc(misc_free, 1)
                else:
                    project(0)

            dve.wait_ge(round_done, 4)
            for n in range(5):
                start(n)
            BEFORE = steps[0]
            steps[0] = 0
            with dve.Fori(0, rounds) as it:
                now[0] = it
                dve.wait_ge(round_done, it * 4 + 4)

                def top4(n):
                    full = [P, TT, TOPK, E0]
                    if n == 0:
                        dve.wait_ge(x2hi_ready, it + 1)
                        dve.tensor_tensor(x2_lo[:, :], x2T[:, :], x2_hi[:, :].bitcast(F32), ALU.subtract)\
                            .then_inc(x2lo_ready, 1)
                    elif n == 1:
                        dve.wait_ge(misc_free, misc_before(it, "sel") + 1)
                        chain(dve.tensor_scalar(sg0[:, :, :], sg0[:, :, :], 1.0, None, ALU.add))
                        chain(dve.reciprocal(sg0[:, :, :], sg0[:, :, :]))
                    elif n == 2:
                        settle()
                        for t in range(TT):
                            ins = dve.max(m8[:, t, :], sg0[:, t, :])
                        chain(ins)
                    elif n == 3:
                        settle()
                        for t in range(TT):
                            ins = dve.max_index(i8[:, t, :], m8[:, t, :], sg0[:, t, :])
                        chain(ins)
                    elif n == 4:
                        chain(dve.tensor_copy(i8f[:, :, :], i8[:, :, :]))
                        chain(dve.tensor_tensor(eqt[:, :, :, :],
                                                iota[:, :].unsqueeze(1).unsqueeze(1).to_broadcast(full),
                                                i8f[:, :, 0:TOPK].unsqueeze(3).to_broadcast(full), ALU.is_equal))
                    elif n == 5:
                        chain(dve.tensor_tensor(eqt[:, :, :, :], eqt[:, :, :, :],
                                                m8[:, :, 0:TOPK].unsqueeze(3).to_broadcast(full), ALU.mult))
                    elif n == 6:
                        chain(dve.tensor_reduce(gate[:, :, :], eqt[:, :, :, :].rearrange("p t k e -> p t e k"),
                                                AX.X, ALU.add))
                    else:
                        chain(dve.tensor_copy(ghl[:, :, 0:E0].bitcast(F32R), gate[:, :, :]))
                        dve.tensor_tensor(ghl[:, :, E0:2 * E0], gate[:, :, :], ghl[:, :, 0:E0], ALU.subtract)\
                            .then_inc(gate_ready, 1)

                dve.scalar_tensor_tensor(acc_tm[:, :, :], xn[:, :, :], 2.0, x_in[:, :, :], ALU.mult, ALU.add)\
                    .then_inc(x_used, 1)
                dve.wait_ge(x_used, it + 1)
                chain(dve.tensor_tensor(acc_tm[:, :, :], acc_tm[:, :, :], rows[:, 1:2, :].to_broadcast([P, TT, P]),
                                        ALU.add))
                for what, g, n in LAYER0:
                    b = g % 2
                    if what == "proj":
                        project(g)
                    elif what == "rot":
                        k = g * HG + n
                        dve.wait_ge(pair_full, pair_before(it, f"rot{g}_{n}") + 1)
                        if k >= 2:
                            dve.wait_ge(ulo_ready, it * ROTS + k - 1)
                        dve.tensor_tensor(rot_a[:, k % 2, :], pair[:, 0, :], cos_t[:, :], ALU.mult)
                        dve.tensor_tensor(rot_b[:, k % 2, :], pair[:, 1, :], sin_t[:, :], ALU.mult)\
                            .then_inc(pair_free, 1)
                    elif what == "max":
                        h, t = n // TT, n % TT
                        r = RING1.index(f"max{g * 16 + n}")
                        dve.wait_ge(ring1_full, it * N1 + r + 1)
                        if n == 0 and g >= 2:
                            misc_filled(f"shift{g - 2}")
                        dve.tensor_reduce(negmax[:, b, t, h:h + 1], ring1[:, r % 2, :], AX.X, ALU.max,
                                          negate=True).then_inc(ring1_free, 1)
                    elif what == "heads":
                        misc_filled(f"heads{g}")
                        o = misc[:, :].rearrange("p (t h d) -> p t h d", t=TT, h=HG)
                        chain(dve.reciprocal(rden[:, :, :], o[:, :, :, HD]))
                        gl = g % NG
                        dst = on_tm[:, :, 32 * gl:32 * gl + 32].rearrange("p t (h d) -> p t h d", h=HG)
                        dve.tensor_tensor(dst, o[:, :, :, 0:HD],
                                          rden[:, :, :].unsqueeze(3).to_broadcast([P, TT, HG, HD]), ALU.mult)\
                            .then_inc(misc_free, 1)
                    elif what == "out":
                        misc_filled(f"out{g}")
                        o = tiles(misc[:, :])
                        if g == 0:
                            chain(dve.tensor_tensor(src[:, :, :], xn[:, :, :], o, ALU.add))
                        dve.tensor_tensor(acc_tm[:, :, :], acc_tm[:, :, :], o, ALU.add).then_inc(misc_free, 1)
                    elif what == "ln2_stats":
                        norm_stats(src)
                    elif what == "ln2_scale":
                        norm_scale(2, src, z2).then_inc(z_ready, 1)
                    elif what == "x2T":
                        misc_filled("x2T")
                        dve.tensor_scalar(x2T[:, :], misc[:, :], col(C_G2), col(C_B2), ALU.mult, ALU.add)\
                            .then_inc(misc_free, 1)
                    elif what == "top4":
                        top4(n)
                    elif what == "expert":
                        r = RING1.index(f"key{n}")
                        dve.wait_ge(ring1_full, it * N1 + r + 1)
                        dve.wait_ge(ring2_free, it * N2 + RING2.index(f"gate{n}") + 1)
                        if n >= 2:
                            dve.wait_ge(val_done, it * (E0 - 1) + n - 1)
                        dve.scalar_tensor_tensor(hmoe[:, n % 2, :], ring1[:, r % 2, :], 0.0, gate_bc[:, n % 2, :],
                                                 ALU.max, ALU.mult).then_inc(ring1_free, 1)
                misc_filled("moe")
                dve.tensor_tensor(x1[:, :, :], acc_tm[:, :, :], tiles(misc[:, :]), ALU.add).then_inc(misc_free, 1)
                dve.wait_ge(misc_free, misc_before(it, "moe") + 1)

                ins = layer_norm(3, x1, xn)
                ins.then_inc(z_ready, 1)
                dve.wait_ge(z_ready, it * 4 + 3)
                chain(dve.tensor_tensor(acc_tm[:, :, :], x1[:, :, :], xn[:, :, :], ALU.add))
                layer_norm(4, xn, z1).then_inc(z_ready, 1)
                misc_filled("xfT")
                dve.tensor_scalar(xfT[:, :], misc[:, :], col(C_LW), col(C_LB), ALU.mult, ALU.add)\
                    .then_inc(misc_free, 1)
                misc_filled("router")
                dve.tensor_copy(lg[:, :, :].rearrange("p t e -> p (t e)"), misc[:, 0:TT * E1]).then_inc(misc_free, 1)
                dve.wait_ge(misc_free, misc_before(it, "router") + 1)
                settle()
                for t in range(TT):
                    ins = dve.max(m81[:, t, :], lg[:, t, :])
                ins.then_inc(top1_ready, 1)
                dve.wait_ge(top1_ready, it + 1)
                settle()
                for t in range(TT):
                    ins = dve.max_index(i81[:, t, :], m81[:, t, :], lg[:, t, :])
                chain(ins)
                chain(dve.tensor_copy(i81f[:, :, :], i81[:, :, :]))
                full = [P, TT, E1]
                chain(dve.tensor_tensor(w_tm[:, :, :], iota[:, 0:E1].unsqueeze(1).to_broadcast(full),
                                        i81f[:, :, 0:1].to_broadcast(full), ALU.is_equal))
                dve.wait_ge(ring2_free, it * N2 + R2_QK + 1)
                dve.tensor_scalar(q1T[:, :], qkT, col(C_GM0), col(C_BE0), ALU.mult, ALU.add)
                dve.tensor_scalar(k1T[:, :], qkT, col(C_GM1), col(C_BE1), ALU.mult, ALU.add).then_inc(q1_ready, 1)
                start(0)
                dve.wait_ge(top1exp_ready, it + 1)
                chain(dve.tensor_tensor(w_tm[:, :, :], w_tm[:, :, :], sc1[:, :].unsqueeze(2).to_broadcast(full),
                                        ALU.mult))
                chain(dve.tensor_copy(whl[:, :, 0:E1].bitcast(F32R), w_tm[:, :, :]))
                dve.tensor_tensor(whl[:, :, E1:2 * E1], w_tm[:, :, :], whl[:, :, 0:E1], ALU.subtract)\
                    .then_inc(w_ready, 1)
                misc_filled("v1l")
                dve.tensor_tensor(v1[:, :, :], tiles(misc[:, :]), rows[:, 2:3, :].to_broadcast([P, TT, P]),
                                  ALU.add).then_inc(misc_free, 1)
                for jt in range(TT):
                    i = R_SIM + jt
                    dve.wait_ge(ring1_full, it * N1 + i + 1)
                    dve.scalar_tensor_tensor(lz[:, LAP[jt]:LAP[jt + 1]], ring1[:, i % 2, 0:T - jt * P],
                                             float(1.0 / (T * LAP_STD)), biasl[:, 0:T - jt * P], ALU.mult, ALU.add)\
                        .then_inc(ring1_free, 1)
                start(1)

                def erf_step(n):
                    if n < 5:
                        if n == 0:
                            dve.wait_ge(lap_step, it * LAP_STEPS + 1)
                        part = slice(n * 256, (n + 1) * 256)
                        ins = dve.reciprocal(lt[:, part], lt[:, part])
                        if n == 4:
                            ins.then_inc(lrec_ready, 1)
                    elif n < 9:
                        if n == 5:
                            dve.wait_ge(lap_step, it * LAP_STEPS + 2)
                        chain(dve.scalar_tensor_tensor(la[:, :], la[:, :], ERF_A[8 - n], lt[:, :], ALU.add, ALU.mult))
                    elif n == 9:
                        dve.wait_ge(lexp_ready, it + 1)
                        chain(dve.tensor_tensor(la[:, :], la[:, :], lp[:, :], ALU.mult))
                    elif n == 10:
                        chain(dve.tensor_scalar(lz[:, :], lz[:, :], 0.0, 0.5, ALU.is_ge, ALU.subtract))
                    elif n == 11:
                        chain(dve.scalar_tensor_tensor(la[:, :], la[:, :], -1.0, lz[:, :], ALU.add, ALU.mult))
                    elif n == 12:
                        chain(dve.tensor_scalar(lz[:, :], la[:, :], -1.0, 0.5, ALU.mult, ALU.add))
                    else:
                        for jt in range(TT):
                            diag = lz[:, LAP[jt]:LAP[jt] + P]
                            ins = dve.tensor_tensor(diag, diag, tri[:, :], ALU.mult)
                        ins.then_inc(attn_ready, 1)

                for e in range(E1 + 1):
                    for a in range(2):
                        i = 2 * e + a
                        dve.wait_ge(ring1_full, it * N1 + R_FFN + i + 1)
                        dve.wait_ge(ring2_free, it * N2 + R2_FFN + i + 1)
                        if i >= 2:
                            dve.wait_ge(down_done, it * (2 * (E1 + 1)) + i - 1)
                        dve.tensor_tensor(hm[:, i % 2, :], sg[:, i % 2, :], ring1[:, (R_FFN + i) % 2, :],
                                          ALU.mult).then_inc(ring1_free, 1)
                        for n in range(len(ERF)):
                            if ERF[n] == i:
                                erf_step(n)
                        if i in START:
                            start(START[i])
                misc_filled("fin")
                dve.tensor_tensor(out_tm[:, :, :], acc_tm[:, :, :], tiles(misc[:, :]), ALU.add).then_inc(misc_free, 1)
                dve.drain().then_inc(round_done, 1)

                assert steps[0] == STEPS, steps[0]


_INS = {"x": "L0_attn_x", "ga": "L0_attn_ln_gamma", "ba": "L0_attn_ln_beta", "w_qkv": "L0_attn_w_qkv",
        "b_qkv": "L0_attn_b_qkv", "w_out": "L0_attn_w_out", "b_out": "L0_attn_b_out", "wq": "L0_ffn_wq",
        "wk": "L0_ffn_wk", "wv": "L0_ffn_wv", "wp": "L0_ffn_wp", "wo": "L0_ffn_wo", "ln1_g": "L0_ffn_ln1_g",
        "ln1_b": "L0_ffn_ln1_b", "ln2_g": "L0_ffn_ln2_g", "ln2_b": "L0_ffn_ln2_b", "sel_w": "L0_ffn_sel_w",
        "keys": "L0_ffn_keys", "values": "L0_ffn_values", "Wqk": "L1_attn_Wqk", "bqk": "L1_attn_bqk",
        "gamma": "L1_attn_gamma", "beta": "L1_attn_beta", "Wv": "L1_attn_Wv", "bv": "L1_attn_bv",
        "rel_emb": "L1_attn_rel_emb", "ln_w": "L1_ffn_ln_w", "ln_b": "L1_ffn_ln_b",
        "router_w": "L1_ffn_router_w", "gate_w": "L1_ffn_gate_w", "up_w": "L1_ffn_up_w",
        "down_w": "L1_ffn_down_w", "sh_gate": "L1_ffn_sh_gate", "sh_up": "L1_ffn_sh_up",
        "sh_down": "L1_ffn_sh_down"}


def _tables():
    import math

    r = np.arange(P)
    freq = (1.0 / np.float32(10000.0) ** (np.arange(0, P, 2, dtype=np.float32) / np.float32(P))).astype(np.float64)
    ang = freq[:, None] * np.arange(T)[None, :]
    s, c = np.sin(ang), np.cos(ang)
    mask = np.zeros((P, HG), np.float32)
    for h in range(HG):
        mask[:96, h] = (r[:96] % 32) // HD == h
        mask[96 + h, h] = 1.0
    ones = np.zeros((32, T), np.float32)
    ones[:HG] = 1.0
    n = np.maximum(np.arange(T)[None, :] - r[:, None], 0)
    half = MAX_BUCKETS // 2
    large = half + (np.log(np.maximum(n, 1).astype(np.float32) / half) / math.log(MAX_DISTANCE / half)
                    * (MAX_BUCKETS - half)).astype(np.int32)
    bucket = np.where(n < half, n, np.minimum(large, MAX_BUCKETS - 1))
    return {"eye": np.eye(P), "pos": np.concatenate([s, c]), "cos": np.concatenate([c, c]),
            "sin": np.concatenate([s, -s]), "headmask": mask, "ones_rows": ones,
            "iota": np.arange(E0), "tri": r[None, :] >= r[:, None], "bucket": bucket}


def kernel(**inputs):
    import concourse.bacc as _bacc
    from concourse.bass_utils import run_bass_kernel_spmd as _run

    nc = _bacc.Bacc("TRN2", target_bir_lowering=False, num_devices=1)
    arrays = {short: np.ascontiguousarray(inputs[name]) for short, name in _INS.items()}
    arrays.update({name: np.ascontiguousarray(a, dtype=np.float32) for name, a in _tables().items()})
    io = {name: nc.dram_tensor(f"in_{name}", a.shape, F32, kind="ExternalInput").ap() for name, a in arrays.items()}
    out = nc.dram_tensor("out_0", arrays["x"].shape, F32, kind="ExternalOutput").ap()
    build(nc, io, out)
    r = _run(nc, [{f"in_{name}": a for name, a in arrays.items()}], core_ids=[0])
    return r.results[0]["out_0"]
```

```python
from contextlib import ExitStack

import numpy as np
import concourse.bass as bass
from concourse import mybir

ALU = mybir.AluOpType
ACT = mybir.ActivationFunctionType
AX = mybir.AxisListType
F32 = mybir.dt.float32
F32R = mybir.dt.float32r
U32 = mybir.dt.uint32

P = 128
TT = 4
T = P * TT
HD = 8
HG = 4
NG = 4
E0, TOPK = 32, 4
E1 = 8
EPS = 1e-5
STEPS = 44
MAX_BUCKETS, MAX_DISTANCE = 32, 128
SHIFTS = 7
ERF_P = 0.3275911
ERF_A = (0.254829592, -0.284496736, 1.421413741, -1.453152027, 1.061405429)


def layer0_steps():
    slots = [[] for _ in range(16 * (2 * NG + 2))]

    def put(slot, what, g=0, n=0):
        slots[slot + 16].append((what, g, n))

    for g in range(2 * NG):
        put(16 * g - 1, "shift", g)
    for g in range(2 * NG):
        for n in range(16):
            put(16 * g + n, "prob", g, n)
    put(SUM, "sum")
    put(PLAIN_PROJ, "proj", 1)
    for g in range(2 * NG):
        if g:
            put(REP[g], "rep", g)
            put(REP[g], "mask", g)
    for g in range(NG):
        for h in range(HG):
            put(16 * (g - 1) + ROT[h], "rot", g, h)
            put(16 * (g - 1) + ROT[h] + 2, "rot_split", g, h)
    for g in range(2 * NG):
        for m in range(16):
            put(MAX[g][0] + m * MAX[g][1] // 16, "max", g, m)
    for g in range(2 * NG):
        for t in range(TT):
            put(16 * g + PV[t], "pv", g, t)
        put(16 * g + PV[3] + 1, "acc", g)
        put(16 * g + HEADS, "heads", g)
    for slot, what, n in GATING:
        put(16 * NG + slot, what, 0, n)
    for e in range(E0):
        put(16 * NG + EXPERT[e], "expert", 0, e)
        if e >= 2:
            put(16 * NG + EXPERT[e], "val", 0, e - 2)
    put(16 * NG + EXPERT[E0 - 1], "val", 0, E0 - 2)
    put(16 * NG + EXPERT[E0 - 1], "val", 0, E0 - 1)
    for n in range(4):
        put(16 * NG + START[n], "start", 0, n)
    put(16 * NG + START[3], "zT")
    put(16 * NG + PLAIN_OUT, "onT", 1)
    put(16 * NG + PLAIN_OUT + 1, "out", 1)
    return [("mask", 0, 0)] + [step for slot in slots for step in slot]


SUM = 8
PLAIN_PROJ = 29
REP = (None, -1, 2, 16, 33, 52, 65, 81)
ROT = (0, 3, 4, 7)
MAX = ((-13, 12), (3, 12), (19, 12), (35, 12), (45, 8), (56, 8), (70, 14), (89, 15))
PV = (5, 10, 13, 17)
HEADS = 20
GATING = ((7, "onT", 0), (9, "out", 0), (11, "ln2_stats", 0), (14, "ln2_scale", 0), (16, "x2T", 0),
          (18, "sel", 0), (30, "gT", 0)) + tuple((s, "top4", k) for k, s in enumerate((19, 21, 22, 23, 24, 25, 27, 29)))
EXPERT = [31 + 2 * e if e < 17 else 64 + (e - 17) // 2 for e in range(E0)]
PLAIN_OUT = 76
START = (64, 66, 68, 69)
LAYER0 = layer0_steps()

MISC = []
PAIR = []
RING1, RING2 = [], []
for _what, _g, _n in LAYER0:
    if _what == "proj":
        MISC += [f"v{_g}"]
    if _what in ("shift", "heads", "onT", "out"):
        MISC += [f"{_what}{_g}"]
    if _what in ("x2T", "sel", "gT", "zT"):
        MISC += [_what]
    if _what in ("proj", "rep"):
        PAIR.append(f"{_what}{_g}")
    if _what == "rot":
        PAIR.append(f"rot{_g}_{_n}")
    if _what == "max":
        RING1.append(f"max{_g * 16 + _n}")
    if _what == "prob":
        RING2.append(f"prob{_g * 16 + _n}")
    if _what == "expert":
        RING1.append(f"key{_n}")
        RING2.append(f"gate{_n}")
MISC += ["moe", "xn1T", "xfT", "router", "v0", "v1l", "wT", "fin"]
PAIR += ["moe", "proj0", "rep0"] + [f"w{e}" for e in range(E1)]
R_SIM = len(RING1)
R_FFN = R_SIM + TT
N1 = R_FFN + 2 * (E1 + 1)
R2_QK = len(RING2)
R2_FFN = R2_QK + 1
N2 = R2_FFN + 2 * (E1 + 1)


def build(nc, io, out):
    rounds = io["x"].shape[0]
    ctx = ExitStack()
    with ctx:
        base = (nc.sbuf_base + 63) // 64 * 64
        cursor = [base]

        def at(name, shape, dt, where):
            return nc.alloc_sbuf_tensor_at(name, shape, dt, offset=where)

        def size(shape):
            return int(np.prod(shape[1:])) * 4

        def sb(name, shape, dt=F32):
            t = at(name, shape, dt, cursor[0])
            cursor[0] += (size(shape) + 31) // 32 * 32
            return t

        def region(nbytes, *layouts):
            start = cursor[0]
            got = []
            for layout in layouts:
                here = start
                for name, shape, dt in layout:
                    got.append(at(name, shape, dt, here))
                    here += (size(shape) + 31) // 32 * 32
                assert here - start <= nbytes, (here - start, nbytes)
            cursor[0] += nbytes
            return got

        ident = sb("ident", [P, P])
        strip = sb("strip", [P, NG, 9, 32], F32R)
        headmask = sb("headmask", [P, HG])
        pick = sb("pick", [64, E0], F32R)
        pick1 = sb("pick1", [16, E1], F32R)
        iota = sb("iota", [P, E0])
        tri = sb("tri", [P, P])
        pos_hi = sb("pos_hi", [P, T], F32R)
        pos_lo = sb("pos_lo", [P, T], F32R)
        cos_t = sb("cos_t", [P, T])
        sin_t = sb("sin_t", [P, T])
        biasl = sb("biasl", [P, T])
        w_att = sb("w_att", [P, 2, 3 * P])
        w_o = sb("w_o", [P, 2, P])
        w_l1 = sb("w_l1", [P, 2, P])
        w_sel = sb("w_sel", [P, E0])
        w_rt = sb("w_rt", [P, E1])
        keys_hi = sb("keys_hi", [P, E0, P], F32R)
        keys_lo = sb("keys_lo", [P, E0, P], F32R)
        vals = sb("vals", [P, E0, P])
        wpu = sb("wpu", [P, 4 * HG, 192], F32R)
        cols = sb("cols", [P, 24])
        rows = sb("rows", [P, 3, P])
        neghalf = sb("neghalf", [P, TT])
        vext = sb("vext", [P, 2, TT, 4 * HG, 16])
        stat = sb("stat", [P, TT, 6])
        mv = sb("mv", [P, TT, 2])
        var = sb("var", [P, TT])
        rstd = sb("rstd", [P, TT])
        x_in = sb("x_in", [P, TT, P])
        xn = sb("xn", [P, TT, P])
        acc_tm = sb("acc_tm", [P, TT, P])
        hT0 = sb("hT0", [P, T])
        qrep0 = sb("qrep0", [P, T], F32R)
        q_hi = sb("q_hi", [P, T], F32R)
        q_lo = sb("q_lo", [P, T], F32R)
        k_hi = sb("k_hi", [P, T], F32R)
        k_lo = sb("k_lo", [P, T], F32R)
        krep = sb("krep", [P, T])
        negmax = sb("negmax", [P, 2, TT, 32])
        rot_a = sb("rot_a", [P, 2, T])
        rot_b = sb("rot_b", [P, 2, T])
        o_sb = sb("o_sb", [P, T])
        on_tm = sb("on_tm", [P, TT, P])
        rden = sb("rden", [P, TT, HG])
        spare = sb("spare", [P, 1])
        pool_spare = sb("pool_spare", [P, 1])
        out_tm = sb("out_tm", [P, TT, P])

        (u_hi, u_lo, src, z2, x2T, x2_hi, x2_lo, gate_bc, hmoe, sg0, eqt, gate, ghl, gT, m8, i8, i8f,
         x1, z1, xn1T, xfT, q1T, k1T, v1, lg, m81, i81, i81f, sc1, w_tm, whl, wT, xe, sg, hm, z_tm, hT1, keys_f) = region(
            33 * 1024,
            [("u_hi", [P, 8, T], F32R), ("u_lo", [P, 8, T], F32R)],
            [("src", [P, TT, P], F32), ("z2", [P, TT, P], F32), ("x2T", [P, T], F32),
             ("x2_hi", [P, T], F32R), ("x2_lo", [P, T], F32R), ("gate_bc", [P, 2, T], F32),
             ("hmoe", [P, 3, T], F32), ("sg0", [P, TT, E0], F32), ("eqt", [P, TT, TOPK, E0], F32),
             ("gate", [P, TT, E0], F32), ("ghl", [P, TT, 2 * E0], F32), ("gT", [64, T], F32R),
             ("m8", [P, TT, 8], F32), ("i8", [P, TT, 8], U32), ("i8f", [P, TT, 8], F32)],
            [("x1", [P, TT, P], F32), ("z1", [P, TT, P], F32), ("xn1T", [P, T], F32),
             ("xfT", [P, T], F32), ("q1T", [P, T], F32), ("k1T", [P, T], F32),
             ("v1", [P, TT, P], F32), ("lg", [P, TT, E1], F32), ("m81", [P, TT, 8], F32),
             ("i81", [P, TT, 8], U32), ("i81f", [P, TT, 8], F32), ("sc1", [P, TT], F32),
             ("w_tm", [P, TT, E1], F32), ("whl", [P, TT, 2 * E1], F32), ("wT", [16, T], F32R),
             ("xe", [P, 2, T], F32), ("sg", [P, 2, T], F32), ("hm", [P, 2, T], F32), ("z_tm", [P, TT, P], F32),
             ("hT1", [P, T], F32)],
            [("keys_f", [P, E0, P], F32)])
        (probs, kmask, qrep12, gate_w, up_w, down_w, lz, la, lt, lp, _, xn1, prep_t, prep_e, pm_f, pos_f,
         onehot, relc, shift, colrows) = region(
            48 * 1024,
            [("probs", [P, 8, T], F32), ("kmask", [P, 3 * HG, T], F32R), ("qrep12", [P, 2, T], F32R)],
            [("gate_w", [P, E1 + 1, 2 * P], F32), ("up_w", [P, E1 + 1, 2 * P], F32),
             ("down_w", [P, E1 + 1, 2, P], F32),
             ("lz", [P, 10 * P], F32), ("la", [P, 10 * P], F32), ("lt", [P, 10 * P], F32),
             ("lp", [P, 10 * P], F32)],
            [("weights_place", [P, (E1 + 1) * 6 * P], F32), ("xn1", [P, TT, P], F32)],
            [("prep_t", [P, T + P], F32), ("prep_e", [P, T + P], F32), ("pm_f", [P, P], F32), ("pos_f", [P, T], F32),
             ("onehot", [MAX_BUCKETS, T + P], F32), ("relc", [MAX_BUCKETS, 1], F32),
             ("shift", [P, 2, SHIFTS], F32), ("colrows", [16, P], F32)])
        assert cursor[0] <= nc.sbuf_usable_end, (cursor[0], nc.sbuf_usable_end)

        def bank(name, shape):
            return ctx.enter_context(nc.psum_tensor(name, shape, F32))

        ring1 = bank("ring1", [P, 2, T])
        ring2 = bank("ring2", [P, 2, T])
        acc = bank("acc", [P, T])
        pair = bank("pair", [P, 2, T])
        misc = bank("misc", [P, T])

        def sem(name):
            return ctx.enter_context(nc.semaphore(name))

        w_loaded = sem("w_loaded")
        keys_loaded = sem("keys_loaded")
        act_prep = sem("act_prep")
        dve_prep = sem("dve_prep")
        pe_prep = sem("pe_prep")
        pool_prep = sem("pool_prep")
        dve_step = sem("dve_step")
        x_loaded = sem("x_loaded")
        x_used = sem("x_used")
        ffn_loaded = sem("ffn_loaded")
        out_stored = sem("out_stored")
        round_done = sem("round_done")
        var_ready = sem("var_ready")
        rstd_ready = sem("rstd_ready")
        z_ready = sem("z_ready")
        misc_full = sem("misc_full")
        misc_free = sem("misc_free")
        pair_full = sem("pair_full")
        pair_free = sem("pair_free")
        ring1_full = sem("ring1_full")
        ring1_free = sem("ring1_free")
        ring2_full = sem("ring2_full")
        ring2_free = sem("ring2_free")
        acc_free = sem("acc_free")
        hi_ready = sem("hi_ready")
        mask_ready = sem("mask_ready")
        usum_ready = sem("usum_ready")
        uhi_ready = sem("uhi_ready")
        ulo_ready = sem("ulo_ready")
        pv_done = sem("pv_done")
        x2hi_ready = sem("x2hi_ready")
        x2lo_ready = sem("x2lo_ready")
        gate_ready = sem("gate_ready")
        val_done = sem("val_done")
        top1_ready = sem("top1_ready")
        top1exp_ready = sem("top1exp_ready")
        w_ready = sem("w_ready")
        q1_ready = sem("q1_ready")
        v1_ready = sem("v1_ready")
        labs_ready = sem("labs_ready")
        lsq_ready = sem("lsq_ready")
        lexp_ready = sem("lexp_ready")
        xe_ready = sem("xe_ready")
        lrec_ready = sem("lrec_ready")
        lap_step = sem("lap_step")
        attn_ready = sem("attn_ready")
        down_done = sem("down_done")

        GROUPS = 2 * NG
        ROTS = NG * HG
        LNS = 5
        LAP_STEPS = 2
        FFN_LOADS = 7 * 16
        NM, NP = len(MISC), len(PAIR)
        NA = GROUPS + 1

        (C_BQ, C_BK, C_GA, C_BA, C_G1, C_B1, C_G2, C_B2, C_BQK, C_GM0, C_GM1, C_BE0, C_BE1,
         C_LW, C_LB, C_Z) = range(16)

        def qrep(g):
            return qrep0 if g % 3 == 0 else qrep12[:, g % 3 - 1, :]

        def col(c):
            return cols[:, c:c + 1]

        def tiles(ap):
            return ap.rearrange("p (t c) -> p t c", t=TT)

        qkT = on_tm[:, :, :].rearrange("p t c -> p (t c)")
        LAP = [0, 4 * P, 7 * P, 9 * P, 10 * P]
        LAP_STD = (0.25 * np.pi) ** 0.5 * 2 ** 0.5
        LAP_MU = 0.5 ** 0.5

        START_MISC, START_PAIR = ["zT", "v0"], ["proj0", "rep0"]

        def misc_before(it, name):
            return START_MISC.index(name) if it is None else it * NM + len(START_MISC) + MISC.index(name)

        def repeated(it, g):
            return pair_before(it, f"rep{g}") + 1 if g else it * NP + len(START_PAIR)

        def norms_before(it, n):
            return n if it is None else it * LNS + 2 + (2, 0, 1, 3, 4).index(n)

        def pair_before(it, name):
            return START_PAIR.index(name) if it is None else it * NP + len(START_PAIR) + PAIR.index(name)

        ERF = (2, 4, 5, 6, 7, 8, 9, 10, 11, 11, 15, 15, 15, 15)

        SP_LOADS = ((pos_f[:, :], io["pos"]), (onehot[:, :], io["onehot"]), (cos_t[:, :], io["cos"]),
                    (krep[96:P, :], io["ones_rows"]), (relc[:, :], io["rel_emb"]),
                    (shift[:, :], io["shift"]),
                    (w_o[:, 0, :], io["w_out"]), (w_o[:, 1, :], io["wo"]),
                    (w_l1[:, 0, :], io["Wqk"]), (w_l1[:, 1, :], io["Wv"]),
                    (w_sel[:, :], io["sel_w"]))
        ACT_LOADS = ((ident[:, :], io["eye"]), (pm_f[:, :], io["wp"]), (headmask[:, :], io["headmask"]),
                     (w_att[:, 0, :], io["w_qkv"]), (w_att[:, 1, 0:P], io["wq"]),
                     (w_att[:, 1, P:2 * P], io["wk"]), (w_att[:, 1, 2 * P:3 * P], io["wv"]),
                     (sin_t[:, :], io["sin"]), (iota[:, :], io["iota"].partition_broadcast(P)),
                     (tri[:, :], io["tri"]), (w_rt[:, :], io["router_w"]),
                     (rows[:, 0, :], io["b_qkv"][2 * P:3 * P].partition_broadcast(P)),
                     (rows[:, 1, :], io["b_out"].partition_broadcast(P)),
                     (rows[:, 2, :], io["bv"].partition_broadcast(P)))
        N_LOADS = C_LB + 1 + len(SP_LOADS) + len(ACT_LOADS)

        block = ctx.enter_context(nc.Block())

        @block.sync
        def _(sp):
            for c, ap in ((C_BQ, io["b_qkv"][0:P]), (C_BK, io["b_qkv"][P:2 * P]), (C_GA, io["ga"]),
                          (C_BA, io["ba"]), (C_G1, io["ln1_g"]), (C_B1, io["ln1_b"]),
                          (C_G2, io["ln2_g"]), (C_B2, io["ln2_b"]), (C_BQK, io["bqk"]),
                          (C_GM0, io["gamma"][0, :]), (C_GM1, io["gamma"][1, :]),
                          (C_BE0, io["beta"][0, :]), (C_BE1, io["beta"][1, :]),
                          (C_LW, io["ln_w"]), (C_LB, io["ln_b"])):
                sp.dma_start(colrows[c:c + 1, :], ap.rearrange("(a p) -> a p", a=1)).then_inc(w_loaded, 16)
            sp.dma_start(x_in[:, :, :], io["x"][0].rearrange("(t p) c -> p t c", p=P)).then_inc(x_loaded, 16)
            for dst, ap in SP_LOADS:
                sp.dma_start(dst, ap).then_inc(w_loaded, 16)
            sp.dma_start(keys_f[:, :, :], io["keys"].rearrange("e d s -> d e s")).then_inc(keys_loaded, 16)
            sp.dma_start(vals[:, :, :], io["values"].rearrange("e s d -> s e d")).then_inc(keys_loaded, 16)

            def one_round(it, following):
                sp.wait_ge(x_used, it + 1)
                sp.dma_start(x_in[:, :, :], io["x"][following].rearrange("(t p) c -> p t c", p=P))\
                    .then_inc(x_loaded, 16)
                sp.wait_ge(pv_done, it * (4 * GROUPS) + 4 * GROUPS)
                sp.dma_start(gate_w[:, 0:E1, :], io["gate_w"].rearrange("e d i -> d e i")).then_inc(ffn_loaded, 16)
                sp.dma_start(gate_w[:, E1, :], io["sh_gate"]).then_inc(ffn_loaded, 16)
                sp.dma_start(up_w[:, 0:E1, :], io["up_w"].rearrange("e d i -> d e i")).then_inc(ffn_loaded, 16)
                sp.dma_start(up_w[:, E1, :], io["sh_up"]).then_inc(ffn_loaded, 16)
                for a in range(2):
                    sp.dma_start(down_w[:, 0:E1, a, :], io["down_w"][:, a * P:(a + 1) * P, :]
                                 .rearrange("e i h -> i e h")).then_inc(ffn_loaded, 16)
                sp.dma_start(down_w[:, E1, :, :],
                             io["sh_down"].rearrange("(a i) h -> i a h", a=2)).then_inc(ffn_loaded, 16)
                sp.wait_ge(misc_free, misc_before(it, "fin") + 1)
                sp.dma_start(out[it].rearrange("(t p) c -> p t c", p=P), out_tm[:, :, :]).then_inc(out_stored, 16)

            with sp.Fori(0, rounds - 1) as it:
                one_round(it, it + 1)
            one_round(rounds - 1, rounds - 1)
            sp.wait_ge(out_stored, rounds * 16 + 16)

        @block.gpsimd
        def _(pool):
            pool.memset(neghalf[:, :], -0.5).then_inc(pool_prep, 1)
            pool.memset(vext[:, :, :, :, :], 0.0).then_inc(pool_prep, 1)
            pool.memset(negmax[:, :, :, :], 0.0).then_inc(pool_prep, 1)
            pool.wait_ge(pool_prep, 2)
            pool.memset(vext[:, :, :, :, HD:HD + 1], 1.0).then_inc(pool_prep, 1)

            def power(it, n):
                pool.wait_ge(var_ready, norms_before(it, n) + 1)
                pool.tensor_tensor(rstd[:, :], var[:, :], neghalf[:, :], ALU.pow).then_inc(rstd_ready, 1)

            power(None, 0)
            power(None, 1)
            pool.memset(out_tm[:, :, :], 0.0).then_inc(out_stored, 16)
            pool.wait_ge(pool_prep, 4)
            pool.wait_ge(act_prep, 3)
            pool.tensor_tensor(keys_lo[:, :, :], keys_f[:, :, :], keys_hi[:, :, :].bitcast(F32), ALU.subtract)
            pool.wait_ge(w_loaded, N_LOADS * 16)
            pool.drain().then_inc(round_done, 1)

            with pool.Fori(0, rounds) as it:
                pool.wait_ge(round_done, it * 4 + 4)

                for what, g, n in LAYER0:
                    b = g % 2
                    k = g * HG + n
                    if what == "ln2_stats":
                        power(it, 2)
                    elif what == "start" and n < 2:
                        power(it, n)
                    elif what == "mask":
                        pool.wait_ge(pair_free, repeated(it, g))
                        if g >= 3:
                            pool.wait_ge(ring2_full, it * N2 + RING2.index(f"prob{(g - 2) * 16 - 1}") + 1)
                        pool.tensor_tensor(pool_spare[:, :], neghalf[:, 0:1], neghalf[:, 0:1], ALU.add)
                        for h in range(HG):
                            ins = pool.tensor_scalar(kmask[:, HG * (g % 3) + h, :], krep[:, :], headmask[:, h:h + 1],
                                                     1.0, ALU.mult, ALU.mult)
                        ins.then_inc(mask_ready, 1)
                    elif what == "rot":
                        pool.wait_ge(pair_free, pair_before(it, f"rot{g}_{n}") + 1)
                        pool.tensor_tensor(rot_a[:, k % 2, :], rot_a[:, k % 2, :], rot_b[:, k % 2, :],
                                           ALU.add).then_inc(usum_ready, 1)
                    elif what == "rot_split":
                        pool.wait_ge(uhi_ready, it * ROTS + k + 1)
                        pool.tensor_tensor(u_lo[:, HG * b + n, :], rot_a[:, k % 2, :],
                                           u_hi[:, HG * b + n, :].bitcast(F32), ALU.subtract).then_inc(ulo_ready, 1)
                power(it, 3)
                power(it, 4)

                def expert_input(e):
                    pool.wait_ge(pair_free, pair_before(it, f"w{e}") + 1)
                    x_e = xe[:, (e + 1) % 2, :]
                    pool.tensor_tensor(x_e, xfT[:, :], x_e, ALU.mult).then_inc(xe_ready, 1)

                def settle():
                    pool.tensor_tensor(pool_spare[:, :], neghalf[:, 0:1], neghalf[:, 0:1], ALU.add)

                def lap(n):
                    if n == 0:
                        pool.wait_ge(labs_ready, it + 1)
                        settle()
                        pool.tensor_scalar(lt[:, :], la[:, :], ERF_P, 1.0, ALU.mult, ALU.add).then_inc(lap_step, 1)
                        return
                    pool.wait_ge(lap_step, it * LAP_STEPS + n)
                    if n == 1:
                        pool.wait_ge(lrec_ready, it + 1)
                    settle()
                    pool.tensor_scalar(la[:, :], lt[:, :], ERF_A[4], 1.0, ALU.mult, ALU.mult).then_inc(lap_step, 1)

                expert_input(0)
                lap(0)
                for e in range(1, 5):
                    expert_input(e)
                lap(1)
                for e in range(5, E1):
                    expert_input(e)
                pool.drain().then_inc(round_done, 1)

        @block.scalar
        def _(act):
            for dst, ap in ACT_LOADS:
                act.dma_start(dst, ap).then_inc(w_loaded, 16)
            act.wait_ge(w_loaded, N_LOADS * 16)
            act.activation(pos_hi[:, :], pos_f[:, :], ACT.Copy).then_inc(act_prep, 1)
            act.wait_ge(pe_prep, 1)
            act.activation(q_hi[:, 0:P], misc[:, 0:P], ACT.Copy).then_inc(act_prep, 1)
            act.wait_ge(keys_loaded, 32)
            act.activation(keys_hi[:, :, :], keys_f[:, :, :], ACT.Copy).then_inc(act_prep, 1)
            act.drain().then_inc(round_done, 1)

            def project(it, a):
                act.wait_ge(pair_full, pair_before(it, f"proj{a}") + 1)
                act.activation(q_hi[:, :], pair[:, 0, :], ACT.Identity, bias=col(C_BQ if a else C_Z))
                act.activation(k_hi[:, :], pair[:, 1, :], ACT.Identity, bias=col(C_BK if a else C_Z))\
                    .then_inc(hi_ready, 1)

            def repeat(it, g):
                act.wait_ge(pair_full, pair_before(it, f"rep{g}") + 1)
                if it is not None:
                    act.wait_ge(mask_ready, it * GROUPS + (g or GROUPS))
                act.activation(qrep(g)[0:96, :], pair[0:96, 0, :], ACT.Copy)
                act.activation(krep[0:96, :], pair[0:96, 1, :], ACT.Copy).then_inc(pair_free, 1)

            act.wait_ge(round_done, 4)
            project(None, 0)
            repeat(None, 0)
            with act.Fori(0, rounds) as it:
                act.wait_ge(round_done, it * 4 + 4)

                def misc_filled(name):
                    return misc_before(it, name) + 1

                for what, g, n in LAYER0:
                    b = g % 2
                    if what == "proj":
                        project(it, g)
                    elif what == "rep":
                        repeat(it, g)
                    elif what == "prob":
                        i = g * 16 + n
                        r = RING2.index(f"prob{i}")
                        act.wait_ge(ring2_full, it * N2 + r + 1)
                        if i >= 8:
                            act.wait_ge(pv_done, it * (4 * GROUPS) + i // 4 - 1)
                        act.activation(probs[:, i % 8, :], ring2[:, r % 2, :], ACT.Exp,
                                       scale=float(HD) ** -0.5).then_inc(ring2_free, 1)
                    elif what == "rot_split":
                        k = g * HG + n
                        act.wait_ge(usum_ready, it * ROTS + k + 1)
                        act.activation(u_hi[:, HG * b + n, :], rot_a[:, k % 2, :], ACT.Copy).then_inc(uhi_ready, 1)
                    elif what == "shift":
                        act.wait_ge(misc_full, misc_filled(f"shift{g}"))
                        act.activation(qrep(g)[96:P, :], misc[0:32, :], ACT.Copy).then_inc(misc_free, 1)
                    elif what == "acc":
                        act.wait_ge(pv_done, it * (4 * GROUPS) + 4 * (g + 1))
                        if g >= 1:
                            act.wait_ge(misc_full, misc_filled(f"heads{g - 1}"))
                        act.activation(o_sb[:, :], acc[:, :], ACT.Copy).then_inc(acc_free, 1)
                    elif what == "onT":
                        act.wait_ge(misc_full, misc_filled(f"onT{g}"))
                        if g == 0:
                            act.wait_ge(out_stored, it * 16 + 16)
                        act.activation(tiles(out_tm[:, :, :].rearrange("p t c -> p (t c)")), tiles(misc[:, :]),
                                       ACT.Copy).then_inc(misc_free, 1)

                    elif what == "x2T":
                        act.wait_ge(misc_free, misc_filled("x2T"))
                        act.activation(x2_hi[:, :], x2T[:, :], ACT.Copy).then_inc(x2hi_ready, 1)
                    elif what == "sel":
                        act.wait_ge(misc_full, misc_filled("sel"))
                        act.activation(sg0[:, :, :].rearrange("p t e -> p (t e)"), misc[:, 0:TT * E0], ACT.Exp,
                                       scale=-1.0).then_inc(misc_free, 1)
                    elif what == "gT":
                        act.wait_ge(misc_full, misc_filled("gT"))
                        act.activation(gT[:, :], misc[0:64, :], ACT.Copy).then_inc(misc_free, 1)
                    elif what == "expert":
                        r = RING2.index(f"gate{n}")
                        act.wait_ge(ring2_full, it * N2 + r + 1)
                        if n >= 2:
                            act.wait_ge(ring1_free, it * N1 + RING1.index(f"key{n - 2}") + 1)
                        act.activation(gate_bc[:, n % 2, :], ring2[:, r % 2, :], ACT.Copy).then_inc(ring2_free, 1)
                act.wait_ge(pair_full, pair_before(it, "moe") + 1)
                act.activation(o_sb[:, :], pair[:, 1, :], ACT.Copy).then_inc(pair_free, 1)
                project(it, 0)

                act.wait_ge(misc_full, misc_filled("xn1T"))
                act.activation(xn1T[:, :], misc[:, :], ACT.Copy).then_inc(misc_free, 1)
                act.wait_ge(ring2_full, it * N2 + R2_QK + 1)
                act.activation(qkT, ring2[:, R2_QK % 2, :], ACT.Silu, bias=col(C_BQK)).then_inc(ring2_free, 1)

                def gate_unit(i):
                    act.wait_ge(ring2_full, it * N2 + R2_FFN + i + 1)
                    if i >= 2:
                        act.wait_ge(ring1_free, it * N1 + R_FFN + i - 1)
                    act.activation(sg[:, i % 2, :], ring2[:, (R2_FFN + i) % 2, :], ACT.Silu).then_inc(ring2_free, 1)

                act.wait_ge(top1_ready, it + 1)
                act.activation(sc1[:, :], m81[:, :, 0], ACT.Sigmoid).then_inc(top1exp_ready, 1)
                gate_unit(0)
                gate_unit(1)
                act.wait_ge(misc_free, misc_filled("v1l"))
                act.activation(v1[:, :, :], v1[:, :, :], ACT.Silu).then_inc(v1_ready, 1)
                repeat(it, 0)
                act.wait_ge(misc_full, misc_filled("wT"))
                act.activation(wT[:, :], misc[0:16, :], ACT.Copy).then_inc(misc_free, 1)
                def weights_bc(e):
                    act.wait_ge(pair_full, pair_before(it, f"w{e}") + 1)
                    if e >= 2:
                        act.wait_ge(ring1_full, it * N1 + R_FFN + 2 * (e - 1) + 2)
                    act.activation(xe[:, (e + 1) % 2, :], pair[:, 0, :], ACT.Copy).then_inc(pair_free, 1)

                weights_bc(0)
                act.wait_ge(ring1_free, it * N1 + R_FFN)
                act.activation(la[:, :], lz[:, :], ACT.Abs).then_inc(labs_ready, 1)
                act.activation(lp[:, :], lz[:, :], ACT.Square).then_inc(lsq_ready, 1)
                for i in range(2, 2 * (E1 + 1)):
                    if i % 2 == 0 and i // 2 < E1:
                        weights_bc(i // 2)
                    gate_unit(i)
                    if i == 5:
                        act.wait_ge(lsq_ready, it + 1)
                        act.activation(lp[:, :], lp[:, :], ACT.Exp, scale=-1.0).then_inc(lexp_ready, 1)
                act.wait_ge(down_done, it * (2 * (E1 + 1)) + 2 * (E1 + 1))
                act.activation(o_sb[:, :], acc[:, :], ACT.Copy).then_inc(acc_free, 1)
                act.drain().then_inc(round_done, 1)

        @block.tensor
        def _(pe):
            pe.wait_ge(w_loaded, N_LOADS * 16)
            pe.transpose(misc[:, 0:P], pm_f[:, :], ident[:, :]).then_inc(pe_prep, 1)
            pe.transpose(ring2[:, 0, 0:C_LB + 1], colrows[0:C_LB + 1, :], ident[0:C_LB + 1, 0:C_LB + 1])
            emb = relc[:, 0:1].to_broadcast([MAX_BUCKETS, P])
            pe.matmul(ring1[:, 0, :], emb, onehot[:, 0:T], start=True, stop=True)
            pe.matmul(ring1[:, 1, 0:P], emb, onehot[:, T:T + P], start=True, stop=True).then_inc(pe_prep, 1)
            pe.wait_ge(dve_prep, 2)
            for g in range(NG):
                pe.matmul(pair[:, 0, g * P:(g + 1) * P], strip[:, g, 4:8, :], q_hi[:, 0:P], start=True, stop=False)
                ins = pe.matmul(pair[:, 0, g * P:(g + 1) * P], strip[:, g, 5:9, :], q_lo[:, 0:P],
                                start=False, stop=True)
            ins.then_inc(pe_prep, 1)
            pe.drain().then_inc(round_done, 1)

            def misc_turn(it, name):
                if it is not None or START_MISC.index(name):
                    pe.wait_ge(misc_free, misc_before(it, name))

            def transposed(it, src_tm, name, norm=None):
                misc_turn(it, name)
                for t in range(TT):
                    if norm is not None:
                        pe.wait_ge(z_ready, norm * TT + t + 1 if it is None else it * 4 * TT + norm * TT + t + 1)
                    ins = pe.transpose(misc[:, t * P:(t + 1) * P], src_tm[:, t * P:(t + 1) * P], ident[:, :])
                ins.then_inc(misc_full, 1)

            def flat(ap):
                return ap[:, :, :].rearrange("p t c -> p (t c)")

            def token_major(it, name, lhs, rhs, width):
                misc_turn(it, name)
                for t in range(TT):
                    ins = pe.matmul(misc[:, t * width:(t + 1) * width], lhs[:, t * P:(t + 1) * P], rhs,
                                    start=True, stop=True)
                ins.then_inc(misc_full, 1)

            def project(it, a):
                hT = hT0 if a else hT1
                if it is not None:
                    pe.wait_ge(pair_free, pair_before(it, f"proj{a}"))
                pe.matmul(pair[:, 0, :], w_att[:, 1 - a, 0:P], hT[:, :], start=True, stop=True)
                pe.matmul(pair[:, 1, :], w_att[:, 1 - a, P:2 * P], hT[:, :], start=True, stop=True)\
                    .then_inc(pair_full, 1)

            def project_values(it, a):
                token_major(it, f"v{a}", hT0 if a else hT1, w_att[:, 1 - a, 2 * P:3 * P], P)

            def repeat(it, g):
                pe.wait_ge(pair_free, pair_before(it, f"rep{g}"))
                gl = g % NG
                pe.matmul(pair[:, 0, :], strip[:, gl, 0:4, :], q_hi[:, :], start=True, stop=False)
                pe.matmul(pair[:, 0, :], strip[:, gl, 2:6, :], q_lo[:, :], start=False, stop=True)
                pe.matmul(pair[:, 1, :], strip[:, gl, 4:8, :], k_hi[:, :], start=True, stop=False)
                pe.matmul(pair[:, 1, :], strip[:, gl, 5:9, :], k_lo[:, :], start=False, stop=True)\
                    .then_inc(pair_full, 1)

            pe.wait_ge(round_done, 4)
            transposed(None, flat(z_tm), "zT", 0)
            pe.wait_ge(misc_free, misc_before(None, "zT") + 1)
            project(None, 0)
            project_values(None, 0)
            repeat(None, 0)
            with pe.Fori(0, rounds) as it:
                pe.wait_ge(round_done, it * 4 + 4)

                def pair_turn(name):
                    pe.wait_ge(pair_free, pair_before(it, name))

                for what, g, n in LAYER0:
                    b = g % 2
                    q = qrep(g)[:, :]
                    rel = g < NG
                    if what == "proj":
                        project(it, g)
                        project_values(it, g)
                    elif what == "rep":
                        repeat(it, g)
                    elif what == "rot":
                        pair_turn(f"rot{g}_{n}")
                        head = g * HG + n
                        pe.matmul(pair[:, 0, :], wpu[0:96, head, 0:P], q[0:96, :], start=True, stop=True)
                        pe.matmul(pair[:, 1, :], wpu[0:96, head, 64:192], q[0:96, :], start=True, stop=True)\
                            .then_inc(pair_full, 1)
                    elif what == "max":
                        h, t = n // TT, n % TT
                        r = RING1.index(f"max{g * 16 + n}")
                        if n == 0:
                            pe.wait_ge(pair_free, repeated(it, g))
                            pe.wait_ge(mask_ready, it * GROUPS + g + 1)
                        if rel and t == 0:
                            pe.wait_ge(uhi_ready, it * ROTS + g * HG + h + 1)
                        if r >= 2:
                            pe.wait_ge(ring1_free, it * N1 + r - 1)
                        ins = pe.matmul(ring1[:, r % 2, :], q[0:96, t * P:(t + 1) * P],
                                        kmask[0:96, HG * (g % 3) + h, :], start=True, stop=not rel)
                        if rel:
                            ins = pe.matmul(ring1[:, r % 2, :], u_hi[:, HG * b + h, t * P:(t + 1) * P],
                                            pos_hi[:, :], start=False, stop=True)
                        ins.then_inc(ring1_full, 1)
                    elif what == "shift":
                        pe.wait_ge(ring1_free, it * N1 + RING1.index(f"max{g * 16 + 15}") + 1)
                        misc_turn(it, f"shift{g}")
                        for t in range(TT):
                            ins = pe.transpose(misc[0:32, t * P:(t + 1) * P], negmax[:, b, t, :], ident[:, :])
                        ins.then_inc(misc_full, 1)
                    elif what == "prob":
                        t, h = n // HG, n % HG
                        r = RING2.index(f"prob{g * 16 + n}")
                        if n == 0:
                            pe.wait_ge(misc_free, misc_before(it, f"shift{g}") + 1)
                            if rel:
                                pe.wait_ge(ulo_ready, it * ROTS + (g + 1) * HG)
                        if r >= 2:
                            pe.wait_ge(ring2_free, it * N2 + r - 1)
                        keys = slice(t * P, (t + 1) * P)
                        ins = pe.matmul(ring2[:, r % 2, :], kmask[:, HG * (g % 3) + h, keys], q,
                                        start=True, stop=not rel)
                        if rel:
                            pe.matmul(ring2[:, r % 2, :], pos_hi[:, keys], u_hi[:, HG * b + h, :],
                                      start=False, stop=False)
                            pe.matmul(ring2[:, r % 2, :], pos_lo[:, keys], u_hi[:, HG * b + h, :],
                                      start=False, stop=False)
                            ins = pe.matmul(ring2[:, r % 2, :], pos_hi[:, keys], u_lo[:, HG * b + h, :],
                                            start=False, stop=True)
                        ins.then_inc(ring2_full, 1)
                    elif what == "pv":
                        pe.wait_ge(ring2_free, it * N2 + RING2.index(f"prob{g * 16 + HG * n + HG - 1}") + 1)
                        if n == 0:
                            pe.wait_ge(misc_free, misc_before(it, "v1") + 1 if g >= NG else it * NM + len(START_MISC))
                            if g >= 1:
                                pe.wait_ge(acc_free, it * NA + g)
                        for h in range(HG):
                            ins = pe.matmul(acc[32 * h:32 * h + 16, :], vext[:, g // NG, n, HG * (g % NG) + h, :],
                                            probs[:, (g * 16 + HG * n + h) % 8, :], start=n == 0, stop=n == TT - 1)
                        ins.then_inc(pv_done, 1)
                    elif what == "heads":
                        pe.wait_ge(acc_free, it * NA + g + 1)
                        transposed(it, o_sb, f"heads{g}")
                    elif what == "onT":
                        transposed(it, flat(on_tm), f"onT{g}")
                    elif what == "out":
                        token_major(it, f"out{g}", flat(out_tm), w_o[:, 1 - g, :], P)
                    elif what == "x2T":
                        transposed(it, flat(z2), "x2T", 1)
                    elif what == "zT":
                        transposed(it, flat(z_tm), "zT", 2)
                    elif what == "sel":
                        token_major(it, "sel", x2T, w_sel[:, :], E0)
                    elif what == "gT":
                        pe.wait_ge(gate_ready, it + 1)
                        misc_turn(it, "gT")
                        for t in range(TT):
                            ins = pe.matmul(misc[0:64, t * P:(t + 1) * P], ghl[:, t, :], ident[:, :],
                                            start=True, stop=True)
                        ins.then_inc(misc_full, 1)
                    elif what == "expert":
                        if n == 0:
                            pe.wait_ge(x2lo_ready, it + 1)
                            pe.wait_ge(misc_free, misc_before(it, "gT") + 1)
                        r = RING2.index(f"gate{n}")
                        pe.wait_ge(ring2_free, it * N2 + r - 1)
                        pe.matmul(ring2[:, r % 2, :], pick[:, n:n + 1].to_broadcast([64, P]), gT[:, :],
                                  start=True, stop=True).then_inc(ring2_full, 1)
                        r = RING1.index(f"key{n}")
                        pe.wait_ge(ring1_free, it * N1 + r - 1)
                        pe.matmul(ring1[:, r % 2, :], keys_hi[:, n, :], x2_hi[:, :], start=True, stop=False)
                        pe.matmul(ring1[:, r % 2, :], keys_hi[:, n, :], x2_lo[:, :], start=False, stop=False)
                        pe.matmul(ring1[:, r % 2, :], keys_lo[:, n, :], x2_hi[:, :], start=False, stop=True)\
                            .then_inc(ring1_full, 1)
                    elif what == "val":
                        pe.wait_ge(ring1_free, it * N1 + RING1.index(f"key{n}") + 1)
                        if n == 0:
                            pair_turn("moe")
                        pe.matmul(pair[:, 1, :], vals[:, n, :], hmoe[:, n % 3, :], start=n == 0, stop=n == E0 - 1)\
                            .then_inc(val_done if n < E0 - 1 else pair_full, 1)

                pe.wait_ge(pair_free, pair_before(it, "moe") + 1)
                transposed(it, o_sb, "moe")

                pe.wait_ge(misc_free, misc_before(it, "zT") + 1)
                project(it, 0)
                transposed(it, flat(xn1), "xn1T", 3)
                pe.wait_ge(misc_free, misc_before(it, "xn1T") + 1)
                pe.wait_ge(ring2_free, it * N2 + R2_QK - 1)
                pe.matmul(ring2[:, R2_QK % 2, :], w_l1[:, 0, :], xn1T[:, :], start=True, stop=True)\
                    .then_inc(ring2_full, 1)
                transposed(it, flat(z1), "xfT", 4)
                token_major(it, "router", xfT, w_rt[:, :], E1)

                def gate_up(e, gates, ups):
                    w = e - 1 if e else E1
                    if e and gates:
                        pe.wait_ge(xe_ready, it * E1 + e)
                    src_e = xe[:, e % 2, :] if e else xfT[:, :]
                    for a in range(2):
                        i = 2 * e + a
                        half = slice(a * P, (a + 1) * P)
                        if gates:
                            pe.wait_ge(ring2_free, it * N2 + R2_FFN + i - 1)
                            pe.matmul(ring2[:, (R2_FFN + i) % 2, :], gate_w[:, w, half], src_e,
                                      start=True, stop=True).then_inc(ring2_full, 1)
                        if ups:
                            pe.wait_ge(ring1_free, it * N1 + R_FFN + i - 1)
                            pe.matmul(ring1[:, (R_FFN + i) % 2, :], up_w[:, w, half], src_e,
                                      start=True, stop=True).then_inc(ring1_full, 1)

                pe.wait_ge(ffn_loaded, it * FFN_LOADS + FFN_LOADS)
                gate_up(0, True, False)
                project_values(it, 0)
                token_major(it, "v1l", xn1T, w_l1[:, 1, :], P)
                repeat(it, 0)
                pe.wait_ge(q1_ready, it + 1)
                for jt in range(TT):
                    i = R_SIM + jt
                    pe.wait_ge(ring1_free, it * N1 + i - 1)
                    pe.matmul(ring1[:, i % 2, 0:T - jt * P], k1T[:, jt * P:(jt + 1) * P], q1T[:, jt * P:T],
                              start=True, stop=True).then_inc(ring1_full, 1)
                gate_up(0, False, True)
                pe.wait_ge(w_ready, it + 1)
                misc_turn(it, "wT")
                for t in range(TT):
                    ins = pe.transpose(misc[0:16, t * P:(t + 1) * P], whl[:, t, :], ident[:, :])
                ins.then_inc(misc_full, 1)
                pe.wait_ge(misc_free, misc_before(it, "wT") + 1)

                def weight(e):
                    pair_turn(f"w{e}")
                    pe.matmul(pair[:, 0, :], pick1[:, e:e + 1].to_broadcast([16, P]), wT[:, :],
                              start=True, stop=True).then_inc(pair_full, 1)

                def down(e):
                    for a in range(2):
                        i = 2 * e + a
                        pe.wait_ge(ring1_free, it * N1 + R_FFN + i + 1)
                        if i == 0:
                            pe.wait_ge(acc_free, it * NA + GROUPS)
                        pe.matmul(acc[:, :], down_w[:, e - 1 if e else E1, a, :], hm[:, i % 2, :],
                                  start=i == 0, stop=i == 2 * E1 + 1).then_inc(down_done, 1)

                weight(0)
                for e in range(1, E1 + 1):
                    if e < E1:
                        weight(e)
                    if e == 1:
                        down(0)
                    gate_up(e, True, True)
                    if e > 1:
                        down(e - 1)
                    if e == 8:
                        pe.wait_ge(attn_ready, it + 1)
                        pe.wait_ge(v1_ready, it + 1)
                        for jt in reversed(range(TT)):
                            pe.matmul(acc[:, jt * P:T], v1[:, jt, :], lz[:, LAP[jt]:LAP[jt + 1]],
                                      start=False, stop=False)
                down(E1)
                pe.wait_ge(acc_free, it * NA + GROUPS + 1)
                transposed(it, o_sb, "fin")
                pe.drain().then_inc(round_done, 1)

        @block.vector
        def _(dve):
            steps, now = [0], [None]

            def prep(ins):
                steps[0] += 1
                ins.then_inc(dve_step, 1)
                dve.wait_ge(dve_step, steps[0])

            def chain(ins):
                steps[0] += 1
                ins.then_inc(dve_step, 1)
                dve.wait_ge(dve_step, steps[0] if now[0] is None else now[0] * STEPS + BEFORE + steps[0])

            def settle():
                dve.memset(spare[:, :], 0.0)

            def misc_filled(name):
                dve.wait_ge(misc_full, misc_before(now[0], name) + 1)

            def norm_stats(src_tm):
                for t in range(TT):
                    ins = dve.bn_stats(stat[:, t, :], src_tm[:, t, :])
                chain(ins)
                settle()
                for t in range(TT):
                    ins = dve.bn_aggr(mv[:, t, :], stat[:, t, :])
                chain(ins)
                dve.tensor_scalar(var[:, :], mv[:, :, 1], EPS, None, ALU.add).then_inc(var_ready, 1)

            def norm_scale(n, src_tm, dst_tm):
                dve.wait_ge(rstd_ready, norms_before(now[0], n) + 1)
                for t in range(TT):
                    ins = dve.tensor_scalar(dst_tm[:, t, :], src_tm[:, t, :], mv[:, t, 0:1], rstd[:, t:t + 1],
                                            ALU.subtract, ALU.mult)
                    if n:
                        ins.then_inc(z_ready, 1)
                return ins

            def project(a):
                dve.wait_ge(pair_full, pair_before(now[0], f"proj{a}") + 1)
                dve.wait_ge(hi_ready, 1 if now[0] is None else now[0] * 2 + (2 if a else 3))
                dve.scalar_tensor_tensor(q_lo[:, :], pair[:, 0, :], col(C_BQ if a else C_Z),
                                         q_hi[:, :].bitcast(F32), ALU.add, ALU.subtract)
                dve.scalar_tensor_tensor(k_lo[:, :], pair[:, 1, :], col(C_BK if a else C_Z),
                                         k_hi[:, :].bitcast(F32), ALU.add, ALU.subtract).then_inc(pair_free, 1)

            def project_values(a):
                misc_filled(f"v{a}")
                v = misc[:, :].rearrange("p (t h d) -> p t h d", t=TT, d=HD)
                if not a:
                    ins = dve.tensor_copy(vext[:, 0, :, :, 0:HD], v)
                else:
                    bias = rows[:, 0:1, :].rearrange("p a (h d) -> p a h d", d=HD)
                    ins = dve.tensor_tensor(vext[:, 1, :, :, 0:HD], v, bias.to_broadcast([P, TT, 4 * HG, HD]),
                                            ALU.add)
                ins.then_inc(misc_free, 1)

            def start(n):
                if n == 0:
                    dve.wait_ge(x_loaded, 16 if now[0] is None else now[0] * 16 + 32)
                    norm_stats(x_in)
                elif n == 1:
                    chain(norm_scale(0, x_in, xn))
                    norm_stats(xn)
                elif n == 2:
                    norm_scale(1, xn, z_tm)
                else:
                    misc_filled("zT")
                    dve.tensor_scalar(hT0[:, :], misc[:, :], col(C_GA), col(C_BA), ALU.mult, ALU.add)
                    dve.tensor_scalar(hT1[:, :], misc[:, :], col(C_G1), col(C_B1), ALU.mult, ALU.add)\
                        .then_inc(misc_free, 1)

            prep(dve.memset(cols[:, C_Z:C_Z + 1], 0.0))
            prep(dve.memset(strip[:, :, :, :].bitcast(F32), 0.0))
            prep(dve.memset(stat[:, :, :], 0.0))
            for n in range(3):
                start(n)
            dve.wait_ge(w_loaded, N_LOADS * 16)
            for blk in (0, 1, 4, 6):
                prep(dve.tensor_copy(strip[:, :, blk, :], ident[:, :].rearrange("p (g c) -> p g c", g=NG)))
            prep(dve.tensor_copy(pick[0:32, :], ident[0:32, 0:32]))
            prep(dve.tensor_copy(pick[32:64, :], ident[32:64, 32:64]))
            prep(dve.tensor_tensor(pick1[:, :], ident[0:16, 0:E1], ident[0:16, E1:2 * E1], ALU.add))
            dve.wait_ge(act_prep, 1)
            dve.tensor_tensor(pos_lo[:, :], pos_f[:, :], pos_hi[:, :].bitcast(F32), ALU.subtract)\
                .then_inc(dve_prep, 1)
            dve.wait_ge(act_prep, 2)
            dve.tensor_tensor(q_lo[:, 0:P], misc[:, 0:P], q_hi[:, 0:P].bitcast(F32), ALU.subtract)\
                .then_inc(dve_prep, 1)
            dve.wait_ge(pe_prep, 2)
            prep(dve.tensor_copy(cols[:, 0:C_LB + 1], ring2[:, 0, 0:C_LB + 1]))
            prep(dve.tensor_copy(prep_t[:, 0:T], ring1[:, 0, :]))
            prep(dve.tensor_copy(prep_t[:, T:T + P], ring1[:, 1, 0:P]))
            width = T + P - 1
            for n in reversed(range(SHIFTS)):
                width -= 1 << n
                prep(dve.tensor_scalar(prep_e[:, 0:width], prep_t[:, 1 << n:(1 << n) + width], shift[:, 0, n:n + 1],
                                       None, ALU.mult))
                prep(dve.scalar_tensor_tensor(prep_t[:, 0:width], prep_t[:, 0:width], shift[:, 1, n:n + 1],
                                              prep_e[:, 0:width], ALU.mult, ALU.add))
            assert width == T
            prep(dve.tensor_scalar(biasl[:, :], prep_t[:, 0:T], float(P ** 0.5 / LAP_STD), float(-LAP_MU / LAP_STD),
                                   ALU.mult, ALU.add))
            dve.wait_ge(pe_prep, 3)
            for g in range(NG):
                for h in range(HG):
                    w = pair[:, 0, g * P:(g + 1) * P]
                    dve.tensor_scalar(wpu[:, g * HG + h, 0:P], w, headmask[:, h:h + 1], None, ALU.mult)
                    ins = dve.tensor_scalar(wpu[:, g * HG + h, P:192], w[:, 0:64], headmask[:, h:h + 1], None, ALU.mult)
            prep(ins)
            prep(dve.memset(acc[:, :], 0.0))
            dve.drain().then_inc(round_done, 1)

            dve.wait_ge(round_done, 4)
            start(3)
            project(0)
            project_values(0)
            BEFORE = steps[0]
            steps[0] = 0
            with dve.Fori(0, rounds) as it:
                now[0] = it
                dve.wait_ge(round_done, it * 4 + 4)

                def top4(n):
                    full = [P, TT, TOPK, E0]
                    if n == 0:
                        dve.wait_ge(x2hi_ready, it + 1)
                        dve.tensor_tensor(x2_lo[:, :], x2T[:, :], x2_hi[:, :].bitcast(F32), ALU.subtract)\
                            .then_inc(x2lo_ready, 1)
                    elif n == 1:
                        dve.wait_ge(misc_free, misc_before(it, "sel") + 1)
                        chain(dve.tensor_scalar(sg0[:, :, :], sg0[:, :, :], 1.0, None, ALU.add))
                        chain(dve.reciprocal(sg0[:, :, :], sg0[:, :, :]))
                    elif n == 2:
                        settle()
                        for t in range(TT):
                            ins = dve.max(m8[:, t, :], sg0[:, t, :])
                        chain(ins)
                    elif n == 3:
                        settle()
                        for t in range(TT):
                            ins = dve.max_index(i8[:, t, :], m8[:, t, :], sg0[:, t, :])
                        chain(ins)
                    elif n == 4:
                        chain(dve.tensor_copy(i8f[:, :, :], i8[:, :, :]))
                        chain(dve.tensor_tensor(eqt[:, :, :, :],
                                                iota[:, :].unsqueeze(1).unsqueeze(1).to_broadcast(full),
                                                i8f[:, :, 0:TOPK].unsqueeze(3).to_broadcast(full), ALU.is_equal))
                    elif n == 5:
                        chain(dve.tensor_tensor(eqt[:, :, :, :], eqt[:, :, :, :],
                                                m8[:, :, 0:TOPK].unsqueeze(3).to_broadcast(full), ALU.mult))
                    elif n == 6:
                        chain(dve.tensor_reduce(gate[:, :, :], eqt[:, :, :, :].rearrange("p t k e -> p t e k"),
                                                AX.X, ALU.add))
                    else:
                        chain(dve.tensor_copy(ghl[:, :, 0:E0].bitcast(F32R), gate[:, :, :]))
                        dve.tensor_tensor(ghl[:, :, E0:2 * E0], gate[:, :, :], ghl[:, :, 0:E0], ALU.subtract)\
                            .then_inc(gate_ready, 1)

                for what, g, n in LAYER0:
                    b = g % 2
                    if what == "proj":
                        project(g)
                        project_values(g)
                    elif what == "start":
                        start(n)
                    elif what == "rot":
                        k = g * HG + n
                        dve.wait_ge(pair_full, pair_before(it, f"rot{g}_{n}") + 1)
                        if k >= 2:
                            dve.wait_ge(ulo_ready, it * ROTS + k - 1)
                        dve.tensor_tensor(rot_a[:, k % 2, :], pair[:, 0, :], cos_t[:, :], ALU.mult)
                        dve.tensor_tensor(rot_b[:, k % 2, :], pair[:, 1, :], sin_t[:, :], ALU.mult)\
                            .then_inc(pair_free, 1)
                    elif what == "sum":
                        dve.scalar_tensor_tensor(acc_tm[:, :, :], xn[:, :, :], 2.0, x_in[:, :, :], ALU.mult, ALU.add)\
                            .then_inc(x_used, 1)
                        dve.wait_ge(x_used, it + 1)
                        chain(dve.tensor_tensor(acc_tm[:, :, :], acc_tm[:, :, :],
                                                rows[:, 1:2, :].to_broadcast([P, TT, P]), ALU.add))
                    elif what == "max":
                        h, t = n // TT, n % TT
                        r = RING1.index(f"max{g * 16 + n}")
                        dve.wait_ge(ring1_full, it * N1 + r + 1)
                        if n == 0 and g >= 2:
                            misc_filled(f"shift{g - 2}")
                        dve.tensor_reduce(negmax[:, b, t, h:h + 1], ring1[:, r % 2, :], AX.X, ALU.max,
                                          negate=True).then_inc(ring1_free, 1)
                    elif what == "heads":
                        misc_filled(f"heads{g}")
                        o = misc[:, :].rearrange("p (t h d) -> p t h d", t=TT, h=HG)
                        chain(dve.reciprocal(rden[:, :, :], o[:, :, :, HD]))
                        gl = g % NG
                        dst = on_tm[:, :, 32 * gl:32 * gl + 32].rearrange("p t (h d) -> p t h d", h=HG)
                        dve.tensor_tensor(dst, o[:, :, :, 0:HD],
                                          rden[:, :, :].unsqueeze(3).to_broadcast([P, TT, HG, HD]), ALU.mult)\
                            .then_inc(misc_free, 1)
                    elif what == "out":
                        misc_filled(f"out{g}")
                        o = tiles(misc[:, :])
                        if g == 0:
                            chain(dve.tensor_tensor(src[:, :, :], xn[:, :, :], o, ALU.add))
                        dve.tensor_tensor(acc_tm[:, :, :], acc_tm[:, :, :], o, ALU.add).then_inc(misc_free, 1)
                    elif what == "ln2_stats":
                        norm_stats(src)
                    elif what == "ln2_scale":
                        norm_scale(2, src, z2)
                    elif what == "x2T":
                        misc_filled("x2T")
                        dve.tensor_scalar(x2T[:, :], misc[:, :], col(C_G2), col(C_B2), ALU.mult, ALU.add)\
                            .then_inc(misc_free, 1)
                    elif what == "top4":
                        top4(n)
                    elif what == "expert":
                        r = RING1.index(f"key{n}")
                        dve.wait_ge(ring1_full, it * N1 + r + 1)
                        dve.wait_ge(ring2_free, it * N2 + RING2.index(f"gate{n}") + 1)
                        if n >= 3:
                            dve.wait_ge(val_done, it * (E0 - 1) + n - 2)
                        dve.scalar_tensor_tensor(hmoe[:, n % 3, :], ring1[:, r % 2, :], 0.0, gate_bc[:, n % 2, :],
                                                 ALU.max, ALU.mult).then_inc(ring1_free, 1)
                misc_filled("moe")
                dve.tensor_tensor(x1[:, :, :], acc_tm[:, :, :], tiles(misc[:, :]), ALU.add).then_inc(misc_free, 1)
                dve.wait_ge(misc_free, misc_before(it, "moe") + 1)

                norm_stats(x1)
                norm_scale(3, x1, xn1)
                dve.wait_ge(z_ready, it * 4 * TT + 4 * TT)
                norm_stats(xn1)
                project(0)
                norm_scale(4, xn1, z1)
                misc_filled("xfT")
                dve.tensor_scalar(xfT[:, :], misc[:, :], col(C_LW), col(C_LB), ALU.mult, ALU.add)\
                    .then_inc(misc_free, 1)
                misc_filled("router")
                dve.tensor_copy(lg[:, :, :].rearrange("p t e -> p (t e)"), misc[:, 0:TT * E1]).then_inc(misc_free, 1)
                dve.wait_ge(misc_free, misc_before(it, "router") + 1)
                settle()
                for t in range(TT):
                    ins = dve.max(m81[:, t, :], lg[:, t, :])
                ins.then_inc(top1_ready, 1)
                dve.wait_ge(top1_ready, it + 1)
                settle()
                for t in range(TT):
                    ins = dve.max_index(i81[:, t, :], m81[:, t, :], lg[:, t, :])
                chain(ins)
                chain(dve.tensor_copy(i81f[:, :, :], i81[:, :, :]))
                full = [P, TT, E1]
                chain(dve.tensor_tensor(w_tm[:, :, :], iota[:, 0:E1].unsqueeze(1).to_broadcast(full),
                                        i81f[:, :, 0:1].to_broadcast(full), ALU.is_equal))
                dve.wait_ge(ring2_free, it * N2 + R2_QK + 1)
                dve.tensor_scalar(q1T[:, :], qkT, col(C_GM0), col(C_BE0), ALU.mult, ALU.add)
                dve.tensor_scalar(k1T[:, :], qkT, col(C_GM1), col(C_BE1), ALU.mult, ALU.add).then_inc(q1_ready, 1)
                chain(dve.tensor_tensor(acc_tm[:, :, :], x1[:, :, :], xn1[:, :, :], ALU.add))
                dve.wait_ge(top1exp_ready, it + 1)
                chain(dve.tensor_tensor(w_tm[:, :, :], w_tm[:, :, :], sc1[:, :].unsqueeze(2).to_broadcast(full),
                                        ALU.mult))
                chain(dve.tensor_copy(whl[:, :, 0:E1].bitcast(F32R), w_tm[:, :, :]))
                dve.tensor_tensor(whl[:, :, E1:2 * E1], w_tm[:, :, :], whl[:, :, 0:E1], ALU.subtract)\
                    .then_inc(w_ready, 1)
                project_values(0)
                misc_filled("v1l")
                dve.tensor_tensor(v1[:, :, :], tiles(misc[:, :]), rows[:, 2:3, :].to_broadcast([P, TT, P]),
                                  ALU.add).then_inc(misc_free, 1)
                for jt in range(TT):
                    i = R_SIM + jt
                    dve.wait_ge(ring1_full, it * N1 + i + 1)
                    dve.scalar_tensor_tensor(lz[:, LAP[jt]:LAP[jt + 1]], ring1[:, i % 2, 0:T - jt * P],
                                             float(1.0 / (T * LAP_STD)), biasl[:, 0:T - jt * P], ALU.mult, ALU.add)\
                        .then_inc(ring1_free, 1)

                def erf_step(n):
                    if n < 5:
                        if n == 0:
                            dve.wait_ge(lap_step, it * LAP_STEPS + 1)
                        part = slice(n * 256, (n + 1) * 256)
                        ins = dve.reciprocal(lt[:, part], lt[:, part])
                        if n == 4:
                            ins.then_inc(lrec_ready, 1)
                    elif n < 9:
                        if n == 5:
                            dve.wait_ge(lap_step, it * LAP_STEPS + 2)
                        chain(dve.scalar_tensor_tensor(la[:, :], la[:, :], ERF_A[8 - n], lt[:, :], ALU.add, ALU.mult))
                    elif n == 9:
                        dve.wait_ge(lexp_ready, it + 1)
                        chain(dve.tensor_tensor(la[:, :], la[:, :], lp[:, :], ALU.mult))
                    elif n == 10:
                        chain(dve.tensor_scalar(lz[:, :], lz[:, :], 0.0, 0.5, ALU.is_ge, ALU.subtract))
                    elif n == 11:
                        chain(dve.scalar_tensor_tensor(la[:, :], la[:, :], -1.0, lz[:, :], ALU.add, ALU.mult))
                    elif n == 12:
                        chain(dve.tensor_scalar(lz[:, :], la[:, :], -1.0, 0.5, ALU.mult, ALU.add))
                    else:
                        for jt in range(TT):
                            diag = lz[:, LAP[jt]:LAP[jt] + P]
                            ins = dve.tensor_tensor(diag, diag, tri[:, :], ALU.mult)
                        ins.then_inc(attn_ready, 1)

                for e in range(E1 + 1):
                    for a in range(2):
                        i = 2 * e + a
                        dve.wait_ge(ring1_full, it * N1 + R_FFN + i + 1)
                        dve.wait_ge(ring2_free, it * N2 + R2_FFN + i + 1)
                        if i >= 2:
                            dve.wait_ge(down_done, it * (2 * (E1 + 1)) + i - 1)
                        dve.tensor_tensor(hm[:, i % 2, :], sg[:, i % 2, :], ring1[:, (R_FFN + i) % 2, :],
                                          ALU.mult).then_inc(ring1_free, 1)
                        for n in range(len(ERF)):
                            if ERF[n] == i:
                                erf_step(n)
                misc_filled("fin")
                dve.tensor_tensor(out_tm[:, :, :], acc_tm[:, :, :], tiles(misc[:, :]), ALU.add).then_inc(misc_free, 1)
                dve.drain().then_inc(round_done, 1)

                assert steps[0] == STEPS, steps[0]


_INS = {"x": "L0_attn_x", "ga": "L0_attn_ln_gamma", "ba": "L0_attn_ln_beta", "w_qkv": "L0_attn_w_qkv",
        "b_qkv": "L0_attn_b_qkv", "w_out": "L0_attn_w_out", "b_out": "L0_attn_b_out", "wq": "L0_ffn_wq",
        "wk": "L0_ffn_wk", "wv": "L0_ffn_wv", "wp": "L0_ffn_wp", "wo": "L0_ffn_wo", "ln1_g": "L0_ffn_ln1_g",
        "ln1_b": "L0_ffn_ln1_b", "ln2_g": "L0_ffn_ln2_g", "ln2_b": "L0_ffn_ln2_b", "sel_w": "L0_ffn_sel_w",
        "keys": "L0_ffn_keys", "values": "L0_ffn_values", "Wqk": "L1_attn_Wqk", "bqk": "L1_attn_bqk",
        "gamma": "L1_attn_gamma", "beta": "L1_attn_beta", "Wv": "L1_attn_Wv", "bv": "L1_attn_bv",
        "rel_emb": "L1_attn_rel_emb", "ln_w": "L1_ffn_ln_w", "ln_b": "L1_ffn_ln_b",
        "router_w": "L1_ffn_router_w", "gate_w": "L1_ffn_gate_w", "up_w": "L1_ffn_up_w",
        "down_w": "L1_ffn_down_w", "sh_gate": "L1_ffn_sh_gate", "sh_up": "L1_ffn_sh_up",
        "sh_down": "L1_ffn_sh_down"}


def _tables():
    import math

    r = np.arange(P)
    freq = (1.0 / np.float32(10000.0) ** (np.arange(0, P, 2, dtype=np.float32) / np.float32(P))).astype(np.float64)
    ang = freq[:, None] * np.arange(T)[None, :]
    s, c = np.sin(ang), np.cos(ang)
    mask = np.zeros((P, HG), np.float32)
    for h in range(HG):
        mask[:96, h] = (r[:96] % 32) // HD == h
        mask[96 + h, h] = 1.0
    ones = np.zeros((32, T), np.float32)
    ones[:HG] = 1.0
    n = np.maximum(np.arange(T + P) - (P - 1), 0)
    half = MAX_BUCKETS // 2
    large = half + (np.log(np.maximum(n, 1).astype(np.float32) / half) / math.log(MAX_DISTANCE / half)
                    * (MAX_BUCKETS - half)).astype(np.int32)
    bucket = np.where(n < half, n, np.minimum(large, MAX_BUCKETS - 1))
    onehot = np.arange(MAX_BUCKETS)[:, None] == bucket[None, :]
    bits = ((P - 1 - r)[:, None] >> np.arange(SHIFTS)[None, :]) & 1
    return {"eye": np.eye(P), "pos": np.concatenate([s, c]), "cos": np.concatenate([c, c]),
            "sin": np.concatenate([s, -s]), "headmask": mask, "ones_rows": ones,
            "iota": np.arange(E0), "tri": r[None, :] >= r[:, None], "onehot": onehot,
            "shift": np.stack([bits, 1 - bits], axis=1)}


def kernel(**inputs):
    import concourse.bacc as _bacc
    from concourse.bass_utils import run_bass_kernel_spmd as _run

    nc = _bacc.Bacc("TRN2", target_bir_lowering=False, num_devices=1)
    arrays = {short: np.ascontiguousarray(inputs[name]) for short, name in _INS.items()}
    arrays.update({name: np.ascontiguousarray(a, dtype=np.float32) for name, a in _tables().items()})
    io = {name: nc.dram_tensor(f"in_{name}", a.shape, F32, kind="ExternalInput").ap() for name, a in arrays.items()}
    out = nc.dram_tensor("out_0", arrays["x"].shape, F32, kind="ExternalOutput").ap()
    build(nc, io, out)
    r = _run(nc, [{f"in_{name}": a for name, a in arrays.items()}], core_ids=[0])
    return r.results[0]["out_0"]
```
